# Optimizing a Trainium2 kernel written in Bass

```python
import numpy as np
import jax
import jax.numpy as jnp

def _softmax(x, axis=-1):
    return jax.nn.softmax(x, axis=axis)

def _gelu(x):
    return jax.nn.gelu(x, approximate=True)

def _silu(x):
    return jax.nn.silu(x)

def _sigmoid(x):
    return jax.nn.sigmoid(x)

def _layernorm(x, axis=-1, eps=1e-05):
    m = jnp.mean(x, axis=axis, keepdims=True)
    v = jnp.var(x, axis=axis, keepdims=True)
    return (x - m) / jnp.sqrt(v + eps)

def _scatter_add(tgt, idx, src, axis=0):
    return tgt.at[idx].add(src)

def _segment_sum(src, seg, n):
    return jax.ops.segment_sum(src, seg, n)
kernel_name = 'mk_adaln_d2_jaxref_r8_f3b2fb'

def setup_inputs(seed: int=0):
    np.random.seed(seed)
    _w = jnp.asarray

    def _L0_attn_setup():
        import jax, jax.numpy as jnp
        import numpy as np
        NUM_HEADS = 16
        NEG = -1000000000.0

        def _split_heads(t, h):
            *lead, s, hd = t.shape
            return jnp.swapaxes(t.reshape(*lead, s, h, hd // h), -3, -2)
        key = jax.random.key(seed)
        ks = jax.random.split(key, 5)
        B, S, D = (4, 256, 128)
        scale = 1.0 / np.sqrt(D)
        return {'x': jax.random.normal(ks[0], (B, S, D), dtype=jnp.float32), 'WQ': jax.random.normal(ks[1], (D, D), dtype=jnp.float32) * scale, 'WK': jax.random.normal(ks[2], (D, D), dtype=jnp.float32) * scale, 'WV': jax.random.normal(ks[3], (D, D), dtype=jnp.float32) * scale, 'WO': jax.random.normal(ks[4], (D, D), dtype=jnp.float32) * scale}
    _L0_attn_in = _L0_attn_setup()

    def _L0_ffn_setup():
        import jax, jax.numpy as jnp
        import numpy as np
        from jax import lax
        HIDDEN = 128
        INTER = 64
        E = 64
        K = 6
        G = 8
        TG = 4
        NSH = 2
        ISH = INTER * NSH

        def _moe_forward(hidden_states, gate_w, gate_bias, eg_w, eu_w, ed_w, sg_w, su_w, sd_w):
            B, S, H = hidden_states.shape
            x = hidden_states.reshape(-1, H)
            T = x.shape[0]
            shared = jax.nn.silu(x @ sg_w.T) * (x @ su_w.T) @ sd_w.T
            logits = x @ gate_w.T
            scores = jax.nn.sigmoid(logits) + gate_bias
            group_scores = scores.reshape(T, G, E // G).max(axis=-1)
            _, sel_groups = lax.top_k(group_scores, TG)
            group_mask = jnp.zeros((T, G), scores.dtype).at[jnp.arange(T)[:, None], sel_groups].set(1.0)
            mask = jnp.repeat(group_mask, E // G, axis=1)
            masked_scores = scores * mask
            topk_w, topk_i = lax.top_k(masked_scores, K)
            topk_w = topk_w / (topk_w.sum(axis=-1, keepdims=True) + 1e-08)
            comb = jnp.zeros((T, E), x.dtype).at[jnp.arange(T)[:, None], topk_i].add(topk_w)
            h = jax.nn.silu(jnp.einsum('th,eih->eti', x, eg_w)) * jnp.einsum('th,eih->eti', x, eu_w)
            routed = jnp.einsum('eti,ehi,te->th', h, ed_w, comb)
            return (shared + routed).reshape(B, S, H)
        key = jax.random.key(seed)
        ks = jax.random.split(key, 9)
        s = 0.02
        return {'hidden_states': jax.random.normal(ks[0], (1, 128, HIDDEN), jnp.float32), 'gate_w': jax.random.normal(ks[1], (E, HIDDEN), jnp.float32) * s, 'gate_bias': jnp.zeros((E,), jnp.float32), 'eg_w': jax.random.normal(ks[2], (E, INTER, HIDDEN), jnp.float32) * s, 'eu_w': jax.random.normal(ks[3], (E, INTER, HIDDEN), jnp.float32) * s, 'ed_w': jax.random.normal(ks[4], (E, HIDDEN, INTER), jnp.float32) * s, 'sg_w': jax.random.normal(ks[5], (ISH, HIDDEN), jnp.float32) * s, 'su_w': jax.random.normal(ks[6], (ISH, HIDDEN), jnp.float32) * s, 'sd_w': jax.random.normal(ks[7], (HIDDEN, ISH), jnp.float32) * s}
    _L0_ffn_in = _L0_ffn_setup()
    _L0_c = _w((lambda *s: np.random.randn(*s).astype(np.float32) * 0.05)(2, 128))
    _L0_wmod = _w((lambda *s: np.random.randn(*s).astype(np.float32) * 0.05)(128, 6 * 128) * 128 ** (-0.5))

    def _L1_attn_setup():
        import jax, jax.numpy as jnp
        import numpy as np
        from jax import lax
        L, B, T, C, F = (4, 4, 256, 128, 512)
        EPS = 1e-05

        def layernorm(x, w, b):
            m = jnp.mean(x, axis=-1, keepdims=True)
            v = jnp.var(x, axis=-1, keepdims=True)
            return (x - m) * lax.rsqrt(v + EPS) * w + b

        def time_shift(x):
            return jnp.pad(x, ((0, 0), (1, 0), (0, 0)))[:, :-1]

        def wkv(time_decay, time_first, k, v):
            w = -jnp.exp(time_decay)
            u = time_first
            kt = jnp.swapaxes(k, 0, 1)
            vt = jnp.swapaxes(v, 0, 1)
            Bn, Cn = (k.shape[0], k.shape[2])
            init = (jnp.zeros((Bn, Cn), k.dtype), jnp.zeros((Bn, Cn), k.dtype), jnp.full((Bn, Cn), -1e+38, k.dtype))

            def step(carry, kv):
                aa, bb, pp = carry
                kk, vv = kv
                ww = u + kk
                qq = jnp.maximum(pp, ww)
                e1 = jnp.exp(pp - qq)
                e2 = jnp.exp(ww - qq)
                out = (e1 * aa + e2 * vv) / (e1 * bb + e2)
                ww2 = pp + w
                qq2 = jnp.maximum(ww2, kk)
                e1b = jnp.exp(ww2 - qq2)
                e2b = jnp.exp(kk - qq2)
                return ((e1b * aa + e2b * vv, e1b * bb + e2b, qq2), out)
            _, out = lax.scan(step, init, (kt, vt))
            return jnp.swapaxes(out, 0, 1)
        key = jax.random.key(seed)
        ks = jax.random.split(key, 16)
        s = 0.02
        d = {}
        d['x'] = jax.random.normal(ks[0], (B, T, C), jnp.float32)
        d['ln0_w'] = jnp.ones((C,), jnp.float32)
        d['ln0_b'] = jnp.zeros((C,), jnp.float32)
        d['ln1_w'] = jnp.ones((L, C), jnp.float32)
        d['ln1_b'] = jnp.zeros((L, C), jnp.float32)
        d['ln2_w'] = jnp.ones((L, C), jnp.float32)
        d['ln2_b'] = jnp.zeros((L, C), jnp.float32)
        d['time_decay'] = jax.random.normal(ks[1], (L, C), jnp.float32) * 0.5
        d['time_first'] = jax.random.normal(ks[2], (L, C), jnp.float32) * 0.5 + jnp.float32(np.log(0.3))
        d['tmk'] = jax.random.uniform(ks[3], (L, C), jnp.float32)
        d['tmv'] = jax.random.uniform(ks[4], (L, C), jnp.float32)
        d['tmr'] = jax.random.uniform(ks[5], (L, C), jnp.float32)
        d['Wk'] = jax.random.normal(ks[6], (L, C, C), jnp.float32) * s
        d['Wv'] = jax.random.normal(ks[7], (L, C, C), jnp.float32) * s
        d['Wr'] = jax.random.normal(ks[8], (L, C, C), jnp.float32) * s
        d['Wo'] = jax.random.normal(ks[9], (L, C, C), jnp.float32) * s
        d['cmk'] = jax.random.uniform(ks[10], (L, C), jnp.float32)
        d['cmr'] = jax.random.uniform(ks[11], (L, C), jnp.float32)
        d['Wck'] = jax.random.normal(ks[12], (L, F, C), jnp.float32) * s
        d['Wcv'] = jax.random.normal(ks[13], (L, C, F), jnp.float32) * s
        d['Wcr'] = jax.random.normal(ks[14], (L, C, C), jnp.float32) * s
        return d
    _L1_attn_in = _L1_attn_setup()

    def _L1_ffn_setup():
        import jax, jax.numpy as jnp
        import numpy as np
        TOP_K = 2
        key = jax.random.key(seed)
        k_x, k_g, k_w1, k_w2, k_w3 = jax.random.split(key, 5)
        B, S, D, H, E = (2, 64, 128, 64, 8)
        x = jax.random.normal(k_x, (B, S, D), dtype=jnp.float32)
        gate_w = jax.random.normal(k_g, (D, E), dtype=jnp.float32) * D ** (-0.5)
        w1 = jax.random.normal(k_w1, (E, D, H), dtype=jnp.float32) * 0.02
        w2 = jax.random.normal(k_w2, (E, H, D), dtype=jnp.float32) * 0.02
        w3 = jax.random.normal(k_w3, (E, D, H), dtype=jnp.float32) * 0.02
        return {'x': x, 'gate_w': gate_w, 'w1': w1, 'w2': w2, 'w3': w3}
    _L1_ffn_in = _L1_ffn_setup()
    _L1_c = _w((lambda *s: np.random.randn(*s).astype(np.float32) * 0.05)(2, 128))
    _L1_wmod = _w((lambda *s: np.random.randn(*s).astype(np.float32) * 0.05)(128, 6 * 128) * 128 ** (-0.5))
    _d = {'L0_attn_x': _L0_attn_in['x'], 'L0_attn_WQ': _L0_attn_in['WQ'], 'L0_attn_WK': _L0_attn_in['WK'], 'L0_attn_WV': _L0_attn_in['WV'], 'L0_attn_WO': _L0_attn_in['WO'], 'L0_ffn_gate_w': _L0_ffn_in['gate_w'], 'L0_ffn_gate_bias': _L0_ffn_in['gate_bias'], 'L0_ffn_eg_w': _L0_ffn_in['eg_w'], 'L0_ffn_eu_w': _L0_ffn_in['eu_w'], 'L0_ffn_ed_w': _L0_ffn_in['ed_w'], 'L0_ffn_sg_w': _L0_ffn_in['sg_w'], 'L0_ffn_su_w': _L0_ffn_in['su_w'], 'L0_ffn_sd_w': _L0_ffn_in['sd_w'], 'L0_c': _L0_c, 'L0_wmod': _L0_wmod, 'L1_attn_ln0_w': _L1_attn_in['ln0_w'], 'L1_attn_ln0_b': _L1_attn_in['ln0_b'], 'L1_attn_ln1_w': _L1_attn_in['ln1_w'], 'L1_attn_ln1_b': _L1_attn_in['ln1_b'], 'L1_attn_ln2_w': _L1_attn_in['ln2_w'], 'L1_attn_ln2_b': _L1_attn_in['ln2_b'], 'L1_attn_time_decay': _L1_attn_in['time_decay'], 'L1_attn_time_first': _L1_attn_in['time_first'], 'L1_attn_tmk': _L1_attn_in['tmk'], 'L1_attn_tmv': _L1_attn_in['tmv'], 'L1_attn_tmr': _L1_attn_in['tmr'], 'L1_attn_Wk': _L1_attn_in['Wk'], 'L1_attn_Wv': _L1_attn_in['Wv'], 'L1_attn_Wr': _L1_attn_in['Wr'], 'L1_attn_Wo': _L1_attn_in['Wo'], 'L1_attn_cmk': _L1_attn_in['cmk'], 'L1_attn_cmr': _L1_attn_in['cmr'], 'L1_attn_Wck': _L1_attn_in['Wck'], 'L1_attn_Wcv': _L1_attn_in['Wcv'], 'L1_attn_Wcr': _L1_attn_in['Wcr'], 'L1_ffn_gate_w': _L1_ffn_in['gate_w'], 'L1_ffn_w1': _L1_ffn_in['w1'], 'L1_ffn_w2': _L1_ffn_in['w2'], 'L1_ffn_w3': _L1_ffn_in['w3'], 'L1_c': _L1_c, 'L1_wmod': _L1_wmod}
    _x0 = _d['L0_attn_x']
    _d['L0_attn_x'] = jax.random.normal(jax.random.fold_in(jax.random.key(seed), 1), (2, 1024, 128), dtype=_x0.dtype)
    del _x0
    return _d

def reference(L0_attn_x, L0_attn_WQ, L0_attn_WK, L0_attn_WV, L0_attn_WO, L0_ffn_gate_w, L0_ffn_gate_bias, L0_ffn_eg_w, L0_ffn_eu_w, L0_ffn_ed_w, L0_ffn_sg_w, L0_ffn_su_w, L0_ffn_sd_w, L0_c, L0_wmod, L1_attn_ln0_w, L1_attn_ln0_b, L1_attn_ln1_w, L1_attn_ln1_b, L1_attn_ln2_w, L1_attn_ln2_b, L1_attn_time_decay, L1_attn_time_first, L1_attn_tmk, L1_attn_tmv, L1_attn_tmr, L1_attn_Wk, L1_attn_Wv, L1_attn_Wr, L1_attn_Wo, L1_attn_cmk, L1_attn_cmr, L1_attn_Wck, L1_attn_Wcv, L1_attn_Wcr, L1_ffn_gate_w, L1_ffn_w1, L1_ffn_w2, L1_ffn_w3, L1_c, L1_wmod):

    def _L0_attn_ref(x, WQ, WK, WV, WO):
        import jax, jax.numpy as jnp
        import numpy as np
        NUM_HEADS = 16
        NEG = -1000000000.0

        def _split_heads(t, h):
            *lead, s, hd = t.shape
            return jnp.swapaxes(t.reshape(*lead, s, h, hd // h), -3, -2)
        h = NUM_HEADS
        S = x.shape[-2]
        Q = _split_heads(x @ WQ.T, h)
        K = _split_heads(x @ WK.T, h)
        V = _split_heads(x @ WV.T, h)
        dk = Q.shape[-1]
        scores = jnp.einsum('bhqd,bhkd->bhqk', Q, K) / jnp.sqrt(jnp.float32(dk))
        causal = jnp.tril(jnp.ones((S, S), dtype=bool))
        scores = jnp.where(causal, scores, NEG)
        m = jnp.max(scores, axis=-1, keepdims=True)
        e = jnp.exp(scores - m)
        attn = e / jnp.sum(e, axis=-1, keepdims=True)
        out = jnp.einsum('bhqk,bhkd->bhqd', attn, V)
        out = jnp.swapaxes(out, -3, -2).reshape(*x.shape[:-1], -1)
        return out @ WO.T

    def _L0_ffn_ref(hidden_states, gate_w, gate_bias, eg_w, eu_w, ed_w, sg_w, su_w, sd_w):
        import jax, jax.numpy as jnp
        import numpy as np
        from jax import lax
        HIDDEN = 128
        INTER = 64
        E = 64
        K = 6
        G = 8
        TG = 4
        NSH = 2
        ISH = INTER * NSH

        def _moe_forward(hidden_states, gate_w, gate_bias, eg_w, eu_w, ed_w, sg_w, su_w, sd_w):
            B, S, H = hidden_states.shape
            x = hidden_states.reshape(-1, H)
            T = x.shape[0]
            shared = jax.nn.silu(x @ sg_w.T) * (x @ su_w.T) @ sd_w.T
            logits = x @ gate_w.T
            scores = jax.nn.sigmoid(logits) + gate_bias
            group_scores = scores.reshape(T, G, E // G).max(axis=-1)
            _, sel_groups = lax.top_k(group_scores, TG)
            group_mask = jnp.zeros((T, G), scores.dtype).at[jnp.arange(T)[:, None], sel_groups].set(1.0)
            mask = jnp.repeat(group_mask, E // G, axis=1)
            masked_scores = scores * mask
            topk_w, topk_i = lax.top_k(masked_scores, K)
            topk_w = topk_w / (topk_w.sum(axis=-1, keepdims=True) + 1e-08)
            comb = jnp.zeros((T, E), x.dtype).at[jnp.arange(T)[:, None], topk_i].add(topk_w)
            h = jax.nn.silu(jnp.einsum('th,eih->eti', x, eg_w)) * jnp.einsum('th,eih->eti', x, eu_w)
            routed = jnp.einsum('eti,ehi,te->th', h, ed_w, comb)
            return (shared + routed).reshape(B, S, H)
        return _moe_forward(hidden_states, gate_w, gate_bias, eg_w, eu_w, ed_w, sg_w, su_w, sd_w)

    def _L1_attn_ref(x, ln0_w, ln0_b, ln1_w, ln1_b, ln2_w, ln2_b, time_decay, time_first, tmk, tmv, tmr, Wk, Wv, Wr, Wo, cmk, cmr, Wck, Wcv, Wcr):
        import jax, jax.numpy as jnp
        import numpy as np
        from jax import lax
        L, B, T, C, F = (4, 4, 256, 128, 512)
        EPS = 1e-05

        def layernorm(x, w, b):
            m = jnp.mean(x, axis=-1, keepdims=True)
            v = jnp.var(x, axis=-1, keepdims=True)
            return (x - m) * lax.rsqrt(v + EPS) * w + b

        def time_shift(x):
            return jnp.pad(x, ((0, 0), (1, 0), (0, 0)))[:, :-1]

        def wkv(time_decay, time_first, k, v):
            w = -jnp.exp(time_decay)
            u = time_first
            kt = jnp.swapaxes(k, 0, 1)
            vt = jnp.swapaxes(v, 0, 1)
            Bn, Cn = (k.shape[0], k.shape[2])
            init = (jnp.zeros((Bn, Cn), k.dtype), jnp.zeros((Bn, Cn), k.dtype), jnp.full((Bn, Cn), -1e+38, k.dtype))

            def step(carry, kv):
                aa, bb, pp = carry
                kk, vv = kv
                ww = u + kk
                qq = jnp.maximum(pp, ww)
                e1 = jnp.exp(pp - qq)
                e2 = jnp.exp(ww - qq)
                out = (e1 * aa + e2 * vv) / (e1 * bb + e2)
                ww2 = pp + w
                qq2 = jnp.maximum(ww2, kk)
                e1b = jnp.exp(ww2 - qq2)
                e2b = jnp.exp(kk - qq2)
                return ((e1b * aa + e2b * vv, e1b * bb + e2b, qq2), out)
            _, out = lax.scan(step, init, (kt, vt))
            return jnp.swapaxes(out, 0, 1)
        x = layernorm(x, ln0_w, ln0_b)
        for l in range(L):
            h = layernorm(x, ln1_w[l], ln1_b[l])
            hh = time_shift(h)
            xk = h * tmk[l] + hh * (1 - tmk[l])
            xv = h * tmv[l] + hh * (1 - tmv[l])
            xr = h * tmr[l] + hh * (1 - tmr[l])
            k = jnp.einsum('btc,oc->bto', xk, Wk[l])
            v = jnp.einsum('btc,oc->bto', xv, Wv[l])
            sr = jax.nn.sigmoid(jnp.einsum('btc,oc->bto', xr, Wr[l]))
            rwkv = sr * wkv(time_decay[l], time_first[l], k, v)
            x = x + jnp.einsum('bto,co->btc', rwkv, Wo[l])
            h = layernorm(x, ln2_w[l], ln2_b[l])
            hh = time_shift(h)
            xk = h * cmk[l] + hh * (1 - cmk[l])
            xr = h * cmr[l] + hh * (1 - cmr[l])
            kf = jnp.einsum('btc,fc->btf', xk, Wck[l])
            kf = jnp.square(jax.nn.relu(kf))
            kv = jnp.einsum('btf,cf->btc', kf, Wcv[l])
            x = x + jax.nn.sigmoid(jnp.einsum('btc,oc->bto', xr, Wcr[l])) * kv
        return x

    def _L1_ffn_ref(x, gate_w, w1, w2, w3):
        import jax, jax.numpy as jnp
        import numpy as np
        TOP_K = 2
        B, S, D = x.shape
        E = gate_w.shape[1]
        xf = x.reshape(B * S, D)
        T = B * S
        logits = xf @ gate_w
        scores = jax.nn.softmax(logits, axis=-1)
        top_scores, top_idx = jax.lax.top_k(scores, TOP_K)
        scale = jnp.zeros((T, E), dtype=x.dtype).at[jnp.arange(T)[:, None], top_idx].set(top_scores)
        xs = scale.T[:, :, None] * xf[None, :, :]
        h = jax.nn.silu(jnp.einsum('etd,edh->eth', xs, w1)) * jnp.einsum('etd,edh->eth', xs, w3)
        y = jnp.einsum('eth,ehd->etd', h, w2)
        out = y.sum(axis=0)
        return out.reshape(B, S, D)
    x = L0_attn_x
    mod = (_silu(L0_c) @ L0_wmod).reshape(L0_c.shape[0], 6, 1, -1)
    sa, ca, ga, sb, cb, gb = (mod[:, 0], mod[:, 1], mod[:, 2], mod[:, 3], mod[:, 4], mod[:, 5])
    ga = (2 * (ga >= 0) - 1) * jnp.maximum(jnp.abs(ga), 0.25)
    gb = (2 * (gb >= 0) - 1) * jnp.maximum(jnp.abs(gb), 0.25)
    h = _layernorm(x, axis=-1) * (1 + ca) + sa
    x = x + ga * _L0_attn_ref(h, L0_attn_WQ, L0_attn_WK, L0_attn_WV, L0_attn_WO)
    h = _layernorm(x, axis=-1) * (1 + cb) + sb
    x = x + gb * _L0_ffn_ref(h, L0_ffn_gate_w, L0_ffn_gate_bias, L0_ffn_eg_w, L0_ffn_eu_w, L0_ffn_ed_w, L0_ffn_sg_w, L0_ffn_su_w, L0_ffn_sd_w)
    mod = (_silu(L1_c) @ L1_wmod).reshape(L1_c.shape[0], 6, 1, -1)
    sa, ca, ga, sb, cb, gb = (mod[:, 0], mod[:, 1], mod[:, 2], mod[:, 3], mod[:, 4], mod[:, 5])
    ga = (2 * (ga >= 0) - 1) * jnp.maximum(jnp.abs(ga), 0.25)
    gb = (2 * (gb >= 0) - 1) * jnp.maximum(jnp.abs(gb), 0.25)
    h = _layernorm(x, axis=-1) * (1 + ca) + sa
    x = x + ga * _L1_attn_ref(h, L1_attn_ln0_w, L1_attn_ln0_b, L1_attn_ln1_w, L1_attn_ln1_b, L1_attn_ln2_w, L1_attn_ln2_b, L1_attn_time_decay, L1_attn_time_first, L1_attn_tmk, L1_attn_tmv, L1_attn_tmr, L1_attn_Wk, L1_attn_Wv, L1_attn_Wr, L1_attn_Wo, L1_attn_cmk, L1_attn_cmr, L1_attn_Wck, L1_attn_Wcv, L1_attn_Wcr)
    h = _layernorm(x, axis=-1) * (1 + cb) + sb
    x = x + gb * _L1_ffn_ref(h, L1_ffn_gate_w, L1_ffn_w1, L1_ffn_w2, L1_ffn_w3)
    return x

_drawn_inputs = setup_inputs


def setup_inputs(seed=0):
    import zlib

    import numpy as np

    out = dict(_drawn_inputs(seed))
    spreads = {'L0_ffn_gate_bias': (0.0, 0.8),
     'L1_attn_ln0_w': (1.0, 0.2),
     'L1_attn_ln0_b': (0.0, 0.342),
     'L1_attn_ln1_w': (1.0, 0.6),
     'L1_attn_ln1_b': (0.0, 0.8),
     'L1_attn_ln2_w': (1.0, 0.6),
     'L1_attn_ln2_b': (0.0, 0.8)}
    factors = {'L0_ffn_gate_w': 8.0,
     'L0_ffn_eg_w': 8.0,
     'L0_ffn_eu_w': 8.0,
     'L0_ffn_ed_w': 8.0,
     'L0_ffn_sg_w': 8.0,
     'L0_ffn_su_w': 8.0,
     'L0_ffn_sd_w': 8.0,
     'L1_attn_time_decay': 8.0,
     'L1_attn_time_first': 8.0,
     'L1_attn_tmk': 8.0,
     'L1_attn_tmv': 8.0,
     'L1_attn_tmr': 8.0,
     'L1_attn_Wk': 8.0,
     'L1_attn_Wv': 7.882,
     'L1_attn_Wr': 8.0,
     'L1_attn_Wo': 7.956,
     'L1_attn_cmk': 8.0,
     'L1_attn_cmr': 8.0,
     'L1_attn_Wck': 8.0,
     'L1_attn_Wcv': 8.0,
     'L1_attn_Wcr': 8.0,
     'L1_ffn_gate_w': 64.0,
     'L1_ffn_w1': 64.0,
     'L1_ffn_w2': 64.0,
     'L1_ffn_w3': 64.0}
    for name, (base, spread) in spreads.items():
        noise = np.random.default_rng([zlib.crc32(name.encode()), seed]).standard_normal(out[name].shape)
        drawn = base * np.exp(spread * noise) if base else spread * noise
        out[name] = jnp.asarray(drawn.astype(out[name].dtype))
    for name, factor in factors.items():
        out[name] = (out[name] * factor).astype(out[name].dtype)
    return out
```

```python
import math
from contextlib import ExitStack

import concourse.bass as bass
from concourse import mybir

ALU = mybir.AluOpType
ACT = mybir.ActivationFunctionType
F32 = mybir.dt.float32
BF16 = mybir.dt.bfloat16
AX_X = mybir.AxisListType.X

P = 128
B = 2
S = 1024
T = B * S
NT = T // P
CH = 512
NC = T // CH
H = 16
DK = P // H
HG = 4
NG = B * H // HG
NEG = -1e30
ROWS = 9 * DK
RING = 4
EXP_LN_SET = 6

VECS = ["ln1_w", "ln1_b", "ln2_w", "ln2_b", "time_decay", "time_first", "tmk", "tmv", "tmr", "cmk", "cmr"]
LN1W, LN1B, LN2W, LN2B, DECAY, FIRST, TMK, TMV, TMR, CMK, CMR = range(11)
LAYERS = 4


class Memory:

    def __init__(self, nc, ctx):
        self.nc, self.ctx = nc, ctx

    def sb(self, name, shape, dt=F32):
        return self.ctx.enter_context(self.nc.sbuf_tensor(name, shape, dt))

    def sem(self, name):
        return self.nc.alloc_semaphore(name)


class LnSems:

    def __init__(self, mem):
        self.centred = mem.sem("ln_centred")
        self.squared = mem.sem("ln_squared")
        self.variance = mem.sem("ln_variance")
        self.logged = mem.sem("ln_logged")
        self.rstd = mem.sem("ln_rstd")
        self.scaled = mem.sem("ln_scaled")


def chunk(c, n=CH):
    return slice(c * n, (c + 1) * n)


def load_act_set(nc, act, set_id):
    act.add_instruction(mybir.InstLoadActFuncSet(name=nc.get_next_instruction_name(), act_func_set_id=set_id,
                                                 engine=mybir.EngineType.Activation, ins=[], outs=[]))


def ln_centre(pe, G, n, src, par=None):
    par = n % 2 if par is None else par
    if not isinstance(n, int) or n >= 2:
        pe.wait_ge(G.ln.scaled, n - 1)
    pe.matmul(G.bank[par][:, :], G.centre[:, :], src, start=True, stop=True).then_inc(G.ln.centred, 1)


def ln_variance(pe, G, n, par=None):
    par = n % 2 if par is None else par
    pe.wait_ge(G.ln.squared, n + 1)
    if not isinstance(n, int) or n >= 2:
        pe.wait_ge(G.ln.rstd, n - 1)
    pe.matmul(G.bank[2 + par][:, :], G.mean[:, :], G.sq[:, par, :], start=True, stop=True)\
        .then_inc(G.ln.variance, 1)


def ln_square(act, G, n, par=None):
    par = n % 2 if par is None else par
    act.wait_ge(G.ln.centred, n + 1)
    if not isinstance(n, int) or n >= 2:
        act.wait_ge(G.ln.variance, n - 1)
    act.activation(G.sq[:, par, :], G.bank[par][:, :], ACT.Square).then_inc(G.ln.squared, 1)


def ln_rstd(act, G, n, par=None):
    par = n % 2 if par is None else par
    act.wait_ge(G.ln.variance, n + 1)
    if not isinstance(n, int) or n >= 2:
        act.wait_ge(G.ln.scaled, n - 1)
    act.activation(G.rs[:, par, :], G.bank[2 + par][:, :], ACT.Ln, bias=G.eps[:, 0:1])\
        .then_inc(G.ln.logged, 1)
    act.wait_ge(G.ln.logged, n + 1)
    act.activation(G.rs[:, par, :], G.rs[:, par, :], ACT.Exp, scale=-0.5).then_inc(G.ln.rstd, 1)


def ln_scale(dve, G, n, dst, w, par=None):
    par = n % 2 if par is None else par
    dve.wait_ge(G.ln.rstd, n + 1)
    dve.scalar_tensor_tensor(dst, G.bank[par][:, :], w, G.rs[:, par, :], ALU.mult, ALU.mult)\
        .then_inc(G.ln.scaled, 1)


class Global:
    pass


def stage_setup(nc, G, A):
    mem = G.mem
    with ExitStack() as ctx:
        m = Memory(nc, ctx)
        x_tok = m.sb("x_tok", [P, NT, P])
        w_nat = m.sb("w_nat", [P, 4, P])
        wo_sp = m.sb("wo_sp", [P, H, 32])
        gate_nat = m.sb("gate_nat", [64, P])
        vec_rows = m.sb("vec_rows", [46, P])
        c_t = m.sb("c_t", [P, 2, B])
        c_silu = m.sb("c_silu", [P, 2, B])
        wmod = m.sb("wmod", [P, 2, 6, P])
        sign = m.sb("sign", [P, 2, 2, B])
        mag = m.sb("mag", [P, 2, 2, B])
        x_in = [mem.sem(f"x_in{c}") for c in range(NC)]
        w_in, vec_in, c_in = mem.sem("w_in"), mem.sem("vec_in"), mem.sem("c_in")
        const_zero, const_done = mem.sem("const_zero"), mem.sem("const_done")
        centre_done, sp_zero, sp_done = mem.sem("centre_done"), mem.sem("sp_zero"), mem.sem("sp_done")
        silu_done, va_zero = mem.sem("silu_done"), mem.sem("va_zero")
        x_turned, x_kept = mem.sem("x_turned"), mem.sem("x_kept")
        w_turned, w_kept = mem.sem("w_turned"), mem.sem("w_kept")
        mod_psum, mod_step, mod_done = mem.sem("mod_psum"), mem.sem("mod_step"), mem.sem("mod_done")
        x_d = A["L0_attn_x"].rearrange("b (t p) c -> p (b t) c", p=P)
        with nc.Block() as block:
            @block.sync
            def _(sp):
                for c in range(NC):
                    sp.dma_start(x_tok[:, 4 * c:4 * c + 4, :], x_d[:, 4 * c:4 * c + 4, :]).then_inc(x_in[c], 16)
                for i, name in enumerate(["WQ", "WK", "WV", "WO"]):
                    sp.dma_start(w_nat[:, i, :], A["L0_attn_" + name]).then_inc(w_in, 16)
                sp.dma_start(gate_nat[:, :], A["L0_ffn_gate_w"]).then_inc(w_in, 16)
                sp.dma_start(G.gate1[:, :], A["L1_ffn_gate_w"]).then_inc(vec_in, 16)
                sp.dma_start(G.gate_bias[:, :], A["L0_ffn_gate_bias"].rearrange("(o e) -> o e", o=1)
                             .to_broadcast([P, 64])).then_inc(vec_in, 16)

            @block.scalar
            def _(act):
                for i in range(2):
                    with nc.allow_non_contiguous_dma(reason="two columns of 128"):
                        act.dma_start(c_t[:, i, :], A[f"L{i}_c"].rearrange("b p -> p b")).then_inc(c_in, 16)
                    act.dma_start(wmod[:, i, :, :], A[f"L{i}_wmod"].rearrange("k (j m) -> k j m", j=6))\
                        .then_inc(c_in, 16)
                for v, name in enumerate(VECS):
                    act.dma_start(vec_rows[4 * v:4 * v + 4, :], A["L1_attn_" + name]).then_inc(vec_in, 16)
                for v, name in enumerate(["ln0_w", "ln0_b"]):
                    act.dma_start(vec_rows[44 + v:45 + v, :], A["L1_attn_" + name].rearrange("(o c) -> o c", o=1))\
                        .then_inc(vec_in, 16)
                act.wait_ge(c_in, 64)
                act.activation(c_silu[:, :, :], c_t[:, :, :], ACT.Silu).then_inc(silu_done, 1)
                load_act_set(nc, act, EXP_LN_SET)
                for c in range(1, NC, 2):
                    act.wait_ge(x_turned, c + 1)
                    act.copy(G.x[:, chunk(c)], G.bank[c][:, :]).then_inc(x_kept, 1)
                act.wait_ge(w_turned, 3)
                act.activation(G.decay[:, :], G.bank[6][:, 4 * DECAY:4 * DECAY + 4], ACT.Exp)\
                    .then_inc(w_kept, 1)

            @block.gpsimd
            def _(pool):
                pool.memset(G.ident[:, :], 0.0).then_inc(const_zero, 1)
                pool.memset(G.mask_qk[:, :], 0.0).then_inc(const_zero, 1)
                pool.memset(G.mask_kq[:, :], 0.0).then_inc(const_zero, 1)
                pool.memset(G.den_row[:, :], 0.0).then_inc(const_zero, 1)
                pool.wait_ge(const_zero, 4)
                pool.affine_select(out=G.ident[:, :], in_=G.ident[:, :], compare_op=ALU.not_equal, fill=1.0, base=0,
                                   pattern=[[-1, P]], channel_multiplier=1).then_inc(const_done, 1)
                pool.affine_select(out=G.mask_qk[:, :], in_=G.mask_qk[:, :], compare_op=ALU.is_ge, fill=NEG, base=0,
                                   pattern=[[-1, P]], channel_multiplier=1).then_inc(const_done, 1)
                pool.affine_select(out=G.mask_kq[:, :], in_=G.mask_kq[:, :], compare_op=ALU.is_ge, fill=NEG, base=0,
                                   pattern=[[1, P]], channel_multiplier=-1).then_inc(const_done, 1)
                pool.affine_select(out=G.den_row[:, :].rearrange("p (g r) -> p g r", g=4),
                                   in_=G.den_row[:, :].rearrange("p (g r) -> p g r", g=4),
                                   compare_op=ALU.not_equal, fill=1.0, base=-DK,
                                   pattern=[[-32, 4], [0, 32]], channel_multiplier=1).then_inc(const_done, 1)
                pool.wait_ge(const_done, 4)
                pool.memset(G.va[:, :, :, :, :], 0.0).then_inc(va_zero, 1)
                pool.wait_ge(va_zero, 1)
                pool.memset(G.va[:, :, :, :, DK:DK + 1], 1.0).then_inc(G.v_pad, 1)
                pool.wait_ge(G.v_pad, 1)
                pool.memset(G.ka[64:96, :, :, :], 1.0).then_inc(G.ones_done, 1)

            @block.vector
            def _(dve):
                dve.memset(G.mean[:, :], 1.0 / P).then_inc(centre_done, 1)
                dve.memset(G.eps[:, :], 1e-5).then_inc(centre_done, 1)
                dve.memset(wo_sp[:, :, :], 0.0).then_inc(sp_zero, 1)
                dve.wait_ge(const_done, 4)
                dve.tensor_scalar(G.centre[:, :], G.ident[:, :], -1.0 / P, None, ALU.add).then_inc(centre_done, 1)
                dve.tensor_copy(G.identb[:, :], G.ident[:, :]).then_inc(centre_done, 1)
                dve.wait_ge(w_in, 80)
                dve.wait_ge(sp_zero, 1)
                dve.tensor_copy(wo_sp[:, :, 0:DK], w_nat[:, 3, :].rearrange("p (h d) -> p h d", h=H))\
                    .then_inc(sp_done, 1)
                for c in range(0, NC, 2):
                    dve.wait_ge(x_turned, c + 1)
                    dve.tensor_copy(G.x[:, chunk(c)], G.bank[c][:, :]).then_inc(x_kept, 1)
                dve.wait_ge(w_turned, 1)
                for i in range(2):
                    dve.tensor_copy(G.wqkv[:, i, :].rearrange("p (d h) -> p h d", d=DK),
                                    G.bank[4][:, chunk(i, P)].rearrange("p (h d) -> p h d", h=H))
                dve.tensor_copy(G.wqkv[:, 2, :], G.bank[4][:, chunk(2, P)]).then_inc(w_kept, 1)
                dve.wait_ge(w_turned, 2)
                dve.tensor_copy(G.wo_t[:, :, :], G.bank[5][:, :].rearrange("p (i m) -> p i m", i=4))\
                    .then_inc(w_kept, 1)
                dve.wait_ge(w_turned, 3)
                dve.wait_ge(w_kept, 3)
                dve.tensor_copy(G.vec[:, :], G.bank[6][:, 0:46]).then_inc(w_kept, 1)
                dve.tensor_copy(G.gate0[:, :], G.bank[6][:, 64:128]).then_inc(w_kept, 1)
                dve.tensor_scalar(G.decay[:, :], G.decay[:, :], -1.0, None, ALU.mult).then_inc(w_kept, 1)
                dve.wait_ge(mod_psum, 1)
                dve.tensor_copy(G.mod[:, :, :, :],
                                G.bank[7][:, 0:24].rearrange("p (l j b) -> p l j b", l=2, j=6)).then_inc(mod_step, 1)
                dve.wait_ge(mod_step, 1)
                gates = G.mod[:, :, 2:6:3, :]
                ones = G.mod[:, :, 1:5:3, :]
                dve.tensor_scalar(sign[:, :, :, :], gates, 0.0, 2.0, ALU.is_ge, ALU.mult).then_inc(mod_step, 1)
                for l in range(2):
                    dve.scalar_tensor_tensor(mag[:, l], gates[:, l], -1.0, gates[:, l], ALU.mult, ALU.max)\
                        .then_inc(mod_step, 1)
                dve.tensor_scalar(ones, ones, 1.0, None, ALU.add).then_inc(mod_step, 1)
                dve.wait_ge(mod_step, 5)
                dve.tensor_scalar(mag[:, :, :, :], mag[:, :, :, :], 0.25, None, ALU.max).then_inc(mod_step, 1)
                dve.wait_ge(mod_step, 6)
                for l in range(2):
                    dve.scalar_tensor_tensor(gates[:, l], sign[:, l], -1.0, mag[:, l], ALU.add, ALU.mult)\
                        .then_inc(mod_done, 1)

            @block.tensor
            def _(pe):
                pe.wait_ge(const_done, 4)
                for c in range(NC):
                    pe.wait_ge(x_in[c], 16)
                    for t in range(4):
                        mm = pe.transpose(G.bank[c][:, chunk(t, P)], x_tok[:, 4 * c + t, :], G.ident[:, :])
                    mm.then_inc(x_turned, 1)
                pe.wait_ge(w_in, 80)
                for i in range(3):
                    mm = pe.transpose(G.bank[4][:, chunk(i, P)], w_nat[:, i, :], G.ident[:, :])
                mm.then_inc(w_turned, 1)
                pe.wait_ge(sp_done, 1)
                for g in range(4):
                    mm = pe.transpose(G.bank[5][:, chunk(g, P)],
                                      wo_sp[:, 4 * g:4 * g + 4, :].rearrange("p h r -> p (h r)"), G.ident[:, :])
                mm.then_inc(w_turned, 1)
                pe.wait_ge(vec_in, 16 * (2 + len(VECS) + 2))
                pe.transpose(G.bank[6][:, 0:46], vec_rows[:, :], G.ident[0:46, 0:46])
                pe.transpose(G.bank[6][:, 64:128], gate_nat[:, :], G.ident[0:64, 0:64]).then_inc(w_turned, 1)
                pe.wait_ge(silu_done, 1)
                for l in range(2):
                    for j in range(6):
                        k = (l * 6 + j) * B
                        mm = pe.matmul(G.bank[7][:, k:k + B], wmod[:, l, j, :], c_silu[:, l, :],
                                       start=True, stop=True)
                mm.then_inc(mod_psum, 1)


def stage_qkv(nc, G):
    mem = G.mem
    with ExitStack() as ctx:
        m = Memory(nc, ctx)
        h = m.sb("h_attn", [P, T])
        part = G.part
        rest = m.sb("rest", [P, 2, 2, CH])
        h_done = mem.sem("h_done")
        qk_psum, v_psum, v_kept = mem.sem("qk_psum"), mem.sem("v_psum"), mem.sem("v_kept")
        hi_done, r1_done, mid_done, lo_done = mem.sem("hi_done"), mem.sem("r1_done"), mem.sem("mid_done"), mem.sem("lo_done")
        parts_out = G.parts_out
        v_pad = G.v_pad
        sa, ca = G.mod[:, 0, 0, :], G.mod[:, 0, 1, :]
        with nc.Block() as block:
            @block.tensor
            def _(pe):
                def project(c):
                    pe.wait_ge(h_done, c + 1)
                    for i in range(2):
                        if c >= 1:
                            pe.wait_ge(lo_done, 2 * (c - 1) + i + 1)
                        pe.matmul(G.bank[4 + i][:, :], G.wqkv[:, i, :], h[:, chunk(c)], start=True, stop=True)\
                            .then_inc(qk_psum, 1)
                    if c >= 1:
                        pe.wait_ge(v_kept, c)
                    for t in range(4):
                        mm = pe.matmul(G.bank[6][:, chunk(t, P)], h[:, chunk(4 * c + t, P)], G.wqkv[:, 2, :],
                                       start=True, stop=True)
                    mm.then_inc(v_psum, 1)

                ln_centre(pe, G, 0, G.x[:, chunk(0)])
                for c in range(NC):
                    if c + 1 < NC:
                        ln_centre(pe, G, c + 1, G.x[:, chunk(c + 1)])
                    ln_variance(pe, G, c)
                    if c >= 1:
                        project(c - 1)
                project(NC - 1)

            @block.scalar
            def _(act):
                def keep(c):
                    for i in range(2):
                        act.wait_ge(qk_psum, 2 * c + i + 1)
                        if c >= 2:
                            act.wait_ge(parts_out[i][c % 2], (16, 48)[i])
                        act.copy(part[:, i, 0, c % 2, :], G.bank[4 + i][:, :]).then_inc(hi_done, 1)
                    act.wait_ge(v_psum, c + 1)
                    for g in range(4):
                        mm = act.copy(G.va[:, 4 * (c // 2) + g, 4 * (c % 2):4 * (c % 2) + 4, :, 0:DK],
                                      G.bank[6][:, :].rearrange("p (t g h d) -> p g t h d", t=4, g=4, h=4)[:, g])
                    mm.then_inc(v_kept, 1)

                ln_square(act, G, 0)
                for c in range(NC):
                    if c + 1 < NC:
                        ln_square(act, G, c + 1)
                    ln_rstd(act, G, c)
                    if c == 0:
                        act.wait_ge(v_pad, 1)
                    if c >= 1:
                        keep(c - 1)
                keep(NC - 1)

            @block.vector
            def _(dve):
                def split(c):
                    for i in range(2):
                        n = 2 * c + i + 1
                        dve.wait_ge(hi_done, n)
                        dve.tensor_tensor(rest[:, i, c % 2, :], G.bank[4 + i][:, :], part[:, i, 0, c % 2, :],
                                          ALU.subtract).then_inc(r1_done, 1)
                    for i in range(2):
                        n = 2 * c + i + 1
                        dve.wait_ge(r1_done, n)
                        dve.tensor_copy(part[:, i, 1, c % 2, :], rest[:, i, c % 2, :]).then_inc(mid_done, 1)
                    for i in range(2):
                        n = 2 * c + i + 1
                        dve.wait_ge(mid_done, n)
                        dve.tensor_tensor(part[:, i, 2, c % 2, :], rest[:, i, c % 2, :], part[:, i, 1, c % 2, :],
                                          ALU.subtract).then_inc(lo_done, 1)

                for c in range(NC):
                    b = c // 2
                    ln_scale(dve, G, c, h[:, chunk(c)], ca[:, b:b + 1])
                    dve.wait_ge(G.ln.scaled, c + 1)
                    dve.tensor_scalar(h[:, chunk(c)], h[:, chunk(c)], sa[:, b:b + 1], None, ALU.add)\
                        .then_inc(h_done, 1)
                    if c >= 1:
                        split(c - 1)
                split(NC - 1)

            @block.sync
            def _(sp):
                def store(c):
                    sp.wait_ge(lo_done, 2 * c + 1)
                    sp.dma_start(G.rows_d[0].rearrange("(a d) h t -> (d h) a t", a=3)[:, :, chunk(c)],
                                 part[:, 0, :, c % 2, :]).then_inc(parts_out[0][c % 2], 16)
                    sp.wait_ge(lo_done, 2 * c + 2)
                    for a in range(3):
                        sp.dma_start(G.rows_d[1].rearrange("(r a d) h t -> a (d h) r t", r=3, a=3)[a][:, :, chunk(c)],
                                     part[:, 1, :, c % 2, :]).then_inc(parts_out[1][c % 2], 16)

                store(0)
                store(1)
                for par in range(2):
                    sp.wait_ge(parts_out[0][par], 16)
                    sp.wait_ge(parts_out[1][par], 48)
                sp.wait_ge(G.ones_done, 1)
                load_group(sp, G, 0)
                store(2)
                store(3)


def load_group(sp, G, g):
    heads, tokens = bass.ds(HG * (g % 4), HG), bass.ds((g // 4) * S, S)
    for r in range(3):
        sp.dma_start(G.qa[3 * DK * r:3 * DK * (r + 1), g % RING, :, :], G.rows_d[0][:, heads, tokens])\
            .then_inc(G.qk_in, 16)
    sp.dma_start(G.ka[0:ROWS, g % RING, :, :], G.rows_d[1][:, heads, tokens]).then_inc(G.qk_in, 16)


def stage_attention(nc, G):
    mem = G.mem
    SCALE = 1.0 / math.sqrt(DK)
    PIECES = [(h, i, k0, min(CH, (i + 1) * P - k0), i if k0 == 0 else 4 + i)
              for h in range(HG) for i in range(8) for k0 in range(0, (i + 1) * P, CH)]
    NP = len(PIECES)
    UNITS = [(c, j, p) for c in range(2) for j in range(4 * c + 4) for p in range(2)]
    NU = len(UNITS)
    NQ = NU // 2
    SCHED, at = [], 0
    for u in range(NU):
        front = range(at, min(NP, at + (6 if u == 0 else 1)))
        back = range(front.stop, min(NP, front.stop + 1))
        SCHED.append((front, back))
        at = back.stop
    assert at == NP
    TURN = next(u for u in range(NU) if SCHED[u][0].stop == NP) + 1
    PV_C0 = 9
    DEN_C0, OUT_C0 = PV_C0 + 2, PV_C0 + 5
    TAIL_DEN = 2

    with ExitStack() as ctx:
        m = Memory(nc, ctx)
        qa, ka, qk_in = G.qa, G.ka, G.qk_in
        va_g = [m.sb(f"va_g{i}", [P, 8, HG, 32]) for i in range(2)]
        pt = m.sb("pt", [P, 4, 2, CH])
        part_max = m.sb("part_max", [P, HG, 12])
        top = m.sb("top", [P, HG, 8])
        neg = m.sb("neg", [P, 3, HG, 8], BF16)
        neg_rest = m.sb("neg_rest", [P, 2, HG, 8])
        neg_t = m.sb("neg_t", [3 * HG * 8, P], BF16)
        acc = m.sb("acc", [P, 2, CH])
        rden = m.sb("rden", [P, 2, CH])

        v_in = mem.sem("v_in")
        piece_psum, piece_max = mem.sem("piece_psum"), mem.sem("piece_max")
        max_step = mem.sem("max_step")
        neg_turned, neg_kept = mem.sem("neg_turned"), mem.sem("neg_kept")
        neg_in = mem.sem("neg_in")
        score_psum, prob_done, pv_done = mem.sem("score_psum"), mem.sem("prob_done"), mem.sem("pv_done")
        acc_kept, den_psum = mem.sem("acc_kept"), mem.sem("den_psum")
        den_log, den_inv, out_done = mem.sem("den_log"), mem.sem("den_inv"), mem.sem("out_done")
        score_bank = [G.pair[0], G.pair[1]]
        max_bank = [G.bank[4], G.bank[5]]
        acc_bank, misc = G.bank[6], G.bank[7]

        def groups(eng, body):
            body(0, 0, first=True)
            body(1, 1)
            with eng.Fori(1, NG // 2 - 1) as pair:
                for k in range(2):
                    body(2 * pair + k, k)
            body(NG - 2, 0)
            body(NG - 1, 1, last=True)

        with nc.Block() as block:
            @block.sync
            def _(sp):
                def neg_rows(g):
                    sp.wait_ge(neg_kept, g + 1)
                    for a in range(3):
                        sp.dma_start(qa[ROWS + a:ROWS + a + 1, g % RING, :, :].rearrange("o h (t c) -> o (h t) c", c=P),
                                     neg_t[32 * a:32 * a + 32, :]).then_inc(neg_in, 16)

                for g in (1, 2):
                    sp.wait_ge(qk_in, 64 * g)
                    load_group(sp, G, g)
                neg_rows(0)
                for par in range(2):
                    sp.wait_ge(G.parts_out[0][par], 32)
                    sp.wait_ge(G.parts_out[1][par], 96)
                neg_rows(1)
                sp.wait_ge(qk_in, 64 * 3)
                load_group(sp, G, 3)
                with sp.Fori(1, NG - 3) as g:
                    scored = NU * g
                    sp.compute_val(scored)
                    sp.wait_ge(qk_in, 64 * (g + 3))
                    sp.wait_ge(score_psum, scored)
                    load_group(sp, G, g + 3)
                    neg_rows(g + 1)
                with sp.Fori(NG - 3, NG - 1) as g:
                    neg_rows(g + 1)

            @block.gpsimd
            def _(pool):
                for g in range(2):
                    pool.tensor_copy(va_g[g][:, :, :, :], G.va[:, g, :, :, :]).then_inc(v_in, 1)
                with pool.Fori(1, NG // 2) as pair:
                    for k in range(2):
                        g = 2 * pair + k
                        pool.wait_ge(pv_done, NQ * (g - 1))
                        pool.tensor_copy(va_g[k][:, :, :, :],
                                         G.va[:, bass.ds(g, 1), :, :, :].rearrange("p o t h r -> p (o t) h r"))\
                            .then_inc(v_in, 1)

            @block.tensor
            def _(pe):
                def pieces(g, which):
                    for n in which:
                        h, i, k0, nk, _ = PIECES[n]
                        if not isinstance(g, int) or NP * g + n >= 2:
                            pe.wait_ge(piece_max, NP * g + n - 1)
                        if n == 0:
                            pe.wait_ge(qk_in, 64 * (g + 1))
                        diagonal = k0 + nk == (i + 1) * P
                        bank = max_bank[n % 2]
                        mm = pe.matmul(bank[:, 0:nk], qa[0:ROWS, g % RING, h, chunk(i, P)],
                                       ka[0:ROWS, g % RING, h, k0:k0 + nk], start=True, stop=True)
                        if diagonal:
                            mm = pe.matmul(bank[:, nk - P:nk], G.identb[:, :], G.mask_qk[:, :], start=False, stop=True,
                                           skip_group_check=True)
                        mm.then_inc(piece_psum, 1)

                def scores(g, u):
                    c, j, p = UNITS[u]
                    q0 = max(CH * c, P * j)
                    n = CH * (c + 1) - q0
                    if u == 0:
                        pe.wait_ge(neg_in, 48 * (g + 1))
                    if u >= 2:
                        pe.wait_ge(prob_done, NU * g + u - 1)
                    for k in range(2):
                        out = score_bank[u % 2][:, k, :]
                        diagonal = j >= 4 * c
                        mm = pe.matmul(out[:, 0:n], ka[0:ROWS + 3, g % RING, 2 * p + k, chunk(j, P)],
                                       qa[0:ROWS + 3, g % RING, 2 * p + k, q0:q0 + n], start=True, stop=True)
                        if diagonal:
                            mm = pe.matmul(out[:, 0:P], G.identb[:, :], G.mask_kq[:, :], start=False, stop=True,
                                           skip_group_check=True)
                    mm.then_inc(score_psum, 1)

                def outputs(g, k, q):
                    c, j, _ = UNITS[2 * q]
                    q0 = max(CH * c, P * j)
                    n = CH * (c + 1) - q0
                    pe.wait_ge(prob_done, NU * g + 2 * q + 2)
                    if q == 0:
                        pe.wait_ge(v_in, g + 1)
                    if j == 0 and (not isinstance(g, int) or 2 * g + c):
                        pe.wait_ge(acc_kept, 2 * g + c)
                    for h in range(HG):
                        mm = pe.matmul(acc_bank[32 * h:32 * h + 32, q0 - CH * c:CH], va_g[k][:, j, h, :],
                                       pt[:, 2 * (q % 2) + h // 2, h % 2, 0:n], start=(j == 0),
                                       stop=(j >= 4 * c), skip_group_check=True)
                    mm.then_inc(pv_done, 1)

                def denominators(g, c):
                    pe.wait_ge(acc_kept, 2 * g + c + 1)
                    if not isinstance(g, int) or 2 * g + c:
                        pe.wait_ge(den_log, 2 * g + c)
                    pe.matmul(misc[:, :], G.den_row[:, :], acc[:, c, :], start=True, stop=True).then_inc(den_psum, 1)

                def turn_neg(g):
                    pe.wait_ge(max_step, 6 * (g + 1))
                    pe.transpose(misc[:, :].bitcast(BF16)[0:3 * HG * 8, 0:P], neg[:, :, :, :].rearrange("p a h t -> p (a h t)"),
                                 G.identb[:, :]).then_inc(neg_turned, 1)

                def group(g, k, first=False, last=False):
                    for u in range(NU):
                        if not last:
                            pieces(g + 1, SCHED[u][0])
                            if u == TURN:
                                pe.wait_ge(den_log, 2 * g + 1)
                                turn_neg(g + 1)
                        scores(g, u)
                        if not last:
                            pieces(g + 1, SCHED[u][1])
                        if u % 2 and u >= 3:
                            outputs(g, k, (u - 3) // 2)
                        if u == DEN_C0:
                            denominators(g, 0)
                        if u == TAIL_DEN and not first:
                            pe.wait_ge(neg_kept, g + 1)
                            denominators(g - 1, 1)
                    outputs(g, k, NQ - 1)

                pieces(0, range(NP))
                turn_neg(0)
                pe.wait_ge(neg_kept, 1)
                groups(pe, group)
                denominators(NG - 1, 1)

            @block.scalar
            def _(act):
                def probabilities(g, u):
                    c, j, p = UNITS[u]
                    n = CH * (c + 1) - max(CH * c, P * j)
                    act.wait_ge(score_psum, NU * g + u + 1)
                    if not isinstance(g, int) or g or u >= 4:
                        act.wait_ge(pv_done, NQ * g + max(0, u // 2 - 1))
                    act.activation(pt[:, u % 4, :, 0:n], score_bank[u % 2][:, :, 0:n], ACT.Exp, scale=SCALE)\
                        .then_inc(prob_done, 1)

                def inverse(g, c):
                    act.wait_ge(den_psum, 2 * g + c + 1)
                    if not isinstance(g, int) or g:
                        act.wait_ge(out_done, 2 * g)
                    act.activation(rden[:, c, :], misc[:, :], ACT.Ln).then_inc(den_log, 1)
                    act.wait_ge(den_log, 2 * g + c + 1)
                    act.activation(rden[:, c, :], rden[:, c, :], ACT.Exp, scale=-1.0).then_inc(den_inv, 1)

                def group(g, k, first=False, last=False):
                    for u in range(NU):
                        probabilities(g, u)
                        if u == DEN_C0 + 1:
                            inverse(g, 0)
                        if u == TAIL_DEN + 1 and not first:
                            inverse(g - 1, 1)

                groups(act, group)
                inverse(NG - 1, 1)

            @block.vector
            def _(dve):
                def pieces(g, which):
                    for n in which:
                        h, i, k0, nk, slot = PIECES[n]
                        dve.wait_ge(piece_psum, NP * g + n + 1)
                        dve.tensor_reduce(part_max[:, h, slot:slot + 1], max_bank[n % 2][:, 0:nk], AX_X, ALU.max)\
                            .then_inc(piece_max, 1)

                def negate(g):
                    dve.wait_ge(piece_max, NP * (g + 1))
                    dve.tensor_tensor(part_max[:, :, 4:8], part_max[:, :, 4:8], part_max[:, :, 8:12], ALU.max)\
                        .then_inc(max_step, 1)
                    dve.wait_ge(max_step, 6 * g + 1)
                    dve.tensor_scalar(neg[:, 0, :, :], part_max[:, :, 0:8], -1.0, None, ALU.mult).then_inc(max_step, 1)
                    dve.wait_ge(max_step, 6 * g + 2)
                    dve.scalar_tensor_tensor(neg_rest[:, 0, :, :], part_max[:, :, 0:8], -1.0, neg[:, 0, :, :],
                                             ALU.mult, ALU.subtract).then_inc(max_step, 1)
                    dve.wait_ge(max_step, 6 * g + 3)
                    dve.tensor_copy(neg[:, 1, :, :], neg_rest[:, 0, :, :]).then_inc(max_step, 1)
                    dve.wait_ge(max_step, 6 * g + 4)
                    dve.tensor_tensor(neg_rest[:, 1, :, :], neg_rest[:, 0, :, :], neg[:, 1, :, :], ALU.subtract)\
                        .then_inc(max_step, 1)
                    dve.wait_ge(max_step, 6 * g + 5)
                    dve.tensor_copy(neg[:, 2, :, :], neg_rest[:, 1, :, :]).then_inc(max_step, 1)

                def keep_neg(g):
                    dve.wait_ge(neg_turned, g + 1)
                    if not isinstance(g, int) or g:
                        dve.wait_ge(neg_in, 48 * g)
                    dve.tensor_copy(neg_t[:, :], misc[:, :].bitcast(BF16)[0:3 * HG * 8, 0:P]).then_inc(neg_kept, 1)

                def keep_acc(g, c):
                    dve.wait_ge(pv_done, NQ * g + (4, NQ)[c])
                    dve.tensor_copy(acc[:, c, :], acc_bank[:, :]).then_inc(acc_kept, 1)

                def normalise(g, c):
                    dve.wait_ge(den_inv, 2 * g + c + 1)
                    dve.tensor_tensor(G.o[:, g % 4, bass.ds((g // 4) * S + c * CH, CH)], acc[:, c, :], rden[:, c, :],
                                      ALU.mult).then_inc(out_done, 1)

                def group(g, k, first=False, last=False):
                    for u in range(NU):
                        if not last:
                            for which in SCHED[u]:
                                pieces(g + 1, which)
                            if u == TURN:
                                negate(g + 1)
                                keep_neg(g + 1)
                        if u == PV_C0 + 1:
                            keep_acc(g, 0)
                        if u == OUT_C0:
                            normalise(g, 0)
                        if u == 0 and not first:
                            keep_acc(g - 1, 1)
                        if u == TAIL_DEN + 2 and not first:
                            normalise(g - 1, 1)

                pieces(0, range(NP))
                negate(0)
                keep_neg(0)
                groups(dve, group)
                keep_acc(NG - 1, 1)
                normalise(NG - 1, 1)


BIG = 3e38


def stage_router(nc, G):
    mem = G.mem
    E, GROUPS, KEEP_GROUPS, TOP = 64, 8, 4, 6
    PER = E // GROUPS
    with ExitStack() as ctx:
        m = Memory(nc, ctx)
        score = m.sb("score", [P, NT, E])
        wide = m.sb("wide", [P, NT, E + 2])
        wide_out = m.sb("wide_out", [P, NT, E + 2])
        gmax = m.sb("gmax", [P, NT, 12])
        gmax_out = m.sb("gmax_out", [P, NT, 12])
        gmask = m.sb("gmask", [P, NT, GROUPS])
        best = m.sb("best", [P, NT, 8])
        pick = m.sb("pick", [P, NT, 8])
        best6 = m.sb("best6", [P, NT, 8])
        pick6 = m.sb("pick6", [P, NT, 8])
        total = m.sb("total", [P, NT, 1])
        chosen = m.sb("chosen", [P, NT, E])
        part = m.sb("comb_part", [E, 2, 3, CH], BF16)
        rest = m.sb("comb_rest", [E, 2, CH])
        wo_psum, x_new, h_done = mem.sem("wo_psum"), mem.sem("x_new"), mem.sem("h2_done")
        logit_psum, exp_done = mem.sem("logit_psum"), mem.sem("gate_exp")
        pads, step, comb_done = mem.sem("route_pads"), mem.sem("route_step"), mem.sem("comb_done")
        comb_psum, comb_split = mem.sem("comb_psum"), mem.sem("comb_split")
        comb_out = [mem.sem(f"comb_out{k}") for k in range(2)]
        ga, cb, sb_ = G.mod[:, 0, 2, :], G.mod[:, 0, 4, :], G.mod[:, 0, 3, :]
        n0 = G.ln_count
        G.ln_count += NC
        with nc.Block() as block:
            @block.tensor
            def _(pe):
                def project(c):
                    if c >= 1:
                        pe.wait_ge(x_new, c)
                    for g in range(4):
                        mm = pe.matmul(G.bank[4][:, :], G.wo_t[:, g, :], G.o[:, g, chunk(c)], start=(g == 0), stop=(g == 3))
                    mm.then_inc(wo_psum, 1)

                def logits(c):
                    pe.wait_ge(h_done, c + 1)
                    if c >= 1:
                        pe.wait_ge(exp_done, c)
                    for t in range(4):
                        mm = pe.matmul(G.bank[5][:, chunk(t, E)], G.h[:, chunk(4 * c + t, P)], G.gate0[:, :],
                                       start=True, stop=True)
                    mm.then_inc(logit_psum, 1)

                def turn(c):
                    pe.wait_ge(comb_done, c + 1)
                    if c >= 1:
                        pe.wait_ge(comb_split, 5 * c)
                    for t in range(4):
                        mm = pe.transpose(G.bank[6][0:E, chunk(t, P)], chosen[:, 4 * c + t, :], G.ident[:, :])
                    mm.then_inc(comb_psum, 1)

                project(0)
                for c in range(NC):
                    if c + 1 < NC:
                        project(c + 1)
                    pe.wait_ge(x_new, c + 1)
                    ln_centre(pe, G, n0 + c, G.x[:, chunk(c)])
                    ln_variance(pe, G, n0 + c)
                    logits(c)
                    if c >= 1:
                        turn(c - 1)
                turn(NC - 1)

            @block.scalar
            def _(act):
                for c in range(NC):
                    ln_square(act, G, n0 + c)
                    ln_rstd(act, G, n0 + c)
                    act.wait_ge(logit_psum, c + 1)
                    act.activation(score[:, 4 * c:4 * c + 4, :],
                                   G.bank[5][:, 0:4 * E].rearrange("p (t e) -> p t e", t=4), ACT.Exp, scale=-1.0)\
                        .then_inc(exp_done, 1)

            @block.vector
            def _(dve):
                count = [0]

                def link(ins):
                    count[0] += 1
                    ins.then_inc(step, 1)
                    dve.wait_ge(step, count[0])

                def residual(c):
                    dve.wait_ge(wo_psum, c + 1)
                    dve.scalar_tensor_tensor(G.x[:, chunk(c)], G.bank[4][:, :], ga[:, c // 2:c // 2 + 1],
                                             G.x[:, chunk(c)], ALU.mult, ALU.add).then_inc(x_new, 1)

                def route(c):
                    t4 = slice(4 * c, 4 * c + 4)
                    sc = score[:, t4, :]
                    dve.wait_ge(exp_done, c + 1)
                    link(dve.tensor_scalar(sc, sc, 1.0, None, ALU.add))
                    link(dve.reciprocal(sc, sc))
                    link(dve.tensor_tensor(sc, sc, G.gate_bias[:, :].unsqueeze(1).to_broadcast([P, 4, E]), ALU.add))
                    link(dve.tensor_reduce(gmax[:, t4, 0:GROUPS], sc.rearrange("p t (g e) -> p t g e", g=GROUPS), AX_X, ALU.max))
                    for t in range(4 * c, 4 * c + 4):
                        last = dve.max(best[:, t, :], gmax[:, t, 0:GROUPS])
                    link(last)
                    link(dve.tensor_copy(pick[:, t4, 0:KEEP_GROUPS], best[:, t4, 0:KEEP_GROUPS]))
                    for t in range(4 * c, 4 * c + 4):
                        last = dve.match_replace(gmax_out[:, t, :], pick[:, t, :], gmax[:, t, :], -BIG)
                    link(last)
                    link(dve.tensor_tensor(gmask[:, t4, :], gmax_out[:, t4, 0:GROUPS], gmax[:, t4, 0:GROUPS], ALU.not_equal))
                    for t in range(4 * c, 4 * c + 4):
                        last = dve.tensor_tensor(wide[:, t, 0:E].rearrange("p (g e) -> p g e", g=GROUPS),
                                                 score[:, t, :].rearrange("p (g e) -> p g e", g=GROUPS),
                                                 gmask[:, t, :].unsqueeze(2).to_broadcast([P, GROUPS, PER]), ALU.mult)
                    link(last)
                    for t in range(4 * c, 4 * c + 4):
                        last = dve.max(best6[:, t, :], wide[:, t, 0:E])
                    link(last)
                    link(dve.tensor_copy(pick6[:, t4, 0:TOP], best6[:, t4, 0:TOP]))
                    link(dve.tensor_reduce(total[:, t4, 0], best6[:, t4, 0:TOP], AX_X, ALU.add))
                    link(dve.tensor_scalar(total[:, t4, :], total[:, t4, :], 1e-8, None, ALU.add))
                    link(dve.reciprocal(total[:, t4, :], total[:, t4, :]))
                    for t in range(4 * c, 4 * c + 4):
                        last = dve.match_replace(wide_out[:, t, :], pick6[:, t, :], wide[:, t, :], -BIG)
                    link(last)
                    link(dve.tensor_tensor(chosen[:, t4, :], wide_out[:, t4, 0:E], wide[:, t4, 0:E], ALU.not_equal))
                    link(dve.tensor_tensor(chosen[:, t4, :], chosen[:, t4, :], wide[:, t4, 0:E], ALU.mult))
                    dve.tensor_tensor(chosen[:, t4, :], chosen[:, t4, :], total[:, t4, :].to_broadcast([P, 4, E]),
                                      ALU.mult).then_inc(comb_done, 1)

                def split(c):
                    k = c % 2
                    dve.wait_ge(comb_psum, c + 1)
                    if c >= 2:
                        dve.wait_ge(comb_out[k], 16 * (c // 2))
                    dve.tensor_copy(part[:, k, 0, :], G.bank[6][0:E, :]).then_inc(comb_split, 1)
                    dve.wait_ge(comb_split, 5 * c + 1)
                    dve.tensor_tensor(rest[:, k, :], G.bank[6][0:E, :], part[:, k, 0, :], ALU.subtract).then_inc(comb_split, 1)
                    dve.wait_ge(comb_split, 5 * c + 2)
                    dve.tensor_copy(part[:, k, 1, :], rest[:, k, :]).then_inc(comb_split, 1)
                    dve.wait_ge(comb_split, 5 * c + 3)
                    dve.tensor_tensor(rest[:, k, :], rest[:, k, :], part[:, k, 1, :], ALU.subtract).then_inc(comb_split, 1)
                    dve.wait_ge(comb_split, 5 * c + 4)
                    dve.tensor_copy(part[:, k, 2, :], rest[:, k, :]).then_inc(comb_split, 1)

                link(dve.memset(wide[:, :, E:E + 2], BIG))
                link(dve.memset(gmax[:, :, GROUPS:12], BIG))
                link(dve.memset(pick[:, :, KEEP_GROUPS:8], BIG))
                link(dve.memset(pick6[:, :, TOP:8], BIG))
                residual(0)
                for c in range(NC):
                    if c + 1 < NC:
                        residual(c + 1)
                    ln_scale(dve, G, n0 + c, G.h[:, chunk(c)], cb[:, c // 2:c // 2 + 1])
                    dve.wait_ge(G.ln.scaled, n0 + c + 1)
                    dve.tensor_scalar(G.h[:, chunk(c)], G.h[:, chunk(c)], sb_[:, c // 2:c // 2 + 1], None, ALU.add)\
                        .then_inc(h_done, 1)
                    route(c)
                    if c >= 1:
                        split(c - 1)
                split(NC - 1)

            @block.sync
            def _(sp):
                for c in range(NC):
                    sp.wait_ge(comb_split, 5 * c + 5)
                    sp.dma_start(G.comb_d[:, :, chunk(c)], part[:, c % 2, :, :]).then_inc(comb_out[c % 2], 16)
                for k in range(2):
                    sp.wait_ge(comb_out[k], 16 * NC // 2)


def stage_experts(nc, G, A):
    mem = G.mem
    STEPS = 33
    with ExitStack() as ctx:
        m = Memory(nc, ctx)
        raw = [m.sb(f"moe_raw{k}", [P, 3, P]) for k in range(2)]
        comb6 = [m.sb(f"comb6_{k}", [6, T], BF16) for k in range(2)]
        wt = [m.sb(f"moe_wt{k}", [P, 3, P]) for k in range(2)]
        sel6 = m.sb("sel6", [6, P], BF16)
        one = m.sb("one", [1, CH], BF16)
        sg = m.sb("moe_silu", [P, 2, CH])
        gu = m.sb("moe_gu", [P, 2, CH])
        hid = m.sb("moe_hid", [P, NC, CH])
        raw_in = [mem.sem(f"moe_raw_in{k}") for k in range(2)]
        comb_in = [mem.sem(f"moe_comb_in{k}") for k in range(2)]
        sel_done = mem.sem("sel_done")
        w_turned, w_kept = mem.sem("moe_turned"), mem.sem("moe_kept")
        g_psum, u_psum, c_psum, y_psum = mem.sem("moe_g"), mem.sem("moe_u"), mem.sem("moe_c"), mem.sem("moe_y")
        silu_done, gu_done, hid_done = mem.sem("moe_silu_done"), mem.sem("moe_gu_done"), mem.sem("moe_hid_done")
        y_bank, g_bank, u_bank, c_bank, t_bank = G.bank[0:4], G.bank[4], G.bank[5], G.bank[6], G.bank[7]

        def steps(eng, body):
            body(0, 0)
            with eng.Fori(0, (STEPS - 3) // 2) as i:
                body(2 * i + 1, 1)
                body(2 * i + 2, 0)
            body(STEPS - 2, 1)
            body(STEPS - 1, 0, last=True)

        def before(s, c):
            return not isinstance(s, int) or 4 * s + c >= 1

        with nc.Block() as block:
            @block.sync
            def _(sp):
                def weights(s, k):
                    e = 2 * (s - 1)
                    for j, name in enumerate(("eg_w", "eu_w")):
                        sp.dma_start(raw[k][:, j, :], A["L0_ffn_" + name].rearrange("e i h -> (e i) h")
                                     [bass.ds(64 * e, P), :]).then_inc(raw_in[k], 16)
                    sp.dma_start(raw[k][:, 2, :].rearrange("h (e i) -> h e i", e=2),
                                 A["L0_ffn_ed_w"][bass.ds(e, 2), :, :].rearrange("e h i -> h e i")).then_inc(raw_in[k], 16)

                def factors(s, k):
                    sp.dma_start(comb6[k][:, :], G.comb_d.rearrange("e a n -> (e a) n")[bass.ds(6 * (s - 1), 6), :])\
                        .then_inc(comb_in[k], 16)

                for j, name in enumerate(("sg_w", "su_w", "sd_w")):
                    sp.dma_start(raw[0][:, j, :], A["L0_ffn_" + name]).then_inc(raw_in[0], 16)
                weights(1, 1)
                factors(1, 1)
                sp.wait_ge(w_turned, 1)
                weights(2, 0)
                factors(2, 0)
                with sp.Fori(0, (STEPS - 3) // 2) as i:
                    for k in (1, 0):
                        s = 2 * i + 2 - k
                        sp.wait_ge(w_turned, s + 1)
                        weights(s + 2, k)
                        sp.wait_ge(c_psum, 4 * s + 4)
                        factors(s + 2, k)

            @block.gpsimd
            def _(pool):
                pool.memset(sel6[:, :], 1.0).then_inc(sel_done, 1)
                pool.memset(one[:, :], 1.0).then_inc(sel_done, 1)
                pool.wait_ge(sel_done, 2)
                pool.affine_select(out=sel6[:, 0:64], in_=sel6[:, 0:64], compare_op=ALU.is_ge, fill=0.0, base=2,
                                   pattern=[[0, 64]], channel_multiplier=-1).then_inc(sel_done, 1)
                pool.affine_select(out=sel6[:, 64:P], in_=sel6[:, 64:P], compare_op=ALU.is_ge, fill=0.0, base=-3,
                                   pattern=[[0, 64]], channel_multiplier=1).then_inc(sel_done, 1)

            @block.tensor
            def _(pe):
                def turn(s, k):
                    pe.wait_ge(raw_in[k], 48 * (s // 2 + 1))
                    pe.wait_ge(w_kept, s)
                    for j in range(3):
                        mm = pe.transpose(t_bank[:, chunk(j, P)], raw[k][:, j, :], G.ident[:, :])
                    mm.then_inc(w_turned, 1)

                def down(s, c, k, first, last):
                    pe.wait_ge(hid_done, 4 * s + c + 1)
                    pe.matmul(y_bank[c][:, :], wt[k][:, 2, :], hid[:, c, :], start=first, stop=last,
                              skip_group_check=True).then_inc(y_psum, 1)

                def step(s, k, last=False):
                    for c in range(NC):
                        if c == 0:
                            pe.wait_ge(w_kept, s + 1)
                        if before(s, c):
                            pe.wait_ge(silu_done, 4 * s + c)
                        pe.matmul(g_bank[:, :], wt[k][:, 0, :], G.h[:, chunk(c)], start=True, stop=True).then_inc(g_psum, 1)
                        if c == 1 and not last:
                            turn(s + 1, 1 - k)
                        if c >= 2:
                            down(s, c - 2, k, isinstance(s, int) and s == 0, last)
                        elif not isinstance(s, int) or s >= 1:
                            down(s - 1, c + 2, 1 - k, isinstance(s, int) and s == 1, False)
                        if before(s, c):
                            pe.wait_ge(gu_done, 4 * s + c)
                        pe.matmul(u_bank[:, :], wt[k][:, 1, :], G.h[:, chunk(c)], start=True, stop=True).then_inc(u_psum, 1)
                        if before(s, c):
                            pe.wait_ge(hid_done, 4 * s + c)
                        if isinstance(s, int) and s == 0:
                            pe.matmul(c_bank[:, :], one[:, 0:P], one[:, :], start=True, stop=True).then_inc(c_psum, 1)
                        else:
                            if c == 0:
                                pe.wait_ge(comb_in[k], 16 * ((s + 1) // 2))
                            pe.matmul(c_bank[:, :], sel6[:, :], comb6[k][:, chunk(c)], start=True, stop=True)\
                                .then_inc(c_psum, 1)
                    if last:
                        down(s, 2, k, False, True)
                        down(s, 3, k, False, True)

                turn(0, 0)
                pe.wait_ge(sel_done, 4)
                step(0, 0)
                step(1, 1)
                with pe.Fori(0, (STEPS - 3) // 2) as i:
                    step(2 * i + 2, 0)
                    step(2 * i + 3, 1)
                step(STEPS - 1, 0, last=True)

            @block.scalar
            def _(act):
                def keep_weights(s, k):
                    act.wait_ge(w_turned, s + 1)
                    if not isinstance(s, int) or s >= 2:
                        act.wait_ge(y_psum, 4 * (s - 1))
                    act.copy(wt[k][:, :, :], t_bank[:, 0:3 * P].rearrange("p (j m) -> p j m", j=3)).then_inc(w_kept, 1)

                def step(s, k, last=False):
                    for c in range(NC):
                        act.wait_ge(g_psum, 4 * s + c + 1)
                        if not isinstance(s, int) or 4 * s + c >= 2:
                            act.wait_ge(gu_done, 4 * s + c - 1)
                        act.activation(sg[:, c % 2, :], g_bank[:, :], ACT.Silu).then_inc(silu_done, 1)
                        if c == 1 and not last:
                            keep_weights(s + 1, 1 - k)

                keep_weights(0, 0)
                steps(act, step)
                load_act_set(nc, act, EXP_LN_SET)

            @block.vector
            def _(dve):
                def step(s, k, last=False):
                    for c in range(NC):
                        n = 4 * s + c
                        dve.wait_ge(silu_done, n + 1)
                        dve.wait_ge(u_psum, n + 1)
                        dve.tensor_tensor(gu[:, c % 2, :], sg[:, c % 2, :], u_bank[:, :], ALU.mult).then_inc(gu_done, 1)
                        dve.wait_ge(gu_done, n + 1)
                        dve.wait_ge(c_psum, n + 1)
                        if not isinstance(s, int) or n >= 4:
                            dve.wait_ge(y_psum, n - 3)
                        dve.tensor_tensor(hid[:, c, :], gu[:, c % 2, :], c_bank[:, :], ALU.mult).then_inc(hid_done, 1)

                steps(dve, step)
                for c in range(NC):
                    dve.wait_ge(y_psum, 4 * (STEPS - 1) + c + 1)
                    dve.scalar_tensor_tensor(G.x[:, chunk(c)], y_bank[c][:, :], G.mod[:, 0, 5, c // 2:c // 2 + 1],
                                             G.x[:, chunk(c)], ALU.mult, ALU.add).then_inc(G.x_l0, 1)


def stage_rwkv_in(nc, G):
    mem = G.mem
    with ExitStack() as ctx:
        m = Memory(nc, ctx)
        h = m.sb("h_mod", [P, T])
        h_done = mem.sem("h3_done")
        n0 = G.ln_count
        G.ln_count += 2 * NC
        ca, sa = G.mod[:, 1, 1, :], G.mod[:, 1, 0, :]
        w, b = G.vec[:, 44:45], G.vec[:, 45:46]
        CALLS = [(0, 0), (0, 1), (0, 2), (1, 0), (0, 3), (1, 1), (1, 2), (1, 3)]
        with nc.Block() as block:
            @block.tensor
            def _(pe):
                for n, (which, c) in enumerate(CALLS):
                    if which == 1:
                        pe.wait_ge(h_done, c + 1)
                    ln_centre(pe, G, n0 + n, (h if which else G.x)[:, chunk(c)])
                    if n >= 1:
                        ln_variance(pe, G, n0 + n - 1)
                ln_variance(pe, G, n0 + 7)

            @block.scalar
            def _(act):
                for n in range(len(CALLS)):
                    ln_square(act, G, n0 + n)
                    if n >= 1:
                        ln_rstd(act, G, n0 + n - 1)
                ln_rstd(act, G, n0 + 7)

            @block.vector
            def _(dve):
                for n, (which, c) in enumerate(CALLS):
                    bb = c // 2
                    if which == 0:
                        ln_scale(dve, G, n0 + n, h[:, chunk(c)], ca[:, bb:bb + 1])
                        dve.wait_ge(G.ln.scaled, n0 + n + 1)
                        dve.tensor_scalar(h[:, chunk(c)], h[:, chunk(c)], sa[:, bb:bb + 1], None, ALU.add).then_inc(h_done, 1)
                    else:
                        ln_scale(dve, G, n0 + n, G.r[:, chunk(c)], w)
                        dve.wait_ge(G.ln.scaled, n0 + n + 1)
                        dve.tensor_scalar(G.r[:, chunk(c)], G.r[:, chunk(c)], b, None, ALU.add).then_inc(G.r_done, 1)


def stage_rwkv(nc, G, A):
    mem = G.mem
    WK, WV, WR, WO, WCR, WCK, WCV = 0, 1, 2, 3, 4, 5, 9
    NB = 13
    STEPS = 13
    with ExitStack() as ctx:
        m = Memory(nc, ctx)
        raw = m.sb("rw_raw", [P, NB, P])
        wt = m.sb("rw_wt", [P, NB + 3, P])
        vv = m.sb("rw_vec", [P, 12])
        hp = m.sb("hp", [P, B, S + 1])
        diff = m.sb("diff", [P, 2, CH])
        mix = m.sb("mix", [P, 3, 2, CH])
        k_s, v_s, sr = (m.sb(n, [P, B, S]) for n in ("k_s", "v_s", "sr"))
        pp, aa, bb = (m.sb(n, [P, S + 1]) for n in ("pp", "aa", "bb"))
        e1b, e2b, e1, e2, qq, d1, n2, rw = (m.sb(n, [P, S]) for n in ("e1b", "e2b", "e1", "e2", "qq", "d1", "n2", "rw"))
        rl = m.sb("relu", [P, 2, CH])
        kf = m.sb("kf", [P, 4, 2, CH])
        sc, kvs = m.sb("sc", [P, 2, CH]), m.sb("kvs", [P, 2, CH])

        w_in = mem.sem("rw_w_in")
        w_turned, w_kept = mem.sem("rw_turned"), mem.sem("rw_kept")
        start = mem.sem("rw_start")
        vec_done = mem.sem("rw_vec_done")
        h_step, h_done = mem.sem("rw_h_step"), mem.sem("rw_h_done")
        mix1, mix2 = mem.sem("rw_mix1"), mem.sem("rw_mix2")
        k_psum, v_psum, r_psum = mem.sem("rw_k"), mem.sem("rw_v"), mem.sem("rw_r")
        k_kept, v_kept, sr_done = mem.sem("rw_k_kept"), mem.sem("rw_v_kept"), mem.sem("rw_sr")
        wd, wa, wp = mem.sem("wkv_dve"), mem.sem("wkv_act"), mem.sem("wkv_pool")
        o_psum, r_mid = mem.sem("rw_o"), mem.sem("rw_r_mid")
        cr_psum, sc_done = mem.sem("rw_cr"), mem.sem("rw_sc")
        f_psum, relu_done, kf_done = mem.sem("rw_f"), mem.sem("rw_relu"), mem.sem("rw_kf")
        kv_psum, kv_step, r_new = mem.sem("rw_kv"), mem.sem("rw_kv_step"), mem.sem("rw_r_new")
        n0 = G.ln_count
        G.ln_count += 8 * LAYERS
        pair = G.psum3

        def seq(b, q):
            return slice(b * S + q * CH, b * S + (q + 1) * CH)

        with nc.Block() as block:
            @block.sync
            def _(sp):
                with sp.Fori(0, LAYERS) as l:
                    sp.wait_ge(w_turned, 4 * l)
                    one = bass.ds(l, 1)
                    for i, name in enumerate(("Wk", "Wv", "Wr", "Wo", "Wcr")):
                        sp.dma_start(raw[:, i, :], A["L1_attn_" + name][one].rearrange("o a c -> (o a) c"))\
                            .then_inc(w_in, 16)
                    sp.dma_start(raw[:, WCK:WCK + 4, :],
                                 A["L1_attn_Wck"][one].rearrange("o (j f) c -> f (o j) c", f=P)).then_inc(w_in, 16)
                    sp.dma_start(raw[:, WCV:WCV + 4, :].rearrange("p j f -> p (j f)"),
                                 A["L1_attn_Wcv"][one].rearrange("o c f -> (o c) f")).then_inc(w_in, 16)

            @block.tensor
            def _(pe):
                def turn(l):
                    pe.wait_ge(w_in, 112 * (l + 1))
                    pe.wait_ge(relu_done, 16 * l)
                    pe.wait_ge(r_new, 4 * l)
                    for i in range(NB):
                        mm = pe.transpose(G.bank[4 + i // 4][:, chunk(i % 4, P)], raw[:, i, :], G.ident[:, :])
                        if i % 4 == 3 or i == NB - 1:
                            mm.then_inc(w_turned, 1)

                def time_mix(l, b):
                    n = n0 + 8 * l + 2 * b
                    if b == 0:
                        pe.wait_ge(sc_done, 2 * l)
                    for q in range(2):
                        ln_centre(pe, G, n + q, G.r[:, seq(b, q)], q)
                    for q in range(2):
                        ln_variance(pe, G, n + q, q)
                    for q in range(2):
                        ch = 4 * l + 2 * b + q
                        pe.wait_ge(mix1, ch + 1)
                        if b == 0 and q == 0:
                            pe.wait_ge(w_kept, 4 * (l + 1))
                        pe.wait_ge(k_kept, ch)
                        pe.matmul(G.bank[4][:, :], wt[:, WK, :], mix[:, 0, q, :], start=True, stop=True).then_inc(k_psum, 1)
                        pe.wait_ge(v_kept, ch)
                        pe.matmul(G.bank[5][:, :], wt[:, WV, :], mix[:, 1, q, :], start=True, stop=True).then_inc(v_psum, 1)
                        pe.wait_ge(sr_done, 2 * l + b)
                        pe.matmul(G.bank[6 + q][:, :], wt[:, WR, :], mix[:, 2, q, :], start=True, stop=True)\
                            .then_inc(r_psum, 1)

                def output(l, b):
                    for q in range(2):
                        pe.wait_ge(wd, STEPS * (2 * l + b + 1))
                        if b == 0:
                            pe.wait_ge((k_kept, v_kept)[q], 4 * l + 4)
                        else:
                            pe.wait_ge(relu_done, 8 * (2 * l + 1))
                        pe.matmul(G.bank[4 + q][:, :], wt[:, WO, :], rw[:, chunk(q)], start=True, stop=True)\
                            .then_inc(o_psum, 1)
                    n = n0 + 8 * l + 4 + 2 * b
                    for q in range(2):
                        pe.wait_ge(r_mid, 4 * l + 2 * b + q + 1)
                        ln_centre(pe, G, n + q, G.r[:, seq(b, q)], q)
                    if b == 1:
                        pe.wait_ge(sc_done, 2 * l + 1)
                    for q in range(2):
                        ln_variance(pe, G, n + q, q)

                def channel_mix(l, b):
                    u = 2 * l + b

                    def up(q, j):
                        if 4 * q + j >= 2:
                            pe.wait_ge(relu_done, 8 * u + 4 * q + j - 1)
                        pe.matmul(G.bank[4 + j % 2][:, :], wt[:, WCK + j, :], mix[:, 0, q, :], start=True, stop=True)\
                            .then_inc(f_psum, 1)

                    def down(q, j):
                        pe.wait_ge(kf_done, 8 * u + 4 * q + j + 1)
                        if j == 0:
                            if b == 0:
                                pe.wait_ge(sr_done, 2 * l + 2)
                            else:
                                pe.wait_ge(r_new, 4 * l + 2)
                        mm = pe.matmul(G.bank[6 + q][:, :], wt[:, WCV + j, :], kf[:, j, q, :], start=(j == 0), stop=(j == 3))
                        if j == 3:
                            mm.then_inc(kv_psum, 1)

                    for q in range(2):
                        pe.wait_ge(mix2, 2 * u + q + 1)
                        up(q, 0)
                        up(q, 1)
                        mm = pe.matmul(G.bank[2 + q][:, :], wt[:, WCR, :], mix[:, 2, q, :], start=True, stop=True)
                        if q == 1:
                            mm.then_inc(cr_psum, 1)
                        for j in range(4):
                            if q == 1:
                                down(0, j)
                            if j < 2:
                                up(q, j + 2)
                    for j in range(4):
                        down(1, j)

                with pe.Fori(0, LAYERS) as l:
                    turn(l)
                    time_mix(l, 0)
                    time_mix(l, 1)
                    for b in range(B):
                        output(l, b)
                        channel_mix(l, b)

            @block.scalar
            def _(act):
                def time_mix(l, b):
                    n = n0 + 8 * l + 2 * b
                    for q in range(2):
                        ln_square(act, G, n + q, q)
                    for q in range(2):
                        ln_rstd(act, G, n + q, q)
                    for q in range(2):
                        ch = 4 * l + 2 * b + q
                        act.wait_ge(k_psum, ch + 1)
                        act.copy(k_s[:, b, chunk(q)], G.bank[4][:, :]).then_inc(k_kept, 1)
                        act.wait_ge(v_psum, ch + 1)
                        act.copy(v_s[:, b, chunk(q)], G.bank[5][:, :]).then_inc(v_kept, 1)
                    act.wait_ge(r_psum, 4 * l + 2 * b + 2)
                    act.activation(sr[:, b, :].rearrange("p (q n) -> p q n", q=2), pair[:, 6:8, :], ACT.Sigmoid)\
                        .then_inc(sr_done, 1)
                    load_act_set(nc, act, EXP_LN_SET)

                def decays(u):
                    act.wait_ge(wd, STEPS * u + 2)
                    act.activation(e1b[:, :], e1b[:, :], ACT.Exp).then_inc(wa, 1)
                    act.wait_ge(wp, 3 * u + 1)
                    act.activation(e2b[:, :], e2b[:, :], ACT.Exp).then_inc(wa, 1)

                def weights(u):
                    act.wait_ge(wd, STEPS * u + 4)
                    act.activation(e1[:, :], e1[:, :], ACT.Exp).then_inc(wa, 1)
                    act.wait_ge(wd, STEPS * u + 5)
                    act.activation(e2[:, :], e2[:, :], ACT.Exp).then_inc(wa, 1)

                def inverse(u):
                    act.wait_ge(wd, STEPS * u + 11)
                    act.activation(e1[:, :], e1[:, :], ACT.Ln).then_inc(wa, 1)
                    act.wait_ge(wa, 6 * u + 5)
                    act.activation(e1[:, :], e1[:, :], ACT.Exp, scale=-1.0).then_inc(wa, 1)

                def relus(u, q):
                    for j in range(4):
                        f = 8 * u + 4 * q + j
                        act.wait_ge(f_psum, f + 1)
                        if 4 * q + j >= 2:
                            act.wait_ge(kf_done, f - 1)
                        else:
                            act.wait_ge(kf_done, 8 * u)
                        act.activation(rl[:, j % 2, :], G.bank[4 + j % 2][:, :], ACT.Relu).then_inc(relu_done, 1)

                def gate(u):
                    act.wait_ge(cr_psum, u + 1)
                    act.activation(sc[:, :, :], pair[:, 2:4, :], ACT.Sigmoid).then_inc(sc_done, 1)
                    load_act_set(nc, act, EXP_LN_SET)

                def norm2(l, b):
                    n = n0 + 8 * l + 4 + 2 * b
                    for q in range(2):
                        ln_square(act, G, n + q, q)
                    for q in range(2):
                        ln_rstd(act, G, n + q, q)

                with act.Fori(0, LAYERS) as l:
                    for i in range(2):
                        act.wait_ge(w_turned, 4 * l + i + 1)
                        act.copy(wt[:, 4 * i:4 * i + 4, :].rearrange("p j m -> p (j m)"), G.bank[4 + i][:, :])\
                            .then_inc(w_kept, 1)
                    time_mix(l, 0)
                    time_mix(l, 1)
                    decays(2 * l)
                    weights(2 * l)
                    inverse(2 * l)
                    norm2(l, 0)
                    decays(2 * l + 1)
                    relus(2 * l, 0)
                    weights(2 * l + 1)
                    relus(2 * l, 1)
                    inverse(2 * l + 1)
                    gate(2 * l)
                    norm2(l, 1)
                    relus(2 * l + 1, 0)
                    relus(2 * l + 1, 1)
                    gate(2 * l + 1)

            @block.gpsimd
            def _(pool):
                def recurrence(l, b):
                    u = 2 * l + b
                    pool.wait_ge(wd, STEPS * u + 1)
                    pool.tensor_tensor(e2b[:, :], k_s[:, b, :], pp[:, 1:S + 1], ALU.subtract).then_inc(wp, 1)
                    pool.wait_ge(wa, 6 * u + 4)
                    pool.tensor_tensor(n2[:, :], e2[:, :], v_s[:, b, :], ALU.mult).then_inc(wp, 1)
                    pool.wait_ge(wd, STEPS * u + 9)
                    pool.tensor_tensor(e1[:, :], e1[:, :], bb[:, 0:S], ALU.mult).then_inc(wp, 1)

                def squares(u, q):
                    for j in range(4):
                        f = 8 * u + 4 * q + j
                        pool.wait_ge(relu_done, f + 1)
                        if q == 0 and j == 0:
                            pool.wait_ge(kv_psum, 2 * u)
                        pool.tensor_tensor(kf[:, j, q, :], rl[:, j % 2, :], rl[:, j % 2, :], ALU.mult).then_inc(kf_done, 1)

                with pool.Fori(0, LAYERS) as l:
                    recurrence(l, 0)
                    u = 2 * l
                    recurrence_1 = 2 * l + 1
                    pool.wait_ge(wd, STEPS * recurrence_1 + 1)
                    pool.tensor_tensor(e2b[:, :], k_s[:, 1, :], pp[:, 1:S + 1], ALU.subtract).then_inc(wp, 1)
                    squares(u, 0)
                    pool.wait_ge(wa, 6 * recurrence_1 + 4)
                    pool.tensor_tensor(n2[:, :], e2[:, :], v_s[:, 1, :], ALU.mult).then_inc(wp, 1)
                    pool.wait_ge(wd, STEPS * recurrence_1 + 9)
                    pool.tensor_tensor(e1[:, :], e1[:, :], bb[:, 0:S], ALU.mult).then_inc(wp, 1)
                    squares(u, 1)
                    squares(u + 1, 0)
                    squares(u + 1, 1)

            @block.vector
            def _(dve):
                def normed(l, b, q, n, w, bias, hs):
                    ln_scale(dve, G, n, hp[:, b, 1 + q * CH:1 + (q + 1) * CH], vv[:, w:w + 1], q)
                    dve.wait_ge(G.ln.scaled, n + 1)
                    h = hp[:, b, 1 + q * CH:1 + (q + 1) * CH]
                    dve.tensor_scalar(h, h, vv[:, bias:bias + 1], None, ALU.add).then_inc(h_step, 1)
                    dve.wait_ge(h_step, hs + 1)
                    before = hp[:, b, q * CH:(q + 1) * CH]
                    dve.tensor_tensor(diff[:, q, :], h, before, ALU.subtract).then_inc(h_step, 1)
                    dve.wait_ge(h_step, hs + 2)
                    return before

                def time_mix(l, b):
                    for q in range(2):
                        ch = 4 * l + 2 * b + q
                        before = normed(l, b, q, n0 + 8 * l + 2 * b + q, LN1W, LN1B, 16 * l + 4 * b + 2 * q)
                        if b == 0:
                            dve.wait_ge(kv_psum, 4 * l)
                        else:
                            dve.wait_ge(r_psum, ch - 1)
                        for i, tm in enumerate((TMK, TMV, TMR)):
                            last = dve.scalar_tensor_tensor(mix[:, i, q, :], diff[:, q, :], vv[:, tm:tm + 1], before,
                                                            ALU.mult, ALU.add)
                        last.then_inc(mix1, 1)

                def recurrence(l, b):
                    u = 2 * l + b
                    at = STEPS * u
                    k, v, w, first = k_s[:, b, :], v_s[:, b, :], vv[:, 11:12], vv[:, FIRST:FIRST + 1]
                    prev, nxt = pp[:, 0:S], pp[:, 1:S + 1]
                    dve.wait_ge(k_kept, 4 * l + 2 * b + 2)
                    dve.tensor_tensor_scan(nxt, w.to_broadcast([P, S]), k, -1e38, ALU.add, ALU.max).then_inc(wd, 1)
                    dve.wait_ge(wd, at + 1)
                    dve.scalar_tensor_tensor(e1b[:, :], prev, w, nxt, ALU.add, ALU.subtract).then_inc(wd, 1)
                    dve.scalar_tensor_tensor(qq[:, :], k, first, prev, ALU.add, ALU.max).then_inc(wd, 1)
                    dve.wait_ge(wd, at + 3)
                    dve.tensor_tensor(e1[:, :], prev, qq[:, :], ALU.subtract).then_inc(wd, 1)
                    dve.scalar_tensor_tensor(e2[:, :], k, first, qq[:, :], ALU.add, ALU.subtract).then_inc(wd, 1)
                    dve.wait_ge(v_kept, 4 * l + 2 * b + 2)
                    dve.wait_ge(wa, 6 * u + 2)
                    dve.tensor_tensor(d1[:, :], e2b[:, :], v, ALU.mult).then_inc(wd, 1)
                    dve.wait_ge(wd, at + 6)
                    dve.tensor_tensor_scan(aa[:, 1:S + 1], e1b[:, :], d1[:, :], 0.0, ALU.mult, ALU.add).then_inc(wd, 1)
                    dve.tensor_tensor_scan(bb[:, 1:S + 1], e1b[:, :], e2b[:, :], 0.0, ALU.mult, ALU.add).then_inc(wd, 1)
                    dve.wait_ge(wd, at + 7)
                    dve.wait_ge(wa, 6 * u + 3)
                    dve.tensor_tensor(qq[:, :], e1[:, :], aa[:, 0:S], ALU.mult).then_inc(wd, 1)
                    dve.wait_ge(wp, 3 * u + 2)
                    dve.wait_ge(wd, at + 9)
                    dve.tensor_tensor(qq[:, :], qq[:, :], n2[:, :], ALU.add).then_inc(wd, 1)
                    dve.wait_ge(wp, 3 * u + 3)
                    dve.tensor_tensor(e1[:, :], e1[:, :], e2[:, :], ALU.add).then_inc(wd, 1)
                    dve.wait_ge(wd, at + 10)
                    dve.wait_ge(sr_done, u + 1)
                    dve.tensor_tensor(qq[:, :], qq[:, :], sr[:, b, :], ALU.mult).then_inc(wd, 1)
                    dve.wait_ge(wd, at + 12)
                    dve.wait_ge(wa, 6 * u + 6)
                    dve.tensor_tensor(rw[:, :], qq[:, :], e1[:, :], ALU.mult).then_inc(wd, 1)

                def residual(l, b):
                    u = 2 * l + b
                    for q in range(2):
                        dve.wait_ge(o_psum, 2 * u + q + 1)
                        dve.tensor_tensor(G.r[:, seq(b, q)], G.r[:, seq(b, q)], G.bank[4 + q][:, :], ALU.add)\
                            .then_inc(r_mid, 1)
                    for q in range(2):
                        before = normed(l, b, q, n0 + 8 * l + 4 + 2 * b + q, LN2W, LN2B, 16 * l + 8 + 4 * b + 2 * q)
                        if b == 0:
                            dve.wait_ge(r_psum, 4 * l + 4)
                        else:
                            dve.wait_ge(cr_psum, 2 * l + 1)
                            dve.wait_ge(f_psum, 8 * (2 * l + 1))
                        for i, tm in ((0, CMK), (2, CMR)):
                            last = dve.scalar_tensor_tensor(mix[:, i, q, :], diff[:, q, :], vv[:, tm:tm + 1], before,
                                                            ALU.mult, ALU.add)
                        last.then_inc(mix2, 1)

                def gated(l, b):
                    u = 2 * l + b
                    dve.wait_ge(sc_done, u + 1)
                    for q in range(2):
                        dve.wait_ge(kv_psum, 2 * u + q + 1)
                        dve.tensor_tensor(kvs[:, q, :], sc[:, q, :], G.bank[6 + q][:, :], ALU.mult).then_inc(kv_step, 1)
                        dve.wait_ge(kv_step, 2 * u + q + 1)
                        dve.tensor_tensor(G.r[:, seq(b, q)], G.r[:, seq(b, q)], kvs[:, q, :], ALU.add).then_inc(r_new, 1)

                dve.memset(hp[:, :, 0:1], 0.0).then_inc(start, 1)
                dve.memset(pp[:, 0:1], -1e38).then_inc(start, 1)
                dve.memset(aa[:, 0:1], 0.0).then_inc(start, 1)
                dve.memset(bb[:, 0:1], 0.0).then_inc(start, 1)
                dve.wait_ge(start, 4)
                with dve.Fori(0, LAYERS) as l:
                    dve.tensor_copy(vv[:, 0:11].unsqueeze(2),
                                    G.vec[:, 0:44].rearrange("p (v l) -> p v l", l=4)[:, :, bass.ds(l, 1)])\
                        .then_inc(vec_done, 1)
                    dve.tensor_copy(vv[:, 11:12], G.decay[:, bass.ds(l, 1)]).then_inc(vec_done, 1)
                    for i in range(2, 4):
                        dve.wait_ge(w_turned, 4 * l + i + 1)
                        dve.tensor_copy(wt[:, 4 * i:4 * i + (4 if i == 2 else 1), :].rearrange("p j m -> p (j m)"),
                                        G.bank[4 + i][:, 0:(4 if i == 2 else 1) * P]).then_inc(w_kept, 1)
                    dve.wait_ge(vec_done, 2 * l + 2)
                    time_mix(l, 0)
                    time_mix(l, 1)
                    recurrence(l, 0)
                    residual(l, 0)
                    recurrence(l, 1)
                    gated(l, 0)
                    residual(l, 1)
                    gated(l, 1)


def stage_last(nc, G, A, out):
    mem = G.mem
    E, TOP = 8, 2
    PAIRS = E // 2
    with ExitStack() as ctx:
        m = Memory(nc, ctx)
        w1, w3 = m.sb("w1", [P, E, 64]), m.sb("w3", [P, E, 64])
        w2 = m.sb("w2", [P, PAIRS, P])
        comb6 = m.sb("comb6", [6, PAIRS, T], BF16)
        sel6 = m.sb("sel6b", [6, P], BF16)
        logit = m.sb("logit", [P, NT, E])
        wide, wide_out = m.sb("wide2", [P, NT, 14]), m.sb("wide2_out", [P, NT, 14])
        best, pick = m.sb("best2", [P, NT, 8]), m.sb("pick2", [P, NT, 8])
        total = m.sb("total2", [P, NT, 1])
        chosen = m.sb("chosen2", [P, NT, E])
        part = m.sb("comb_part2", [E, 3, T], BF16)
        rest = m.sb("comb_rest2", [E, 2, T])
        cs, gs, us, sg, hid = (m.sb(n, [P, 2, CH]) for n in ("l_cs", "l_gs", "l_us", "l_sg", "l_hid"))
        o_tok = m.sb("o_tok", [P, NT, P])
        w_in, sel_done = mem.sem("l_w_in"), mem.sem("l_sel")
        x_new, h_done = mem.sem("l_x_new"), mem.sem("l_h_done")
        logit_psum, step, shifted, exp_done = mem.sem("l_logit"), mem.sem("l_step"), mem.sem("l_shifted"), mem.sem("l_exp")
        comb_done, comb_psum, split_done = mem.sem("l_comb"), mem.sem("l_comb_psum"), mem.sem("l_split")
        comb_out, comb_in = mem.sem("l_comb_out"), mem.sem("l_comb_in")
        c_psum, g_psum, u_psum, y_psum = mem.sem("l_c"), mem.sem("l_g"), mem.sem("l_u"), mem.sem("l_y")
        cs_done, gs_done, us_done, silu_done, hid_done = (mem.sem(n) for n in ("l_cs_d", "l_gs_d", "l_us_d", "l_silu_d", "l_hid_d"))
        x_fin, o_psum, o_kept, o_out = mem.sem("l_x_fin"), mem.sem("l_o"), mem.sem("l_o_kept"), mem.sem("l_o_out")
        ga, cb, sb_, gb = (G.mod[:, 1, j, :] for j in (2, 4, 3, 5))
        n0 = G.ln_count
        G.ln_count += NC
        NN = PAIRS * NC
        out_d = out.rearrange("b (t p) c -> p (b t) c", p=P)
        with nc.Block() as block:
            @block.sync
            def _(sp):
                for dst, name in ((w1, "w1"), (w3, "w3")):
                    sp.dma_start(dst[:, :, :], A["L1_ffn_" + name].rearrange("e d h -> d e h")).then_inc(w_in, 16)
                sp.dma_start(w2[:, :, :], A["L1_ffn_w2"].rearrange("(p e) h d -> (e h) p d", e=2)).then_inc(w_in, 16)
                sp.wait_ge(split_done, 5)
                sp.dma_start(G.comb1_d[:, :, :], part[:, :, :]).then_inc(comb_out, 16)
                sp.wait_ge(comb_out, 16)
                sp.dma_start(comb6[:, :, :], G.comb1_d.rearrange("(p e) a n -> (e a) p n", e=2)).then_inc(comb_in, 16)
                for c in range(NC):
                    sp.wait_ge(o_kept, c + 1)
                    sp.dma_start(out_d[:, 4 * c:4 * c + 4, :], o_tok[:, 4 * c:4 * c + 4, :]).then_inc(o_out, 16)
                sp.wait_ge(o_out, 16 * NC)

            @block.gpsimd
            def _(pool):
                pool.memset(sel6[:, :], 1.0).then_inc(sel_done, 1)
                pool.wait_ge(sel_done, 1)
                pool.affine_select(out=sel6[:, 0:64], in_=sel6[:, 0:64], compare_op=ALU.is_ge, fill=0.0, base=2,
                                   pattern=[[0, 64]], channel_multiplier=-1).then_inc(sel_done, 1)
                pool.affine_select(out=sel6[:, 64:P], in_=sel6[:, 64:P], compare_op=ALU.is_ge, fill=0.0, base=-3,
                                   pattern=[[0, 64]], channel_multiplier=1).then_inc(sel_done, 1)

            @block.tensor
            def _(pe):
                def logits(c):
                    pe.wait_ge(h_done, c + 1)
                    for t in range(4 * c, 4 * c + 4):
                        mm = pe.matmul(G.bank[4][:, chunk(t, E)], G.h[:, chunk(t, P)], G.gate1[:, :], start=True, stop=True)
                    mm.then_inc(logit_psum, 1)

                def down(n):
                    c = n % NC
                    pe.wait_ge(hid_done, n + 1)
                    pe.matmul(G.bank[c][:, :], w2[:, n // NC, :], hid[:, n % 2, :], start=(n < NC), stop=(n >= NN - NC),
                              skip_group_check=True).then_inc(y_psum, 1)

                for c in range(NC):
                    pe.wait_ge(x_new, c + 1)
                    ln_centre(pe, G, n0 + c, G.x[:, chunk(c)])
                    ln_variance(pe, G, n0 + c)
                    if c >= 1:
                        logits(c - 1)
                logits(NC - 1)
                pe.wait_ge(comb_done, 1)
                for c in range(NC):
                    for t in range(4):
                        mm = pe.transpose(G.bank[c][0:E, chunk(t, P)], chosen[:, 4 * c + t, :], G.ident[:, :])
                mm.then_inc(comb_psum, 1)
                pe.wait_ge(w_in, 48)
                pe.wait_ge(sel_done, 3)
                pe.wait_ge(comb_in, 16)
                for n in range(NN):
                    p, c = n // NC, n % NC
                    if n >= 1:
                        pe.wait_ge(cs_done, n)
                    pe.matmul(G.bank[6][:, :], sel6[:, :], comb6[:, p, chunk(c)], start=True, stop=True).then_inc(c_psum, 1)
                    if n >= 1:
                        pe.wait_ge(gs_done, n)
                    pe.matmul(G.bank[4][:, :], w1[:, 2 * p:2 * p + 2, :].rearrange("p e h -> p (e h)"), G.h[:, chunk(c)],
                              start=True, stop=True).then_inc(g_psum, 1)
                    if n >= 1:
                        pe.wait_ge(us_done, n)
                    pe.matmul(G.bank[5][:, :], w3[:, 2 * p:2 * p + 2, :].rearrange("p e h -> p (e h)"), G.h[:, chunk(c)],
                              start=True, stop=True).then_inc(u_psum, 1)
                    if n >= 1:
                        down(n - 1)
                down(NN - 1)
                for c in range(NC):
                    pe.wait_ge(x_fin, c + 1)
                    for t in range(4):
                        mm = pe.transpose(G.bank[4 + c][:, chunk(t, P)], G.x[:, chunk(4 * c + t, P)], G.ident[:, :])
                    mm.then_inc(o_psum, 1)

            @block.scalar
            def _(act):
                for c in range(NC):
                    ln_square(act, G, n0 + c)
                    ln_rstd(act, G, n0 + c)
                act.wait_ge(shifted, 1)
                act.activation(logit[:, :, :], logit[:, :, :], ACT.Exp).then_inc(exp_done, 1)

                def silu(n):
                    act.wait_ge(gs_done, n + 1)
                    act.activation(sg[:, n % 2, :], gs[:, n % 2, :], ACT.Silu).then_inc(silu_done, 1)

                for n in range(NN):
                    act.wait_ge(c_psum, n + 1)
                    if n >= 2:
                        act.wait_ge(us_done, n - 1)
                    act.copy(cs[:, n % 2, :], G.bank[6][:, :]).then_inc(cs_done, 1)
                    if n >= 1:
                        silu(n - 1)
                silu(NN - 1)

            @block.vector
            def _(dve):
                count = [0]

                def link(ins):
                    count[0] += 1
                    ins.then_inc(step, 1)
                    dve.wait_ge(step, count[0])

                for c in range(NC):
                    dve.scalar_tensor_tensor(G.x[:, chunk(c)], G.r[:, chunk(c)], ga[:, c // 2:c // 2 + 1],
                                             G.x[:, chunk(c)], ALU.mult, ALU.add).then_inc(x_new, 1)
                link(dve.memset(wide[:, :, E:14], BIG))
                link(dve.memset(pick[:, :, TOP:8], BIG))
                for c in range(NC):
                    ln_scale(dve, G, n0 + c, G.h[:, chunk(c)], cb[:, c // 2:c // 2 + 1])
                    dve.wait_ge(G.ln.scaled, n0 + c + 1)
                    dve.tensor_scalar(G.h[:, chunk(c)], G.h[:, chunk(c)], sb_[:, c // 2:c // 2 + 1], None, ALU.add)\
                        .then_inc(h_done, 1)
                dve.wait_ge(logit_psum, NC)
                link(dve.tensor_copy(logit[:, :, :], G.bank[4][:, 0:NT * E].rearrange("p (t e) -> p t e", t=NT)))
                link(dve.tensor_reduce(total[:, :, 0], logit[:, :, :], AX_X, ALU.max))
                dve.tensor_tensor(logit[:, :, :], logit[:, :, :], total[:, :, :].to_broadcast([P, NT, E]), ALU.subtract)\
                    .then_inc(shifted, 1)
                dve.wait_ge(exp_done, 1)
                link(dve.tensor_reduce(total[:, :, 0], logit[:, :, :], AX_X, ALU.add))
                link(dve.reciprocal(total[:, :, :], total[:, :, :]))
                link(dve.tensor_tensor(wide[:, :, 0:E], logit[:, :, :], total[:, :, :].to_broadcast([P, NT, E]), ALU.mult))
                for t in range(NT):
                    last = dve.max(best[:, t, :], wide[:, t, 0:E])
                link(last)
                link(dve.tensor_copy(pick[:, :, 0:TOP], best[:, :, 0:TOP]))
                for t in range(NT):
                    last = dve.match_replace(wide_out[:, t, :], pick[:, t, :], wide[:, t, :], -BIG)
                link(last)
                link(dve.tensor_tensor(chosen[:, :, :], wide_out[:, :, 0:E], wide[:, :, 0:E], ALU.not_equal))
                dve.tensor_tensor(chosen[:, :, :], chosen[:, :, :], wide[:, :, 0:E], ALU.mult).then_inc(comb_done, 1)
                dve.wait_ge(comb_psum, 1)
                turned = G.psum3[0:E, 0:NC, :]
                r0, r1 = (rest[:, k, :].rearrange("e (c n) -> e c n", c=NC) for k in range(2))
                p0, p1, p2 = (part[:, k, :].rearrange("e (c n) -> e c n", c=NC) for k in range(3))
                dve.tensor_copy(p0, turned).then_inc(split_done, 1)
                dve.wait_ge(split_done, 1)
                dve.tensor_tensor(r0, turned, p0, ALU.subtract).then_inc(split_done, 1)
                dve.wait_ge(split_done, 2)
                dve.tensor_copy(p1, r0).then_inc(split_done, 1)
                dve.wait_ge(split_done, 3)
                dve.tensor_tensor(r1, r0, p1, ALU.subtract).then_inc(split_done, 1)
                dve.wait_ge(split_done, 4)
                dve.tensor_copy(p2, r1).then_inc(split_done, 1)

                def join(n):
                    dve.wait_ge(silu_done, n + 1)
                    dve.wait_ge(us_done, n + 1)
                    if n >= 2:
                        dve.wait_ge(y_psum, n - 1)
                    dve.tensor_tensor(hid[:, n % 2, :], sg[:, n % 2, :], us[:, n % 2, :], ALU.mult).then_inc(hid_done, 1)

                for n in range(NN):
                    dve.wait_ge(cs_done, n + 1)
                    dve.wait_ge(g_psum, n + 1)
                    dve.tensor_tensor(gs[:, n % 2, :], G.bank[4][:, :], cs[:, n % 2, :], ALU.mult).then_inc(gs_done, 1)
                    dve.wait_ge(u_psum, n + 1)
                    dve.tensor_tensor(us[:, n % 2, :], G.bank[5][:, :], cs[:, n % 2, :], ALU.mult).then_inc(us_done, 1)
                    if n >= 1:
                        join(n - 1)
                join(NN - 1)
                for c in range(NC):
                    dve.wait_ge(y_psum, NN - NC + c + 1)
                    dve.scalar_tensor_tensor(G.x[:, chunk(c)], G.bank[c][:, :], gb[:, c // 2:c // 2 + 1],
                                             G.x[:, chunk(c)], ALU.mult, ALU.add).then_inc(x_fin, 1)
                for c in range(NC):
                    dve.wait_ge(o_psum, c + 1)
                    dve.tensor_copy(o_tok[:, 4 * c:4 * c + 4, :],
                                    G.bank[4 + c][:, :].rearrange("p (t m) -> p t m", t=4)).then_inc(o_kept, 1)


def build(nc, A, out):
    G = Global()
    with ExitStack() as ctx:
        mem = G.mem = Memory(nc, ctx)
        psum = ctx.enter_context(nc.psum_tensor("psum", [P, 8, CH], F32))
        G.bank = [psum[:, i, :] for i in range(8)]
        G.pair = [psum[:, 0:2, :], psum[:, 2:4, :]]
        G.ident = mem.sb("ident", [P, P])
        G.identb = mem.sb("identb", [P, P], BF16)
        G.mask_qk = mem.sb("mask_qk", [P, P], BF16)
        G.mask_kq = mem.sb("mask_kq", [P, P], BF16)
        G.den_row = mem.sb("den_row", [P, P])
        G.mean = mem.sb("mean", [P, P])
        G.centre = mem.sb("centre", [P, P])
        G.eps = mem.sb("eps", [P, 1])
        G.x = mem.sb("x", [P, T])
        G.vec = mem.sb("vec", [P, 46])
        G.decay = mem.sb("decay", [P, LAYERS])
        G.mod = mem.sb("mod", [P, 2, 6, B])
        G.gate0 = mem.sb("gate0", [P, 64])
        G.gate1 = mem.sb("gate1", [P, 8])
        G.gate_bias = mem.sb("gate_bias", [P, 64])
        G.wqkv = mem.sb("wqkv", [P, 3, P])
        G.wo_t = mem.sb("wo_t", [P, 4, P])
        G.sq = mem.sb("ln_sq", [P, 2, CH])
        G.rs = mem.sb("ln_rs", [P, 2, CH])
        G.ln = LnSems(mem)
        G.h = mem.sb("h", [P, T])
        G.x_l0, G.r_done = mem.sem("x_l0"), mem.sem("r_done")
        G.ln_count = NC
        G.comb_d = nc.dram_tensor("comb_parts", [64, 3, T], BF16).ap()
        G.psum3 = psum
        G.comb1_d = nc.dram_tensor("comb1_parts", [8, 3, T], BF16).ap()
        G.rows_d = [nc.dram_tensor("rows_q", [3 * DK, H, T], BF16).ap(),
                    nc.dram_tensor("rows_k", [ROWS, H, T], BF16).ap()]
        with ExitStack() as attn:
            m = Memory(nc, attn)
            G.qa = m.sb("qa", [ROWS + 3, RING, HG, S], BF16)
            G.ka = m.sb("ka", [96, RING, HG, S], BF16)
            G.part = m.sb("part", [P, 2, 3, 2, CH], BF16)
            G.parts_out = [[mem.sem(f"parts_out_{n}{par}") for par in range(2)] for n in "qk"]
            G.va = m.sb("va", [P, NG, 8, HG, 32])
            G.v_pad = mem.sem("v_pad")
            G.ones_done = mem.sem("ones_done")
            G.qk_in = mem.sem("qk_in")
            stage_setup(nc, G, A)
            G.o = m.sb("o", [P, 4, T])
            stage_qkv(nc, G)
            stage_attention(nc, G)
            stage_router(nc, G)
        stage_experts(nc, G, A)
        G.r = mem.sb("r", [P, T])
        stage_rwkv_in(nc, G)
        stage_rwkv(nc, G, A)
        stage_last(nc, G, A, out)


_INS = ['L0_attn_x', 'L0_attn_WQ', 'L0_attn_WK', 'L0_attn_WV', 'L0_attn_WO', 'L0_ffn_gate_w', 'L0_ffn_gate_bias',
        'L0_ffn_eg_w', 'L0_ffn_eu_w', 'L0_ffn_ed_w', 'L0_ffn_sg_w', 'L0_ffn_su_w', 'L0_ffn_sd_w', 'L0_c', 'L0_wmod',
        'L1_attn_ln0_w', 'L1_attn_ln0_b', 'L1_attn_ln1_w', 'L1_attn_ln1_b', 'L1_attn_ln2_w', 'L1_attn_ln2_b',
        'L1_attn_time_decay', 'L1_attn_time_first', 'L1_attn_tmk', 'L1_attn_tmv', 'L1_attn_tmr', 'L1_attn_Wk',
        'L1_attn_Wv', 'L1_attn_Wr', 'L1_attn_Wo', 'L1_attn_cmk', 'L1_attn_cmr', 'L1_attn_Wck', 'L1_attn_Wcv',
        'L1_attn_Wcr', 'L1_ffn_gate_w', 'L1_ffn_w1', 'L1_ffn_w2', 'L1_ffn_w3', 'L1_c', 'L1_wmod']


def kernel(**inputs):
    import numpy as _np
    import concourse.bacc as _bacc
    from concourse.bass_utils import run_bass_kernel_spmd as _run

    nc = _bacc.Bacc("TRN2", target_bir_lowering=False, num_devices=1)
    arrays, aps = {}, {}
    for name in _INS:
        arrays["in_" + name] = _np.ascontiguousarray(inputs[name])
        aps[name] = nc.dram_tensor("in_" + name, arrays["in_" + name].shape, F32, kind="ExternalInput").ap()
    out = nc.dram_tensor("out_x", (B, S, P), F32, kind="ExternalOutput").ap()
    build(nc, aps, out)
    return _run(nc, [arrays], core_ids=[0]).results[0]["out_x"]
```

```python
import math
from contextlib import ExitStack

import concourse.bass as bass
from concourse import mybir

ALU = mybir.AluOpType
ACT = mybir.ActivationFunctionType
F32 = mybir.dt.float32
BF16 = mybir.dt.bfloat16
AX_X = mybir.AxisListType.X

P = 128
B = 2
S = 1024
T = B * S
NT = T // P
CH = 512
NC = T // CH
H = 16
DK = P // H
HG = 4
NG = B * H // HG
NEG = -1e30
ROWS = 9 * DK
RING = 4
EXP_LN_SET = 6

VECS = ["ln1_w", "ln1_b", "ln2_w", "ln2_b", "time_decay", "time_first", "tmk", "tmv", "tmr", "cmk", "cmr"]
LN1W, LN1B, LN2W, LN2B, DECAY, FIRST, TMK, TMV, TMR, CMK, CMR = range(11)
LAYERS = 4


class Memory:

    def __init__(self, nc, ctx):
        self.nc, self.ctx = nc, ctx

    def sb(self, name, shape, dt=F32):
        return self.ctx.enter_context(self.nc.sbuf_tensor(name, shape, dt))

    def sem(self, name):
        return self.nc.alloc_semaphore(name)


class LnSems:

    def __init__(self, mem):
        self.centred = mem.sem("ln_centred")
        self.squared = mem.sem("ln_squared")
        self.variance = mem.sem("ln_variance")
        self.logged = mem.sem("ln_logged")
        self.rstd = mem.sem("ln_rstd")
        self.scaled = mem.sem("ln_scaled")


def chunk(c, n=CH):
    return slice(c * n, (c + 1) * n)


def load_act_set(nc, act, set_id):
    act.add_instruction(mybir.InstLoadActFuncSet(name=nc.get_next_instruction_name(), act_func_set_id=set_id,
                                                 engine=mybir.EngineType.Activation, ins=[], outs=[]))


def ln_centre(pe, G, n, src, par=None):
    par = n % 2 if par is None else par
    if not isinstance(n, int) or n >= 2:
        pe.wait_ge(G.ln.scaled, n - 1)
    pe.matmul(G.bank[par][:, :], G.centre[:, :], src, start=True, stop=True).then_inc(G.ln.centred, 1)


def ln_variance(pe, G, n, par=None):
    par = n % 2 if par is None else par
    pe.wait_ge(G.ln.squared, n + 1)
    if not isinstance(n, int) or n >= 2:
        pe.wait_ge(G.ln.rstd, n - 1)
    pe.matmul(G.bank[2 + par][:, :], G.mean[:, :], G.sq[:, par, :], start=True, stop=True)\
        .then_inc(G.ln.variance, 1)


def ln_square(act, G, n, par=None):
    par = n % 2 if par is None else par
    act.wait_ge(G.ln.centred, n + 1)
    if not isinstance(n, int) or n >= 2:
        act.wait_ge(G.ln.variance, n - 1)
    act.activation(G.sq[:, par, :], G.bank[par][:, :], ACT.Square).then_inc(G.ln.squared, 1)


def ln_rstd(act, G, n, par=None):
    par = n % 2 if par is None else par
    act.wait_ge(G.ln.variance, n + 1)
    if not isinstance(n, int) or n >= 2:
        act.wait_ge(G.ln.scaled, n - 1)
    act.activation(G.rs[:, par, :], G.bank[2 + par][:, :], ACT.Ln, bias=G.eps[:, 0:1])\
        .then_inc(G.ln.logged, 1)
    act.wait_ge(G.ln.logged, n + 1)
    act.activation(G.rs[:, par, :], G.rs[:, par, :], ACT.Exp, scale=-0.5).then_inc(G.ln.rstd, 1)


def ln_scale(dve, G, n, dst, w, par=None):
    par = n % 2 if par is None else par
    dve.wait_ge(G.ln.rstd, n + 1)
    dve.scalar_tensor_tensor(dst, G.bank[par][:, :], w, G.rs[:, par, :], ALU.mult, ALU.mult)\
        .then_inc(G.ln.scaled, 1)


class Global:
    pass


def stage_setup(nc, G, A):
    mem = G.mem
    with ExitStack() as ctx:
        m = Memory(nc, ctx)
        x_tok = m.sb("x_tok", [P, NT, P])
        w_nat = m.sb("w_nat", [P, 4, P])
        wo_sp = m.sb("wo_sp", [P, H, 32])
        gate_nat = m.sb("gate_nat", [64, P])
        vec_rows = m.sb("vec_rows", [46, P])
        c_t = m.sb("c_t", [P, 2, B])
        c_silu = m.sb("c_silu", [P, 2, B])
        wmod = m.sb("wmod", [P, 2, 6, P])
        sign = m.sb("sign", [P, 2, 2, B])
        mag = m.sb("mag", [P, 2, 2, B])
        x_in = [mem.sem(f"x_in{c}") for c in range(NC)]
        w_in, vec_in, c_in = mem.sem("w_in"), mem.sem("vec_in"), mem.sem("c_in")
        const_zero, const_done = mem.sem("const_zero"), mem.sem("const_done")
        centre_done, sp_zero, sp_done = mem.sem("centre_done"), mem.sem("sp_zero"), mem.sem("sp_done")
        silu_done, va_zero = mem.sem("silu_done"), mem.sem("va_zero")
        x_turned, x_kept = mem.sem("x_turned"), mem.sem("x_kept")
        w_turned, w_kept = mem.sem("w_turned"), mem.sem("w_kept")
        mod_psum, mod_step, mod_done = mem.sem("mod_psum"), mem.sem("mod_step"), mem.sem("mod_done")
        x_d = A["L0_attn_x"].rearrange("b (t p) c -> p (b t) c", p=P)
        with nc.Block() as block:
            @block.sync
            def _(sp):
                for c in range(NC):
                    sp.dma_start(x_tok[:, 4 * c:4 * c + 4, :], x_d[:, 4 * c:4 * c + 4, :]).then_inc(x_in[c], 16)
                for i, name in enumerate(["WQ", "WK", "WV", "WO"]):
                    sp.dma_start(w_nat[:, i, :], A["L0_attn_" + name]).then_inc(w_in, 16)
                sp.dma_start(gate_nat[:, :], A["L0_ffn_gate_w"]).then_inc(w_in, 16)
                sp.dma_start(G.gate1[:, :], A["L1_ffn_gate_w"]).then_inc(vec_in, 16)
                sp.dma_start(G.gate_bias[:, :], A["L0_ffn_gate_bias"].rearrange("(o e) -> o e", o=1)
                             .to_broadcast([P, 64])).then_inc(vec_in, 16)

            @block.scalar
            def _(act):
                for i in range(2):
                    with nc.allow_non_contiguous_dma(reason="two columns of 128"):
                        act.dma_start(c_t[:, i, :], A[f"L{i}_c"].rearrange("b p -> p b")).then_inc(c_in, 16)
                    act.dma_start(wmod[:, i, :, :], A[f"L{i}_wmod"].rearrange("k (j m) -> k j m", j=6))\
                        .then_inc(c_in, 16)
                for v, name in enumerate(VECS):
                    act.dma_start(vec_rows[4 * v:4 * v + 4, :], A["L1_attn_" + name]).then_inc(vec_in, 16)
                for v, name in enumerate(["ln0_w", "ln0_b"]):
                    act.dma_start(vec_rows[44 + v:45 + v, :], A["L1_attn_" + name].rearrange("(o c) -> o c", o=1))\
                        .then_inc(vec_in, 16)
                act.wait_ge(c_in, 64)
                act.activation(c_silu[:, :, :], c_t[:, :, :], ACT.Silu).then_inc(silu_done, 1)
                load_act_set(nc, act, EXP_LN_SET)
                for c in range(1, NC, 2):
                    act.wait_ge(x_turned, c + 1)
                    act.copy(G.x[:, chunk(c)], G.bank[c][:, :]).then_inc(x_kept, 1)
                act.wait_ge(w_turned, 3)
                act.activation(G.decay[:, :], G.bank[6][:, 4 * DECAY:4 * DECAY + 4], ACT.Exp)\
                    .then_inc(w_kept, 1)

            @block.gpsimd
            def _(pool):
                pool.memset(G.ident[:, :], 0.0).then_inc(const_zero, 1)
                pool.memset(G.mask_qk[:, :], 0.0).then_inc(const_zero, 1)
                pool.memset(G.mask_kq[:, :], 0.0).then_inc(const_zero, 1)
                pool.memset(G.den_row[:, :], 0.0).then_inc(const_zero, 1)
                pool.wait_ge(const_zero, 4)
                pool.affine_select(out=G.ident[:, :], in_=G.ident[:, :], compare_op=ALU.not_equal, fill=1.0, base=0,
                                   pattern=[[-1, P]], channel_multiplier=1).then_inc(const_done, 1)
                pool.affine_select(out=G.mask_qk[:, :], in_=G.mask_qk[:, :], compare_op=ALU.is_ge, fill=NEG, base=0,
                                   pattern=[[-1, P]], channel_multiplier=1).then_inc(const_done, 1)
                pool.affine_select(out=G.mask_kq[:, :], in_=G.mask_kq[:, :], compare_op=ALU.is_ge, fill=NEG, base=0,
                                   pattern=[[1, P]], channel_multiplier=-1).then_inc(const_done, 1)
                pool.affine_select(out=G.den_row[:, :].rearrange("p (g r) -> p g r", g=4),
                                   in_=G.den_row[:, :].rearrange("p (g r) -> p g r", g=4),
                                   compare_op=ALU.not_equal, fill=1.0, base=-DK,
                                   pattern=[[-32, 4], [0, 32]], channel_multiplier=1).then_inc(const_done, 1)
                pool.wait_ge(const_done, 4)
                pool.memset(G.va[:, :, :, :, :], 0.0).then_inc(va_zero, 1)
                pool.wait_ge(va_zero, 1)
                pool.memset(G.va[:, :, :, :, DK:DK + 1], 1.0).then_inc(G.v_pad, 1)
                pool.wait_ge(G.v_pad, 1)
                pool.memset(G.ka[64:96, :, :, :], 1.0).then_inc(G.ones_done, 1)

            @block.vector
            def _(dve):
                dve.memset(G.mean[:, :], 1.0 / P).then_inc(centre_done, 1)
                dve.memset(G.eps[:, :], 1e-5).then_inc(centre_done, 1)
                dve.memset(wo_sp[:, :, :], 0.0).then_inc(sp_zero, 1)
                dve.wait_ge(const_done, 4)
                dve.tensor_scalar(G.centre[:, :], G.ident[:, :], -1.0 / P, None, ALU.add).then_inc(centre_done, 1)
                dve.tensor_copy(G.identb[:, :], G.ident[:, :]).then_inc(centre_done, 1)
                dve.wait_ge(w_in, 80)
                dve.wait_ge(sp_zero, 1)
                dve.tensor_copy(wo_sp[:, :, 0:DK], w_nat[:, 3, :].rearrange("p (h d) -> p h d", h=H))\
                    .then_inc(sp_done, 1)
                for c in range(0, NC, 2):
                    dve.wait_ge(x_turned, c + 1)
                    dve.tensor_copy(G.x[:, chunk(c)], G.bank[c][:, :]).then_inc(x_kept, 1)
                dve.wait_ge(w_turned, 1)
                for i in range(2):
                    dve.tensor_copy(G.wqkv[:, i, :].rearrange("p (d h) -> p h d", d=DK),
                                    G.bank[4][:, chunk(i, P)].rearrange("p (h d) -> p h d", h=H))
                dve.tensor_copy(G.wqkv[:, 2, :], G.bank[4][:, chunk(2, P)]).then_inc(w_kept, 1)
                dve.wait_ge(w_turned, 2)
                dve.tensor_copy(G.wo_t[:, :, :], G.bank[5][:, :].rearrange("p (i m) -> p i m", i=4))\
                    .then_inc(w_kept, 1)
                dve.wait_ge(w_turned, 3)
                dve.wait_ge(w_kept, 3)
                dve.tensor_copy(G.vec[:, :], G.bank[6][:, 0:46]).then_inc(w_kept, 1)
                dve.tensor_copy(G.gate0[:, :], G.bank[6][:, 64:128]).then_inc(w_kept, 1)
                dve.tensor_scalar(G.decay[:, :], G.decay[:, :], -1.0, None, ALU.mult).then_inc(w_kept, 1)
                dve.wait_ge(mod_psum, 1)
                dve.tensor_copy(G.mod[:, :, :, :],
                                G.bank[7][:, 0:24].rearrange("p (l j b) -> p l j b", l=2, j=6)).then_inc(mod_step, 1)
                dve.wait_ge(mod_step, 1)
                gates = G.mod[:, :, 2:6:3, :]
                ones = G.mod[:, :, 1:5:3, :]
                dve.tensor_scalar(sign[:, :, :, :], gates, 0.0, 2.0, ALU.is_ge, ALU.mult).then_inc(mod_step, 1)
                for l in range(2):
                    dve.scalar_tensor_tensor(mag[:, l], gates[:, l], -1.0, gates[:, l], ALU.mult, ALU.max)\
                        .then_inc(mod_step, 1)
                dve.tensor_scalar(ones, ones, 1.0, None, ALU.add).then_inc(mod_step, 1)
                dve.wait_ge(mod_step, 5)
                dve.tensor_scalar(mag[:, :, :, :], mag[:, :, :, :], 0.25, None, ALU.max).then_inc(mod_step, 1)
                dve.wait_ge(mod_step, 6)
                for l in range(2):
                    dve.scalar_tensor_tensor(gates[:, l], sign[:, l], -1.0, mag[:, l], ALU.add, ALU.mult)\
                        .then_inc(mod_done, 1)

            @block.tensor
            def _(pe):
                pe.wait_ge(const_done, 4)
                for c in range(NC):
                    pe.wait_ge(x_in[c], 16)
                    for t in range(4):
                        mm = pe.transpose(G.bank[c][:, chunk(t, P)], x_tok[:, 4 * c + t, :], G.ident[:, :])
                    mm.then_inc(x_turned, 1)
                pe.wait_ge(w_in, 80)
                for i in range(3):
                    mm = pe.transpose(G.bank[4][:, chunk(i, P)], w_nat[:, i, :], G.ident[:, :])
                mm.then_inc(w_turned, 1)
                pe.wait_ge(sp_done, 1)
                for g in range(4):
                    mm = pe.transpose(G.bank[5][:, chunk(g, P)],
                                      wo_sp[:, 4 * g:4 * g + 4, :].rearrange("p h r -> p (h r)"), G.ident[:, :])
                mm.then_inc(w_turned, 1)
                pe.wait_ge(vec_in, 16 * (2 + len(VECS) + 2))
                pe.transpose(G.bank[6][:, 0:46], vec_rows[:, :], G.ident[0:46, 0:46])
                pe.transpose(G.bank[6][:, 64:128], gate_nat[:, :], G.ident[0:64, 0:64]).then_inc(w_turned, 1)
                pe.wait_ge(silu_done, 1)
                for l in range(2):
                    for j in range(6):
                        k = (l * 6 + j) * B
                        mm = pe.matmul(G.bank[7][:, k:k + B], wmod[:, l, j, :], c_silu[:, l, :],
                                       start=True, stop=True)
                mm.then_inc(mod_psum, 1)


def stage_qkv(nc, G):
    mem = G.mem
    with ExitStack() as ctx:
        m = Memory(nc, ctx)
        h = m.sb("h_attn", [P, T])
        part = G.part
        rest = m.sb("rest", [P, 2, 2, CH])
        h_done = mem.sem("h_done")
        qk_psum, v_psum, v_kept = mem.sem("qk_psum"), mem.sem("v_psum"), mem.sem("v_kept")
        hi_done, r1_done, mid_done, lo_done = mem.sem("hi_done"), mem.sem("r1_done"), mem.sem("mid_done"), mem.sem("lo_done")
        parts_out = G.parts_out
        v_pad = G.v_pad
        sa, ca = G.mod[:, 0, 0, :], G.mod[:, 0, 1, :]
        with nc.Block() as block:
            @block.tensor
            def _(pe):
                def project(c):
                    pe.wait_ge(h_done, c + 1)
                    for i in range(2):
                        if c >= 1:
                            pe.wait_ge(lo_done, 2 * (c - 1) + i + 1)
                        pe.matmul(G.bank[4 + i][:, :], G.wqkv[:, i, :], h[:, chunk(c)], start=True, stop=True)\
                            .then_inc(qk_psum, 1)
                    if c >= 1:
                        pe.wait_ge(v_kept, c)
                    for t in range(4):
                        mm = pe.matmul(G.bank[6][:, chunk(t, P)], h[:, chunk(4 * c + t, P)], G.wqkv[:, 2, :],
                                       start=True, stop=True)
                    mm.then_inc(v_psum, 1)

                ln_centre(pe, G, 0, G.x[:, chunk(0)])
                for c in range(NC):
                    if c + 1 < NC:
                        ln_centre(pe, G, c + 1, G.x[:, chunk(c + 1)])
                    ln_variance(pe, G, c)
                    if c >= 1:
                        project(c - 1)
                project(NC - 1)

            @block.scalar
            def _(act):
                def keep(c):
                    for i in range(2):
                        act.wait_ge(qk_psum, 2 * c + i + 1)
                        if c >= 2:
                            act.wait_ge(parts_out[i][c % 2], (16, 48)[i])
                        act.copy(part[:, i, 0, c % 2, :], G.bank[4 + i][:, :]).then_inc(hi_done, 1)
                    act.wait_ge(v_psum, c + 1)
                    for g in range(4):
                        mm = act.copy(G.va[:, 4 * (c // 2) + g, 4 * (c % 2):4 * (c % 2) + 4, :, 0:DK],
                                      G.bank[6][:, :].rearrange("p (t g h d) -> p g t h d", t=4, g=4, h=4)[:, g])
                    mm.then_inc(v_kept, 1)

                ln_square(act, G, 0)
                for c in range(NC):
                    if c + 1 < NC:
                        ln_square(act, G, c + 1)
                    ln_rstd(act, G, c)
                    if c == 0:
                        act.wait_ge(v_pad, 1)
                    if c >= 1:
                        keep(c - 1)
                keep(NC - 1)

            @block.vector
            def _(dve):
                def split(c):
                    for i in range(2):
                        n = 2 * c + i + 1
                        dve.wait_ge(hi_done, n)
                        dve.tensor_tensor(rest[:, i, c % 2, :], G.bank[4 + i][:, :], part[:, i, 0, c % 2, :],
                                          ALU.subtract).then_inc(r1_done, 1)
                    for i in range(2):
                        n = 2 * c + i + 1
                        dve.wait_ge(r1_done, n)
                        dve.tensor_copy(part[:, i, 1, c % 2, :], rest[:, i, c % 2, :]).then_inc(mid_done, 1)
                    for i in range(2):
                        n = 2 * c + i + 1
                        dve.wait_ge(mid_done, n)
                        dve.tensor_tensor(part[:, i, 2, c % 2, :], rest[:, i, c % 2, :], part[:, i, 1, c % 2, :],
                                          ALU.subtract).then_inc(lo_done, 1)

                for c in range(NC):
                    b = c // 2
                    ln_scale(dve, G, c, h[:, chunk(c)], ca[:, b:b + 1])
                    dve.wait_ge(G.ln.scaled, c + 1)
                    dve.tensor_scalar(h[:, chunk(c)], h[:, chunk(c)], sa[:, b:b + 1], None, ALU.add)\
                        .then_inc(h_done, 1)
                    if c >= 1:
                        split(c - 1)
                split(NC - 1)

            @block.sync
            def _(sp):
                def store(c):
                    sp.wait_ge(lo_done, 2 * c + 1)
                    sp.dma_start(G.rows_d[0].rearrange("(a d) h t -> (d h) a t", a=3)[:, :, chunk(c)],
                                 part[:, 0, :, c % 2, :]).then_inc(parts_out[0][c % 2], 16)
                    sp.wait_ge(lo_done, 2 * c + 2)
                    for a in range(3):
                        sp.dma_start(G.rows_d[1].rearrange("(r a d) h t -> a (d h) r t", r=3, a=3)[a][:, :, chunk(c)],
                                     part[:, 1, :, c % 2, :]).then_inc(parts_out[1][c % 2], 16)

                store(0)
                store(1)
                for par in range(2):
                    sp.wait_ge(parts_out[0][par], 16)
                    sp.wait_ge(parts_out[1][par], 48)
                sp.wait_ge(G.ones_done, 1)
                load_group(sp, G, 0)
                store(2)
                store(3)


def load_group(sp, G, g):
    heads, tokens = bass.ds(HG * (g % 4), HG), bass.ds((g // 4) * S, S)
    for r in range(3):
        sp.dma_start(G.qa[3 * DK * r:3 * DK * (r + 1), g % RING, :, :], G.rows_d[0][:, heads, tokens])\
            .then_inc(G.qk_in, 16)
    sp.dma_start(G.ka[0:ROWS, g % RING, :, :], G.rows_d[1][:, heads, tokens]).then_inc(G.qk_in, 16)


def stage_attention(nc, G):
    mem = G.mem
    SCALE = 1.0 / math.sqrt(DK)
    PIECES = [(h, i, k0, min(CH, (i + 1) * P - k0), i if k0 == 0 else 4 + i)
              for h in range(HG) for i in range(8) for k0 in range(0, (i + 1) * P, CH)]
    NP = len(PIECES)
    UNITS = [(c, j, p) for c in range(2) for j in range(4 * c + 4) for p in range(2)]
    NU = len(UNITS)
    NQ = NU // 2
    SCHED, at = [], 0
    for u in range(NU):
        front = range(at, min(NP, at + (6 if u == 0 else 1)))
        back = range(front.stop, min(NP, front.stop + 1))
        SCHED.append((front, back))
        at = back.stop
    assert at == NP
    TURN = next(u for u in range(NU) if SCHED[u][0].stop == NP) + 1
    PV_C0 = 9
    DEN_C0, OUT_C0 = PV_C0 + 2, PV_C0 + 5
    PROJECT = 8
    TAIL_DEN = 2

    with ExitStack() as ctx:
        m = Memory(nc, ctx)
        qa, ka, qk_in = G.qa, G.ka, G.qk_in
        va_g = [m.sb(f"va_g{i}", [P, 8, HG, 32]) for i in range(2)]
        pt = m.sb("pt", [P, 4, 2, CH])
        part_max = m.sb("part_max", [P, HG, 12])
        top = m.sb("top", [P, HG, 8])
        neg = m.sb("neg", [P, 3, HG, 8], BF16)
        neg_rest = m.sb("neg_rest", [P, 2, HG, 8])
        neg_t = m.sb("neg_t", [3 * HG * 8, P], BF16)
        acc = m.sb("acc", [P, 2, CH])
        rden = m.sb("rden", [P, 2, CH])

        v_in = mem.sem("v_in")
        piece_psum, piece_max = mem.sem("piece_psum"), mem.sem("piece_max")
        max_step = mem.sem("max_step")
        neg_turned, neg_kept = mem.sem("neg_turned"), mem.sem("neg_kept")
        neg_in = mem.sem("neg_in")
        score_psum, prob_done, pv_done = mem.sem("score_psum"), mem.sem("prob_done"), mem.sem("pv_done")
        acc_kept, den_psum = mem.sem("acc_kept"), mem.sem("den_psum")
        den_log, den_inv, out_done = mem.sem("den_log"), mem.sem("den_inv"), mem.sem("out_done")
        score_bank = [G.pair[0], G.pair[1]]
        max_bank = [G.bank[4], G.bank[5]]
        acc_bank, misc = G.bank[6], G.bank[7]

        def groups(eng, body):
            body(0, 0, first=True)
            body(1, 1)
            with eng.Fori(1, NG // 2 - 1) as pair:
                for k in range(2):
                    body(2 * pair + k, k)
            body(NG - 2, 0)
            body(NG - 1, 1, last=True)

        with nc.Block() as block:
            @block.sync
            def _(sp):
                def neg_rows(g):
                    sp.wait_ge(neg_kept, g + 1)
                    for a in range(3):
                        sp.dma_start(qa[ROWS + a:ROWS + a + 1, g % RING, :, :].rearrange("o h (t c) -> o (h t) c", c=P),
                                     neg_t[32 * a:32 * a + 32, :]).then_inc(neg_in, 16)

                for g in (1, 2):
                    sp.wait_ge(qk_in, 64 * g)
                    load_group(sp, G, g)
                neg_rows(0)
                for par in range(2):
                    sp.wait_ge(G.parts_out[0][par], 32)
                    sp.wait_ge(G.parts_out[1][par], 96)
                neg_rows(1)
                sp.wait_ge(qk_in, 64 * 3)
                load_group(sp, G, 3)
                with sp.Fori(1, NG - 3) as g:
                    scored = NU * g
                    sp.compute_val(scored)
                    sp.wait_ge(qk_in, 64 * (g + 3))
                    sp.wait_ge(score_psum, scored)
                    load_group(sp, G, g + 3)
                    neg_rows(g + 1)
                with sp.Fori(NG - 3, NG - 1) as g:
                    neg_rows(g + 1)

            @block.gpsimd
            def _(pool):
                for g in range(2):
                    pool.tensor_copy(va_g[g][:, :, :, :], G.va[:, g, :, :, :]).then_inc(v_in, 1)
                with pool.Fori(1, NG // 2) as pair:
                    for k in range(2):
                        g = 2 * pair + k
                        pool.wait_ge(pv_done, NQ * (g - 1))
                        pool.tensor_copy(va_g[k][:, :, :, :],
                                         G.va[:, bass.ds(g, 1), :, :, :].rearrange("p o t h r -> p (o t) h r"))\
                            .then_inc(v_in, 1)

            @block.tensor
            def _(pe):
                def pieces(g, which):
                    for n in which:
                        h, i, k0, nk, _ = PIECES[n]
                        if not isinstance(g, int) or NP * g + n >= 2:
                            pe.wait_ge(piece_max, NP * g + n - 1)
                        if n == 0:
                            pe.wait_ge(qk_in, 64 * (g + 1))
                        diagonal = k0 + nk == (i + 1) * P
                        bank = max_bank[n % 2]
                        mm = pe.matmul(bank[:, 0:nk], qa[0:ROWS, g % RING, h, chunk(i, P)],
                                       ka[0:ROWS, g % RING, h, k0:k0 + nk], start=True, stop=True)
                        if diagonal:
                            mm = pe.matmul(bank[:, nk - P:nk], G.identb[:, :], G.mask_qk[:, :], start=False, stop=True,
                                           skip_group_check=True)
                        mm.then_inc(piece_psum, 1)

                def scores(g, u):
                    c, j, p = UNITS[u]
                    q0 = max(CH * c, P * j)
                    n = CH * (c + 1) - q0
                    if u == 0:
                        pe.wait_ge(neg_in, 48 * (g + 1))
                    if u >= 2:
                        pe.wait_ge(prob_done, NU * g + u - 1)
                    for k in range(2):
                        out = score_bank[u % 2][:, k, :]
                        diagonal = j >= 4 * c
                        mm = pe.matmul(out[:, 0:n], ka[0:ROWS + 3, g % RING, 2 * p + k, chunk(j, P)],
                                       qa[0:ROWS + 3, g % RING, 2 * p + k, q0:q0 + n], start=True, stop=True)
                        if diagonal:
                            mm = pe.matmul(out[:, 0:P], G.identb[:, :], G.mask_kq[:, :], start=False, stop=True,
                                           skip_group_check=True)
                    mm.then_inc(score_psum, 1)

                def outputs(g, k, q):
                    c, j, _ = UNITS[2 * q]
                    q0 = max(CH * c, P * j)
                    n = CH * (c + 1) - q0
                    pe.wait_ge(prob_done, NU * g + 2 * q + 2)
                    if q == 0:
                        pe.wait_ge(v_in, g + 1)
                    if j == 0 and (not isinstance(g, int) or 2 * g + c):
                        pe.wait_ge(acc_kept, 2 * g + c)
                    for h in range(HG):
                        mm = pe.matmul(acc_bank[32 * h:32 * h + 32, q0 - CH * c:CH], va_g[k][:, j, h, :],
                                       pt[:, 2 * (q % 2) + h // 2, h % 2, 0:n], start=(j == 0),
                                       stop=(j >= 4 * c), skip_group_check=True)
                    mm.then_inc(pv_done, 1)

                def denominators(g, c):
                    pe.wait_ge(acc_kept, 2 * g + c + 1)
                    if not isinstance(g, int) or 2 * g + c:
                        pe.wait_ge(den_log, 2 * g + c)
                    pe.matmul(misc[:, :], G.den_row[:, :], acc[:, c, :], start=True, stop=True).then_inc(den_psum, 1)

                def turn_neg(g):
                    pe.wait_ge(max_step, 6 * (g + 1))
                    pe.transpose(misc[:, :].bitcast(BF16)[0:3 * HG * 8, 0:P], neg[:, :, :, :].rearrange("p a h t -> p (a h t)"),
                                 G.identb[:, :]).then_inc(neg_turned, 1)

                def group(g, k, first=False, last=False):
                    for u in range(NU):
                        if not last:
                            pieces(g + 1, SCHED[u][0])
                            if u == TURN:
                                pe.wait_ge(den_log, 2 * g + 1)
                                turn_neg(g + 1)
                        scores(g, u)
                        if not last:
                            pieces(g + 1, SCHED[u][1])
                        if u % 2 and u >= 3:
                            outputs(g, k, (u - 3) // 2)
                        if u == DEN_C0:
                            denominators(g, 0)
                        if u == TAIL_DEN and not first:
                            pe.wait_ge(neg_kept, g + 1)
                            denominators(g - 1, 1)
                        if u == PROJECT and last:
                            pe.wait_ge(out_done, NG)
                            project(pe, G, 0)
                            project(pe, G, 1)
                    outputs(g, k, NQ - 1)

                pieces(0, range(NP))
                turn_neg(0)
                pe.wait_ge(neg_kept, 1)
                groups(pe, group)
                denominators(NG - 1, 1)

            @block.scalar
            def _(act):
                def probabilities(g, u):
                    c, j, p = UNITS[u]
                    n = CH * (c + 1) - max(CH * c, P * j)
                    act.wait_ge(score_psum, NU * g + u + 1)
                    if not isinstance(g, int) or g or u >= 4:
                        act.wait_ge(pv_done, NQ * g + max(0, u // 2 - 1))
                    act.activation(pt[:, u % 4, :, 0:n], score_bank[u % 2][:, :, 0:n], ACT.Exp, scale=SCALE)\
                        .then_inc(prob_done, 1)

                def inverse(g, c):
                    act.wait_ge(den_psum, 2 * g + c + 1)
                    if not isinstance(g, int) or g:
                        act.wait_ge(out_done, 2 * g)
                    act.activation(rden[:, c, :], misc[:, :], ACT.Ln).then_inc(den_log, 1)
                    act.wait_ge(den_log, 2 * g + c + 1)
                    act.activation(rden[:, c, :], rden[:, c, :], ACT.Exp, scale=-1.0).then_inc(den_inv, 1)

                def group(g, k, first=False, last=False):
                    for u in range(NU):
                        probabilities(g, u)
                        if u == DEN_C0 + 1:
                            inverse(g, 0)
                        if u == TAIL_DEN + 1 and not first:
                            inverse(g - 1, 1)

                groups(act, group)
                inverse(NG - 1, 1)

            @block.vector
            def _(dve):
                def pieces(g, which):
                    for n in which:
                        h, i, k0, nk, slot = PIECES[n]
                        dve.wait_ge(piece_psum, NP * g + n + 1)
                        dve.tensor_reduce(part_max[:, h, slot:slot + 1], max_bank[n % 2][:, 0:nk], AX_X, ALU.max)\
                            .then_inc(piece_max, 1)

                def negate(g):
                    dve.wait_ge(piece_max, NP * (g + 1))
                    dve.tensor_tensor(part_max[:, :, 4:8], part_max[:, :, 4:8], part_max[:, :, 8:12], ALU.max)\
                        .then_inc(max_step, 1)
                    dve.wait_ge(max_step, 6 * g + 1)
                    dve.tensor_scalar(neg[:, 0, :, :], part_max[:, :, 0:8], -1.0, None, ALU.mult).then_inc(max_step, 1)
                    dve.wait_ge(max_step, 6 * g + 2)
                    dve.scalar_tensor_tensor(neg_rest[:, 0, :, :], part_max[:, :, 0:8], -1.0, neg[:, 0, :, :],
                                             ALU.mult, ALU.subtract).then_inc(max_step, 1)
                    dve.wait_ge(max_step, 6 * g + 3)
                    dve.tensor_copy(neg[:, 1, :, :], neg_rest[:, 0, :, :]).then_inc(max_step, 1)
                    dve.wait_ge(max_step, 6 * g + 4)
                    dve.tensor_tensor(neg_rest[:, 1, :, :], neg_rest[:, 0, :, :], neg[:, 1, :, :], ALU.subtract)\
                        .then_inc(max_step, 1)
                    dve.wait_ge(max_step, 6 * g + 5)
                    dve.tensor_copy(neg[:, 2, :, :], neg_rest[:, 1, :, :]).then_inc(max_step, 1)

                def keep_neg(g):
                    dve.wait_ge(neg_turned, g + 1)
                    if not isinstance(g, int) or g:
                        dve.wait_ge(neg_in, 48 * g)
                    dve.tensor_copy(neg_t[:, :], misc[:, :].bitcast(BF16)[0:3 * HG * 8, 0:P]).then_inc(neg_kept, 1)

                def keep_acc(g, c):
                    dve.wait_ge(pv_done, NQ * g + (4, NQ)[c])
                    dve.tensor_copy(acc[:, c, :], acc_bank[:, :]).then_inc(acc_kept, 1)

                def normalise(g, c):
                    dve.wait_ge(den_inv, 2 * g + c + 1)
                    dve.tensor_tensor(G.o[:, g % 4, bass.ds((g // 4) * S + c * CH, CH)], acc[:, c, :], rden[:, c, :],
                                      ALU.mult).then_inc(out_done, 1)

                def group(g, k, first=False, last=False):
                    for u in range(NU):
                        if not last:
                            for which in SCHED[u]:
                                pieces(g + 1, which)
                            if u == TURN:
                                negate(g + 1)
                                keep_neg(g + 1)
                        if u == PV_C0 + 1:
                            keep_acc(g, 0)
                        if u == OUT_C0:
                            normalise(g, 0)
                        if u == 0 and not first:
                            keep_acc(g - 1, 1)
                        if u == TAIL_DEN + 2 and not first:
                            normalise(g - 1, 1)
                        if u == PROJECT and last:
                            add_attention(dve, G, 0)
                            add_attention(dve, G, 1)

                pieces(0, range(NP))
                negate(0)
                keep_neg(0)
                groups(dve, group)
                keep_acc(NG - 1, 1)
                normalise(NG - 1, 1)


def project(pe, G, c):
    for g in range(4):
        mm = pe.matmul(G.bank[5 if c == 1 else 4][:, :], G.wo_t[:, g, :], G.o[:, g, chunk(c)], start=(g == 0), stop=(g == 3))
    mm.then_inc(G.wo_psum, 1)


def add_attention(dve, G, c):
    dve.wait_ge(G.wo_psum, c + 1)
    dve.scalar_tensor_tensor(G.x[:, chunk(c)], G.bank[5 if c == 1 else 4][:, :], G.mod[:, 0, 2, c // 2:c // 2 + 1],
                             G.x[:, chunk(c)], ALU.mult, ALU.add).then_inc(G.x_new, 1)


BIG = 3e38


def stage_router(nc, G, A):
    mem = G.mem
    E, GROUPS, KEEP_GROUPS, TOP = 64, 8, 4, 6
    PER = E // GROUPS
    with ExitStack() as ctx:
        m = Memory(nc, ctx)
        score = m.sb("score", [P, NT, E])
        wide = m.sb("wide", [P, NT, E + 2])
        wide_out = m.sb("wide_out", [P, NT, E + 2])
        gmax = m.sb("gmax", [P, NT, 12])
        gmax_out = m.sb("gmax_out", [P, NT, 12])
        gmask = m.sb("gmask", [P, NT, GROUPS])
        best = m.sb("best", [P, NT, 8])
        pick = m.sb("pick", [P, NT, 8])
        best6 = m.sb("best6", [P, NT, 8])
        pick6 = m.sb("pick6", [P, NT, 8])
        total = m.sb("total", [P, NT, 1])
        chosen = m.sb("chosen", [P, NT, E])
        comb = m.sb("comb", [E, 2, CH])
        x_new, h_done = G.x_new, mem.sem("h2_done")
        logit_psum, exp_done = mem.sem("logit_psum"), mem.sem("gate_exp")
        pads, step, comb_done = mem.sem("route_pads"), mem.sem("route_step"), mem.sem("comb_done")
        comb_psum, comb_kept = mem.sem("comb_psum"), mem.sem("comb_kept")
        comb_out = [mem.sem(f"comb_out{k}") for k in range(2)]
        cb, sb_ = G.mod[:, 0, 4, :], G.mod[:, 0, 3, :]
        n0 = G.ln_count
        G.ln_count += NC
        with nc.Block() as block:
            @block.tensor
            def _(pe):
                def logits(c):
                    pe.wait_ge(h_done, c + 1)
                    if c >= 1:
                        pe.wait_ge(exp_done, c)
                    for t in range(4):
                        mm = pe.matmul(G.bank[5][:, chunk(t, E)], G.h[:, chunk(4 * c + t, P)], G.gate0[:, :],
                                       start=True, stop=True)
                    mm.then_inc(logit_psum, 1)

                def turn(c):
                    pe.wait_ge(comb_done, c + 1)
                    if c >= 1:
                        pe.wait_ge(comb_kept, c)
                    for t in range(4):
                        mm = pe.transpose(G.bank[6][0:E, chunk(t, P)], chosen[:, 4 * c + t, :], G.ident[:, :])
                    mm.then_inc(comb_psum, 1)

                def norm(c):
                    pe.wait_ge(x_new, c + 1)
                    ln_centre(pe, G, n0 + c, G.x[:, chunk(c)])
                    ln_variance(pe, G, n0 + c)

                norm(0)
                norm(1)
                logits(0)
                project(pe, G, 2)
                logits(1)
                for c in range(2, NC):
                    norm(c)
                    if c + 1 < NC:
                        pe.wait_ge(x_new, c + 1)
                        project(pe, G, c + 1)
                    logits(c)
                    turn(c - 2)
                turn(NC - 2)
                turn(NC - 1)

            @block.scalar
            def _(act):
                def keep_comb(c):
                    act.wait_ge(comb_psum, c + 1)
                    if c >= 2:
                        act.wait_ge(comb_out[c % 2], 16 * (c // 2))
                    act.copy(comb[:, c % 2, :], G.bank[6][0:E, :]).then_inc(comb_kept, 1)

                def exponentials(c):
                    act.wait_ge(logit_psum, c + 1)
                    act.activation(score[:, 4 * c:4 * c + 4, :],
                                   G.bank[5][:, 0:4 * E].rearrange("p (t e) -> p t e", t=4), ACT.Exp, scale=-1.0)\
                        .then_inc(exp_done, 1)

                for c in range(2):
                    ln_square(act, G, n0 + c)
                    ln_rstd(act, G, n0 + c)
                exponentials(0)
                exponentials(1)
                for c in range(2, NC):
                    ln_square(act, G, n0 + c)
                    ln_rstd(act, G, n0 + c)
                    exponentials(c)
                    keep_comb(c - 2)
                keep_comb(NC - 2)
                keep_comb(NC - 1)

            @block.vector
            def _(dve):
                count = [0]

                def link(ins):
                    count[0] += 1
                    ins.then_inc(step, 1)
                    dve.wait_ge(step, count[0])

                def route(c):
                    t4 = slice(4 * c, 4 * c + 4)
                    sc = score[:, t4, :]
                    dve.wait_ge(exp_done, c + 1)
                    link(dve.tensor_scalar(sc, sc, 1.0, None, ALU.add))
                    link(dve.reciprocal(sc, sc))
                    link(dve.tensor_tensor(sc, sc, G.gate_bias[:, :].unsqueeze(1).to_broadcast([P, 4, E]), ALU.add))
                    link(dve.tensor_reduce(gmax[:, t4, 0:GROUPS], sc.rearrange("p t (g e) -> p t g e", g=GROUPS), AX_X, ALU.max))
                    for t in range(4 * c, 4 * c + 4):
                        last = dve.max(best[:, t, :], gmax[:, t, 0:GROUPS])
                    link(last)
                    link(dve.tensor_copy(pick[:, t4, 0:KEEP_GROUPS], best[:, t4, 0:KEEP_GROUPS]))
                    for t in range(4 * c, 4 * c + 4):
                        last = dve.match_replace(gmax_out[:, t, :], pick[:, t, :], gmax[:, t, :], -BIG)
                    link(last)
                    link(dve.tensor_tensor(gmask[:, t4, :], gmax_out[:, t4, 0:GROUPS], gmax[:, t4, 0:GROUPS], ALU.not_equal))
                    for t in range(4 * c, 4 * c + 4):
                        last = dve.tensor_tensor(wide[:, t, 0:E].rearrange("p (g e) -> p g e", g=GROUPS),
                                                 score[:, t, :].rearrange("p (g e) -> p g e", g=GROUPS),
                                                 gmask[:, t, :].unsqueeze(2).to_broadcast([P, GROUPS, PER]), ALU.mult)
                    link(last)
                    for t in range(4 * c, 4 * c + 4):
                        last = dve.max(best6[:, t, :], wide[:, t, 0:E])
                    link(last)
                    link(dve.tensor_copy(pick6[:, t4, 0:TOP], best6[:, t4, 0:TOP]))
                    link(dve.tensor_reduce(total[:, t4, 0], best6[:, t4, 0:TOP], AX_X, ALU.add))
                    link(dve.tensor_scalar(total[:, t4, :], total[:, t4, :], 1e-8, None, ALU.add))
                    link(dve.reciprocal(total[:, t4, :], total[:, t4, :]))
                    for t in range(4 * c, 4 * c + 4):
                        last = dve.match_replace(wide_out[:, t, :], pick6[:, t, :], wide[:, t, :], -BIG)
                    link(last)
                    link(dve.tensor_tensor(chosen[:, t4, :], wide_out[:, t4, 0:E], wide[:, t4, 0:E], ALU.not_equal))
                    link(dve.tensor_tensor(chosen[:, t4, :], chosen[:, t4, :], wide[:, t4, 0:E], ALU.mult))
                    dve.tensor_tensor(chosen[:, t4, :], chosen[:, t4, :], total[:, t4, :].to_broadcast([P, 4, E]),
                                      ALU.mult).then_inc(comb_done, 1)

                link(dve.memset(wide[:, :, E:E + 2], BIG))
                link(dve.memset(gmax[:, :, GROUPS:12], BIG))
                link(dve.memset(pick[:, :, KEEP_GROUPS:8], BIG))
                link(dve.memset(pick6[:, :, TOP:8], BIG))
                def norm(c):
                    ln_scale(dve, G, n0 + c, G.h[:, chunk(c)], cb[:, c // 2:c // 2 + 1])
                    dve.wait_ge(G.ln.scaled, n0 + c + 1)
                    dve.tensor_scalar(G.h[:, chunk(c)], G.h[:, chunk(c)], sb_[:, c // 2:c // 2 + 1], None, ALU.add)\
                        .then_inc(h_done, 1)

                norm(0)
                norm(1)
                for c in range(NC):
                    if c + 2 < NC:
                        add_attention(dve, G, c + 2)
                    route(c)
                    if c + 2 < NC:
                        norm(c + 2)

            @block.sync
            def _(sp):
                for j, name in enumerate(("sg_w", "su_w", "sd_w")):
                    sp.dma_start(G.raw[0][:, j, :], A["L0_ffn_" + name]).then_inc(G.raw_in[0], 16)
                load_experts(sp, G, A, 1, 1)
                for c in range(NC):
                    sp.wait_ge(comb_kept, c + 1)
                    sp.dma_start(G.comb_d[:, chunk(c)], comb[:, c % 2, :]).then_inc(comb_out[c % 2], 16)
                for k in range(2):
                    sp.wait_ge(comb_out[k], 16 * NC // 2)


def load_experts(sp, G, A, s, k):
    e = 2 * (s - 1)
    for j, name in enumerate(("eg_w", "eu_w")):
        sp.dma_start(G.raw[k][:, j, :], A["L0_ffn_" + name].rearrange("e i h -> (e i) h")[bass.ds(64 * e, P), :])\
            .then_inc(G.raw_in[k], 16)
    sp.dma_start(G.raw[k][:, 2, :].rearrange("h (e i) -> h e i", e=2),
                 A["L0_ffn_ed_w"][bass.ds(e, 2), :, :].rearrange("e h i -> h e i")).then_inc(G.raw_in[k], 16)


def stage_experts(nc, G, A):
    mem = G.mem
    STEPS = 33
    with ExitStack() as ctx:
        m = Memory(nc, ctx)
        raw, raw_in = G.raw, G.raw_in
        comb = [m.sb(f"moe_comb{k}", [P, T]) for k in range(2)]
        wt = [m.sb(f"moe_wt{k}", [P, 3, P]) for k in range(2)]
        sg = m.sb("moe_silu", [P, 2, CH])
        gu = m.sb("moe_gu", [P, 2, CH])
        hid = m.sb("moe_hid", [P, NC, CH])
        comb_in = [mem.sem(f"moe_comb_in{k}") for k in range(2)]
        w_turned, w_kept = mem.sem("moe_turned"), mem.sem("moe_kept")
        g_psum, u_psum, y_psum = mem.sem("moe_g"), mem.sem("moe_u"), mem.sem("moe_y")
        silu_done, gu_done, hid_done = mem.sem("moe_silu_done"), mem.sem("moe_gu_done"), mem.sem("moe_hid_done")
        y_bank, g_bank, u_bank, t_bank = G.bank[0:4], G.bank[4], G.bank[5], G.bank[7]

        def steps(eng, body):
            body(0, 0)
            with eng.Fori(0, (STEPS - 3) // 2) as i:
                body(2 * i + 1, 1)
                body(2 * i + 2, 0)
            body(STEPS - 2, 1)
            body(STEPS - 1, 0, last=True)

        def before(s, c):
            return not isinstance(s, int) or 4 * s + c >= 1

        with nc.Block() as block:
            @block.sync
            def _(sp):
                def factors(s, k):
                    for e in range(2):
                        sp.dma_start(comb[k][chunk(e, 64), :], G.comb_d[bass.ds(2 * (s - 1) + e, 1), :].to_broadcast([64, T]))\
                            .then_inc(comb_in[k], 16)

                factors(1, 1)
                sp.wait_ge(w_turned, 1)
                load_experts(sp, G, A, 2, 0)
                factors(2, 0)
                with sp.Fori(0, (STEPS - 3) // 2) as i:
                    for k in (1, 0):
                        s = 2 * i + 2 - k
                        sp.wait_ge(w_turned, s + 1)
                        load_experts(sp, G, A, s + 2, k)
                        sp.wait_ge(hid_done, 4 * s + 4)
                        factors(s + 2, k)

            @block.tensor
            def _(pe):
                def turn(s, k):
                    pe.wait_ge(raw_in[k], 48 * (s // 2 + 1))
                    pe.wait_ge(w_kept, s)
                    for j in range(3):
                        mm = pe.transpose(t_bank[:, chunk(j, P)], raw[k][:, j, :], G.ident[:, :])
                    mm.then_inc(w_turned, 1)

                def down(s, c, k, first, last):
                    pe.wait_ge(hid_done, 4 * s + c + 1)
                    pe.matmul(y_bank[c][:, :], wt[k][:, 2, :], hid[:, c, :], start=first, stop=last,
                              skip_group_check=True).then_inc(y_psum, 1)

                def step(s, k, last=False):
                    for c in range(NC):
                        if c == 0:
                            pe.wait_ge(w_kept, s + 1)
                        if before(s, c):
                            pe.wait_ge(silu_done, 4 * s + c)
                        pe.matmul(g_bank[:, :], wt[k][:, 0, :], G.h[:, chunk(c)], start=True, stop=True).then_inc(g_psum, 1)
                        if c == 1 and not last:
                            turn(s + 1, 1 - k)
                        if c >= 2:
                            down(s, c - 2, k, isinstance(s, int) and s == 0, last)
                        elif not isinstance(s, int) or s >= 1:
                            down(s - 1, c + 2, 1 - k, isinstance(s, int) and s == 1, False)
                        if before(s, c):
                            pe.wait_ge(gu_done, 4 * s + c)
                        pe.matmul(u_bank[:, :], wt[k][:, 1, :], G.h[:, chunk(c)], start=True, stop=True).then_inc(u_psum, 1)
                    if last:
                        down(s, 2, k, False, True)
                        down(s, 3, k, False, True)

                turn(0, 0)
                step(0, 0)
                step(1, 1)
                with pe.Fori(0, (STEPS - 3) // 2) as i:
                    step(2 * i + 2, 0)
                    step(2 * i + 3, 1)
                step(STEPS - 1, 0, last=True)

            @block.scalar
            def _(act):
                def keep_weights(s, k):
                    act.wait_ge(w_turned, s + 1)
                    if not isinstance(s, int) or s >= 2:
                        act.wait_ge(y_psum, 4 * (s - 1))
                    act.copy(wt[k][:, :, :], t_bank[:, 0:3 * P].rearrange("p (j m) -> p j m", j=3)).then_inc(w_kept, 1)

                def step(s, k, last=False):
                    for c in range(NC):
                        act.wait_ge(g_psum, 4 * s + c + 1)
                        if not isinstance(s, int) or 4 * s + c >= 2:
                            act.wait_ge(gu_done, 4 * s + c - 1)
                        act.activation(sg[:, c % 2, :], g_bank[:, :], ACT.Silu).then_inc(silu_done, 1)
                        if c == 1 and not last:
                            keep_weights(s + 1, 1 - k)

                keep_weights(0, 0)
                steps(act, step)
                load_act_set(nc, act, EXP_LN_SET)

            @block.vector
            def _(dve):
                def step(s, k, last=False):
                    for c in range(NC):
                        n = 4 * s + c
                        dve.wait_ge(silu_done, n + 1)
                        dve.wait_ge(u_psum, n + 1)
                        dve.tensor_tensor(gu[:, c % 2, :], sg[:, c % 2, :], u_bank[:, :], ALU.mult).then_inc(gu_done, 1)
                        dve.wait_ge(gu_done, n + 1)
                        if c == 0 and not (isinstance(s, int) and s == 0):
                            dve.wait_ge(comb_in[k], 32 * ((s + 1) // 2))
                        if not isinstance(s, int) or n >= 4:
                            dve.wait_ge(y_psum, n - 3)
                        if isinstance(s, int) and s == 0:
                            dve.tensor_copy(hid[:, c, :], gu[:, c % 2, :]).then_inc(hid_done, 1)
                        else:
                            dve.tensor_tensor(hid[:, c, :], gu[:, c % 2, :], comb[k][:, chunk(c)], ALU.mult).then_inc(hid_done, 1)

                steps(dve, step)
                for c in range(NC):
                    dve.wait_ge(y_psum, 4 * (STEPS - 1) + c + 1)
                    dve.scalar_tensor_tensor(G.x[:, chunk(c)], y_bank[c][:, :], G.mod[:, 0, 5, c // 2:c // 2 + 1],
                                             G.x[:, chunk(c)], ALU.mult, ALU.add).then_inc(G.x_l0, 1)


def load_time_weights(sp, G, A, l):
    for i, name in enumerate(("Wk", "Wv", "Wr", "Wo")):
        sp.dma_start(G.raw_a[:, i, :], A["L1_attn_" + name][bass.ds(l, 1)].rearrange("o a c -> (o a) c")).then_inc(G.a_in, 16)


def load_channel_weights(sp, G, A, l):
    one = bass.ds(l, 1)
    sp.dma_start(G.raw_c[:, 0:4, :], A["L1_attn_Wck"][one].rearrange("o (j f) c -> f (o j) c", f=P)).then_inc(G.c_in, 16)
    sp.dma_start(G.raw_c[:, 4:8, :].rearrange("p j f -> p (j f)"), A["L1_attn_Wcv"][one].rearrange("o c f -> (o c) f"))\
        .then_inc(G.c_in, 16)
    sp.dma_start(G.raw_c[:, 8, :], A["L1_attn_Wcr"][one].rearrange("o a c -> (o a) c")).then_inc(G.c_in, 16)


def stage_rwkv_in(nc, G, A):
    mem = G.mem
    with ExitStack() as ctx:
        m = Memory(nc, ctx)
        h = m.sb("h_mod", [P, T])
        h_done = mem.sem("h3_done")
        n0 = G.ln_count
        G.ln_count += 2 * NC
        ca, sa = G.mod[:, 1, 1, :], G.mod[:, 1, 0, :]
        w, b = G.vec[:, 44:45], G.vec[:, 45:46]
        CALLS = [(0, 0), (0, 1), (0, 2), (1, 0), (0, 3), (1, 1), (1, 2), (1, 3)]
        with nc.Block() as block:
            @block.sync
            def _(sp):
                load_time_weights(sp, G, A, 0)
                load_channel_weights(sp, G, A, 0)

            @block.tensor
            def _(pe):
                for n, (which, c) in enumerate(CALLS):
                    if n >= 2:
                        ln_variance(pe, G, n0 + n - 1)
                    if which == 1:
                        pe.wait_ge(h_done, c + 1)
                    ln_centre(pe, G, n0 + n, (h if which else G.x)[:, chunk(c)])
                    if n == 1:
                        ln_variance(pe, G, n0)
                ln_variance(pe, G, n0 + 7)

            @block.scalar
            def _(act):
                for n in range(len(CALLS)):
                    if n >= 2:
                        ln_rstd(act, G, n0 + n - 1)
                    ln_square(act, G, n0 + n)
                    if n == 1:
                        ln_rstd(act, G, n0)
                ln_rstd(act, G, n0 + 7)

            @block.vector
            def _(dve):
                for n, (which, c) in enumerate(CALLS):
                    bb = c // 2
                    if which == 0:
                        ln_scale(dve, G, n0 + n, h[:, chunk(c)], ca[:, bb:bb + 1])
                        dve.wait_ge(G.ln.scaled, n0 + n + 1)
                        dve.tensor_scalar(h[:, chunk(c)], h[:, chunk(c)], sa[:, bb:bb + 1], None, ALU.add).then_inc(h_done, 1)
                    else:
                        ln_scale(dve, G, n0 + n, G.r[:, chunk(c)], w)
                        dve.wait_ge(G.ln.scaled, n0 + n + 1)
                        dve.tensor_scalar(G.r[:, chunk(c)], G.r[:, chunk(c)], b, None, ALU.add).then_inc(G.r_done, 1)


def stage_rwkv(nc, G, A):
    mem = G.mem
    WK, WV, WR, WO = 0, 1, 2, 3
    WCK, WCV, WCR = 0, 4, 8
    STEPS, ACT_STEPS = 17, 8
    LAST = 2 * LAYERS - 1
    with ExitStack() as ctx:
        m = Memory(nc, ctx)
        raw_a, raw_c, a_in, c_in = G.raw_a, G.raw_c, G.a_in, G.c_in
        wt_a, wt_c = m.sb("wt_a", [P, 4, P]), m.sb("wt_c", [P, 9, P])
        vec_a = m.sb("vec_a", [P, 12])
        vec_c = m.sb("vec_c", [P, 11])
        hp = m.sb("hp", [P, B, S + 1])
        diff_a, diff_c = m.sb("diff_a", [P, 2, CH]), m.sb("diff_c", [P, 2, CH])
        mix_a, mix_c = m.sb("mix_a", [P, 3, 2, CH]), m.sb("mix_c", [P, 2, 2, CH])
        k_s, v_s, sr = (m.sb(n, [P, S]) for n in ("k_s", "v_s", "sr"))
        pp, aa, bb = (m.sb(n, [P, S + 1]) for n in ("pp", "aa", "bb"))
        e1b, e2b, e1, e2, num, den, n2, rw = (m.sb(n, [P, S]) for n in ("e1b", "e2b", "e1", "e2", "num", "den", "n2", "rw"))
        rl = m.sb("relu", [P, 2, CH])
        kf = m.sb("kf", [P, 4, 2, CH])
        sc, kvs = m.sb("sc", [P, 2, CH]), m.sb("kvs", [P, 2, CH])

        a_turned, a_kept = mem.sem("rw_a_turned"), mem.sem("rw_a_kept")
        c_turned, c_kept = mem.sem("rw_c_turned"), mem.sem("rw_c_kept")
        start = mem.sem("rw_start")
        vec_a_done, vec_c_done = mem.sem("rw_vec_a"), mem.sem("rw_vec_c")
        h_step = mem.sem("rw_h_step")
        mixed_a, mixed_c = mem.sem("rw_mixed_a"), mem.sem("rw_mixed_c")
        part_mixed = mem.sem("rw_part_mixed")
        mixed_p = mem.sem("rw_mixed_p")
        k_psum, v_psum, r_psum = mem.sem("rw_k"), mem.sem("rw_v"), mem.sem("rw_r")
        k_kept, v_kept, sr_done = mem.sem("rw_k_kept"), mem.sem("rw_v_kept"), mem.sem("rw_sr")
        wd, wa, wp = mem.sem("wkv_dve"), mem.sem("wkv_act"), mem.sem("wkv_pool")
        o_psum, r_mid = mem.sem("rw_o"), mem.sem("rw_r_mid")
        cr_psum, sc_done = mem.sem("rw_cr"), mem.sem("rw_sc")
        f_psum, relu_done, kf_done = mem.sem("rw_f"), mem.sem("rw_relu"), mem.sem("rw_kf")
        kv_psum, kv_step = mem.sem("rw_kv"), mem.sem("rw_kv_step")
        r_kept = mem.sem("rw_r_kept")
        r_new = mem.sem("rw_r_new")
        n0 = G.ln_count
        G.ln_count += 8 * LAYERS
        banks = G.psum3

        def seq(b, q):
            return slice(b * S + q * CH, b * S + (q + 1) * CH)

        def ln_time(u, q):
            return n0 + 4 * u - 2 + q

        def ln_channel(u, q):
            return n0 + 4 * u + (2 if isinstance(u, int) and u == LAST else 4) + q

        def layers(eng, body):
            with eng.Fori(0, LAYERS - 1) as l:
                body(l, 0)
                body(l, 1)
            body(LAYERS - 1, 0)
            body(LAYERS - 1, 1, last=True)

        with nc.Block() as block:
            @block.sync
            def _(sp):
                with sp.Fori(0, LAYERS - 1) as l:
                    sp.wait_ge(a_turned, l + 1)
                    load_time_weights(sp, G, A, l + 1)
                    sp.wait_ge(c_turned, 3 * (l + 1))
                    load_channel_weights(sp, G, A, l + 1)

            @block.tensor
            def _(pe):
                def turn_a(l):
                    pe.wait_ge(a_in, 64 * (l + 1))
                    for i in range(4):
                        mm = pe.transpose(G.bank[6][:, chunk(i, P)], raw_a[:, i, :], G.ident[:, :])
                    mm.then_inc(a_turned, 1)

                def turn_c(l, u):
                    pe.wait_ge(c_in, 48 * (l + 1))
                    for i in range(9):
                        if i == 8:
                            pe.wait_ge(r_mid, 2 * u + 2)
                        mm = pe.transpose(G.bank[(6, 7, 5)[i // 4]][:, chunk(i % 4, P)], raw_c[:, i, :], G.ident[:, :])
                        if i % 4 == 3 or i == 8:
                            mm.then_inc(c_turned, 1)

                def output(u):
                    for q in range(2):
                        pe.wait_ge(wd, STEPS * u + 16 + q)
                        pe.matmul(G.bank[4 + q][:, :], wt_a[:, WO, :], rw[:, chunk(q)], start=True, stop=True)\
                            .then_inc(o_psum, 1)

                def norm(number, b, ready):
                    for q in range(2):
                        ready(q)
                        ln_centre(pe, G, number(q), G.r[:, seq(b, q)], q)
                    for q in range(2):
                        ln_variance(pe, G, number(q), q)

                def kvr(u):
                    for q in range(2):
                        pe.wait_ge(mixed_a, 2 * u + q + 1)
                        if q == 1:
                            pe.wait_ge(k_kept, 2 * u + 1)
                            pe.wait_ge(v_kept, 2 * u + 1)
                        pe.matmul(G.bank[4][:, :], wt_a[:, WK, :], mix_a[:, 0, q, :], start=True, stop=True).then_inc(k_psum, 1)
                        pe.matmul(G.bank[5][:, :], wt_a[:, WV, :], mix_a[:, 1, q, :], start=True, stop=True).then_inc(v_psum, 1)
                    for q in range(2):
                        pe.wait_ge(mixed_p, (4 * u - 2 if not isinstance(u, int) or u else 0) + q + 1)
                        pe.matmul(G.bank[6 + q][:, :], wt_a[:, WR, :], mix_a[:, 2, q, :], start=True, stop=True)\
                            .then_inc(r_psum, 1)

                def channel_mix(u, last):
                    def up(q, j):
                        if 4 * q + j >= 2:
                            pe.wait_ge(relu_done, 8 * u + 4 * q + j - 1)
                        pe.matmul(G.bank[4 + j % 2][:, :], wt_c[:, WCK + j, :], mix_c[:, 0, q, :], start=True, stop=True)\
                            .then_inc(f_psum, 1)

                    def down(q, j):
                        pe.wait_ge(kf_done, 8 * u + 4 * q + j + 1)
                        if q == 0 and j == 0:
                            if last:
                                pe.wait_ge(r_new, 2 * u + 2)
                            else:
                                pe.wait_ge(r_kept, u + 2)
                        mm = pe.matmul(G.bank[6 + q][:, :], wt_c[:, WCV + j, :], kf[:, j, q, :], start=(j == 0), stop=(j == 3))
                        if j == 3:
                            mm.then_inc(kv_psum, 1)

                    if not last:
                        pe.wait_ge(k_kept, 2 * u + 4)
                        pe.wait_ge(v_kept, 2 * u + 4)
                    def gate(q):
                        pe.wait_ge(mixed_p, 4 * u + (2 if last else 4) + q + 1)
                        if q == 0:
                            pe.wait_ge(G.ln.rstd, ln_channel(u, 1) + 1)
                        pe.matmul(G.bank[2 + q][:, :], wt_c[:, WCR, :], mix_c[:, 1, q, :], start=True, stop=True)\
                            .then_inc(cr_psum, 1)

                    pe.wait_ge(mixed_c, 2 * u + 1)
                    for j in range(4):
                        up(0, j)
                    gate(0)
                    pe.wait_ge(mixed_c, 2 * u + 2)
                    up(1, 0)
                    up(1, 1)
                    gate(1)
                    for j in range(4):
                        down(0, j)
                        if j < 2:
                            up(1, j + 2)
                    for j in range(4):
                        down(1, j)

                def body(l, b, last=False):
                    u = 2 * l + b
                    output(u)
                    if not last:
                        norm(lambda q: ln_time(u + 1, q), 1 - b, lambda q: pe.wait_ge(r_new, 2 * u + q + 1))
                        if b == 0:
                            turn_c(l, u)
                        else:
                            turn_a(l + 1)
                    norm(lambda q: ln_channel(u, q), b, lambda q: pe.wait_ge(r_mid, 2 * u + q + 1))
                    if not last:
                        if b == 0:
                            pe.wait_ge(c_kept, 3 * (l + 1))
                        else:
                            pe.wait_ge(a_kept, l + 2)
                        kvr(u + 1)
                    channel_mix(u, last)

                turn_a(0)
                norm(lambda q: n0 + q, 0, lambda q: None)
                pe.wait_ge(a_kept, 1)
                kvr(0)
                layers(pe, body)

            @block.scalar
            def _(act):
                def norm(number):
                    for q in range(2):
                        ln_square(act, G, number(q), q)
                    for q in range(2):
                        ln_rstd(act, G, number(q), q)

                def keep_a(l):
                    act.wait_ge(a_turned, l + 1)
                    act.copy(wt_a[:, :, :].rearrange("p j m -> p (j m)"), G.bank[6][:, :]).then_inc(a_kept, 1)

                def keep_c(l):
                    for i in range(3):
                        act.wait_ge(c_turned, 3 * l + i + 1)
                        act.copy(wt_c[:, 4 * i:min(9, 4 * i + 4), :].rearrange("p j m -> p (j m)"),
                                 G.bank[(6, 7, 5)[i]][:, 0:(4, 4, 1)[i] * P]).then_inc(c_kept, 1)

                def gate_part(call, diff, vec, tm, mix):
                    for q in range(2):
                        act.wait_ge(h_step, 4 * call + 3 + q)
                        act.activation(mix[:, q, :], diff[:, q, :], ACT.Copy, scale=vec[:, tm:tm + 1]).then_inc(part_mixed, 1)

                def keep_kv(u):
                    for q in range(2):
                        act.wait_ge(k_psum, 2 * u + q + 1)
                        act.copy(k_s[:, chunk(q)], G.bank[4][:, :]).then_inc(k_kept, 1)
                        act.wait_ge(v_psum, 2 * u + q + 1)
                        act.copy(v_s[:, chunk(q)], G.bank[5][:, :]).then_inc(v_kept, 1)

                def keep_r(u):
                    act.wait_ge(r_psum, 2 * u + 2)
                    act.copy(sr[:, :].rearrange("p (q n) -> p q n", q=2), banks[:, 6:8, :]).then_inc(r_kept, 1)

                def decays(u):
                    act.wait_ge(wd, STEPS * u + 2)
                    act.activation(e2b[:, :], e2b[:, :], ACT.Exp).then_inc(wa, 1)
                    act.wait_ge(wd, STEPS * u + 3)
                    act.activation(e1b[:, :], e1b[:, :], ACT.Exp).then_inc(wa, 1)

                def weights(u):
                    act.wait_ge(wd, STEPS * u + 5)
                    act.activation(e2[:, :], e2[:, :], ACT.Exp).then_inc(wa, 1)
                    act.wait_ge(wd, STEPS * u + 6)
                    act.activation(e1[:, :], e1[:, :], ACT.Exp, scale=-1.0).then_inc(wa, 1)

                def inverse(u):
                    for q in range(2):
                        act.wait_ge(wd, STEPS * u + 12 + q)
                        act.activation(den[:, chunk(q)], den[:, chunk(q)], ACT.Ln).then_inc(wa, 1)
                        act.wait_ge(wa, ACT_STEPS * u + 5 + 2 * q)
                        act.activation(den[:, chunk(q)], den[:, chunk(q)], ACT.Exp, scale=-1.0).then_inc(wa, 1)

                def relus(u, q, js):
                    for j in js:
                        f = 8 * u + 4 * q + j
                        act.wait_ge(f_psum, f + 1)
                        if 4 * q + j >= 2:
                            act.wait_ge(kf_done, f - 1)
                        act.activation(rl[:, j % 2, :], G.bank[4 + j % 2][:, :], ACT.Relu).then_inc(relu_done, 1)

                def receptance(u):
                    act.wait_ge(r_kept, u + 1)
                    act.activation(sr[:, :], sr[:, :], ACT.Sigmoid).then_inc(sr_done, 1)

                def gate(u):
                    act.wait_ge(cr_psum, 2 * u + 2)
                    act.activation(sc[:, :, :], banks[:, 2:4, :], ACT.Sigmoid).then_inc(sc_done, 1)

                def body(l, b, last=False):
                    u = 2 * l + b
                    if not last:
                        norm(lambda q: ln_time(u + 1, q))
                        if b == 0:
                            keep_c(l)
                        else:
                            keep_a(l + 1)
                    norm(lambda q: ln_channel(u, q))
                    if not last:
                        gate_part(2 * u + 1, diff_a, vec_a, TMR, mix_a[:, 2])
                        keep_kv(u + 1)
                    gate_part(2 * u + (1 if last else 2), diff_c, vec_c, CMR, mix_c[:, 1])
                    if not last:
                        keep_r(u + 1)
                    relus(u, 0, range(2))
                    if not last:
                        decays(u + 1)
                    relus(u, 0, range(2, 4))
                    if not last:
                        weights(u + 1)
                    relus(u, 1, range(2))
                    if not last:
                        receptance(u + 1)
                    gate(u)
                    load_act_set(nc, act, EXP_LN_SET)
                    relus(u, 1, range(2, 4))
                    if not last:
                        inverse(u + 1)

                keep_a(0)
                norm(lambda q: n0 + q)
                gate_part(0, diff_a, vec_a, TMR, mix_a[:, 2])
                keep_kv(0)
                keep_r(0)
                decays(0)
                weights(0)
                receptance(0)
                load_act_set(nc, act, EXP_LN_SET)
                inverse(0)
                layers(act, body)

            @block.gpsimd
            def _(pool):
                def gate_mix(b, call, mix):
                    for q in range(2):
                        pool.wait_ge(part_mixed, 2 * call + q + 1)
                        pool.tensor_tensor(mix[:, q, :], mix[:, q, :], hp[:, b, q * CH:(q + 1) * CH], ALU.add)\
                            .then_inc(mixed_p, 1)

                def term_2(u):
                    pool.wait_ge(wa, ACT_STEPS * u + 3)
                    pool.wait_ge(v_kept, 2 * u + 2)
                    pool.tensor_tensor(n2[:, :], e2[:, :], v_s[:, :], ALU.mult).then_inc(wp, 1)

                def squares(u, q):
                    for j in range(4):
                        pool.wait_ge(relu_done, 8 * u + 4 * q + j + 1)
                        pool.tensor_tensor(kf[:, j, q, :], rl[:, j % 2, :], rl[:, j % 2, :], ALU.mult).then_inc(kf_done, 1)

                def body(l, b, last=False):
                    u = 2 * l + b
                    if not last:
                        gate_mix(1 - b, 2 * u + 1, mix_a[:, 2])
                    gate_mix(b, 2 * u + (1 if last else 2), mix_c[:, 1])
                    squares(u, 0)
                    if not last:
                        term_2(u + 1)
                    squares(u, 1)

                gate_mix(0, 0, mix_a[:, 2])
                term_2(0)
                layers(pool, body)

            @block.vector
            def _(dve):
                def vectors_a(l):
                    dve.tensor_copy(vec_a[:, 0:11].unsqueeze(2),
                                    G.vec[:, 0:44].rearrange("p (v l) -> p v l", l=4)[:, :, bass.ds(l, 1)])\
                        .then_inc(vec_a_done, 1)
                    dve.tensor_copy(vec_a[:, 11:12], G.decay[:, bass.ds(l, 1)]).then_inc(vec_a_done, 1)
                    dve.wait_ge(vec_a_done, 2 * l + 2)

                def vectors_c(l):
                    dve.tensor_copy(vec_c[:, 0:11].unsqueeze(2),
                                    G.vec[:, 0:44].rearrange("p (v l) -> p v l", l=4)[:, :, bass.ds(l, 1)])\
                        .then_inc(vec_c_done, 1)
                    dve.wait_ge(vec_c_done, l + 1)

                def mixes(b, number, call, diff, vec, w, bias, weights, mix, mixed):
                    here = [hp[:, b, 1 + q * CH:1 + (q + 1) * CH] for q in range(2)]
                    before = [hp[:, b, q * CH:(q + 1) * CH] for q in range(2)]
                    for q in range(2):
                        ln_scale(dve, G, number(q), here[q], vec[:, w:w + 1], q)
                    for q in range(2):
                        dve.wait_ge(G.ln.scaled, number(q) + 1)
                        dve.tensor_scalar(here[q], here[q], vec[:, bias:bias + 1], None, ALU.add).then_inc(h_step, 1)
                    for q in range(2):
                        dve.wait_ge(h_step, 4 * call + q + 1)
                        dve.tensor_tensor(diff[:, q, :], here[q], before[q], ALU.subtract).then_inc(h_step, 1)
                    for q in range(2):
                        dve.wait_ge(h_step, 4 * call + 3 + q)
                        for i, tm in enumerate(weights):
                            last = dve.scalar_tensor_tensor(mix[:, i, q, :], diff[:, q, :], vec[:, tm:tm + 1], before[q],
                                                            ALU.mult, ALU.add)
                        last.then_inc(mixed, 1)

                def time_mix(u, b, number, call):
                    mixes(b, number, call, diff_a, vec_a, LN1W, LN1B, (TMK, TMV), mix_a, mixed_a)

                def recurrence(u):
                    at = STEPS * u
                    w, first = vec_a[:, 11:12], vec_a[:, FIRST:FIRST + 1]
                    prev, nxt = pp[:, 0:S], pp[:, 1:S + 1]
                    dve.wait_ge(k_kept, 2 * u + 2)
                    dve.tensor_tensor_scan(nxt, w.to_broadcast([P, S]), k_s[:, :], -1e38, ALU.add, ALU.max).then_inc(wd, 1)
                    dve.wait_ge(wd, at + 1)
                    dve.tensor_tensor(e2b[:, :], k_s[:, :], nxt, ALU.subtract).then_inc(wd, 1)
                    dve.scalar_tensor_tensor(e1b[:, :], prev, w, nxt, ALU.add, ALU.subtract).then_inc(wd, 1)
                    dve.scalar_tensor_tensor(num[:, :], k_s[:, :], first, prev, ALU.add, ALU.subtract).then_inc(wd, 1)
                    dve.wait_ge(wd, at + 4)
                    dve.tensor_scalar(e2[:, :], num[:, :], 0.0, None, ALU.min).then_inc(wd, 1)
                    dve.tensor_scalar(e1[:, :], num[:, :], 0.0, None, ALU.max).then_inc(wd, 1)
                    dve.wait_ge(v_kept, 2 * u + 2)
                    dve.wait_ge(wa, ACT_STEPS * u + 1)
                    dve.tensor_tensor(den[:, :], e2b[:, :], v_s[:, :], ALU.mult).then_inc(wd, 1)
                    dve.wait_ge(wa, ACT_STEPS * u + 2)
                    dve.tensor_tensor_scan(bb[:, 1:S + 1], e1b[:, :], e2b[:, :], 0.0, ALU.mult, ALU.add).then_inc(wd, 1)
                    dve.wait_ge(wd, at + 7)
                    dve.tensor_tensor_scan(aa[:, 1:S + 1], e1b[:, :], den[:, :], 0.0, ALU.mult, ALU.add).then_inc(wd, 1)
                    dve.wait_ge(wd, at + 9)
                    dve.wait_ge(wa, ACT_STEPS * u + 4)
                    dve.tensor_tensor(den[:, :], e1[:, :], bb[:, 0:S], ALU.mult).then_inc(wd, 1)
                    dve.tensor_tensor(num[:, :], e1[:, :], aa[:, 0:S], ALU.mult).then_inc(wd, 1)
                    dve.wait_ge(wd, at + 10)
                    for q in range(2):
                        dve.tensor_tensor(den[:, chunk(q)], den[:, chunk(q)], e2[:, chunk(q)], ALU.add).then_inc(wd, 1)
                    dve.wait_ge(wp, u + 1)
                    dve.wait_ge(wd, at + 11)
                    dve.tensor_tensor(num[:, :], num[:, :], n2[:, :], ALU.add).then_inc(wd, 1)
                    dve.wait_ge(wd, at + 14)
                    dve.wait_ge(sr_done, u + 1)
                    dve.tensor_tensor(num[:, :], num[:, :], sr[:, :], ALU.mult).then_inc(wd, 1)
                    dve.wait_ge(wd, at + 15)
                    for q in range(2):
                        dve.wait_ge(wa, ACT_STEPS * u + 6 + 2 * q)
                        dve.tensor_tensor(rw[:, chunk(q)], num[:, chunk(q)], den[:, chunk(q)], ALU.mult).then_inc(wd, 1)

                def gated(u, b):
                    dve.wait_ge(sc_done, u + 1)
                    for q in range(2):
                        dve.wait_ge(kv_psum, 2 * u + q + 1)
                        dve.tensor_tensor(kvs[:, q, :], sc[:, q, :], G.bank[6 + q][:, :], ALU.mult).then_inc(kv_step, 1)
                        dve.wait_ge(kv_step, 2 * u + q + 1)
                        dve.tensor_tensor(G.r[:, seq(b, q)], G.r[:, seq(b, q)], kvs[:, q, :], ALU.add).then_inc(r_new, 1)

                def body(l, b, last=False):
                    u = 2 * l + b
                    for q in range(2):
                        dve.wait_ge(o_psum, 2 * u + q + 1)
                        dve.tensor_tensor(G.r[:, seq(b, q)], G.r[:, seq(b, q)], G.bank[4 + q][:, :], ALU.add)\
                            .then_inc(r_mid, 1)
                    if b == 0:
                        vectors_c(l)
                    if not last:
                        if b == 1:
                            vectors_a(l + 1)
                        time_mix(u + 1, 1 - b, lambda q: ln_time(u + 1, q), 2 * u + 1)
                    mixes(b, lambda q: ln_channel(u, q), 2 * u + (1 if last else 2), diff_c, vec_c, LN2W, LN2B, (CMK,), mix_c, mixed_c)
                    if not last:
                        recurrence(u + 1)
                    gated(u, b)

                dve.memset(hp[:, :, 0:1], 0.0).then_inc(start, 1)
                dve.memset(pp[:, 0:1], -1e38).then_inc(start, 1)
                dve.memset(aa[:, 0:1], 0.0).then_inc(r_new, 1)
                dve.memset(bb[:, 0:1], 0.0).then_inc(r_new, 1)
                dve.wait_ge(start, 2)
                dve.wait_ge(r_new, 2)
                vectors_a(0)
                time_mix(0, 0, lambda q: n0 + q, 0)
                recurrence(0)
                layers(dve, body)


def stage_last(nc, G, A, out):
    mem = G.mem
    E, TOP = 8, 2
    PAIRS = E // 2
    NN = PAIRS * NC
    with ExitStack() as ctx:
        m = Memory(nc, ctx)
        w1, w3 = m.sb("w1", [P, E, 64]), m.sb("w3", [P, E, 64])
        w2 = m.sb("w2", [P, PAIRS, P])
        logit = m.sb("logit", [P, NT, E])
        wide, wide_out = m.sb("wide2", [P, NT, 14]), m.sb("wide2_out", [P, NT, 14])
        best, pick = m.sb("best2", [P, NT, 8]), m.sb("pick2", [P, NT, 8])
        total = m.sb("total2", [P, NT, 1])
        chosen = m.sb("chosen2", [P, NT, E])
        cs, gs, us, sg, hid = (m.sb(n, [P, 2, CH]) for n in ("l_cs", "l_gs", "l_us", "l_sg", "l_hid"))
        o_tok = m.sb("o_tok", [P, NT, P])
        w_in = mem.sem("l_w_in")
        x_new, h_done = mem.sem("l_x_new"), mem.sem("l_h_done")
        logit_psum, step, shifted, exp_done = mem.sem("l_logit"), mem.sem("l_step"), mem.sem("l_shifted"), mem.sem("l_exp")
        comb_done = mem.sem("l_comb")
        c_psum, g_psum, u_psum, y_psum = mem.sem("l_c"), mem.sem("l_g"), mem.sem("l_u"), mem.sem("l_y")
        cs_done, gs_done, us_done, silu_done, hid_done = (mem.sem(n) for n in ("l_cs_d", "l_gs_d", "l_us_d", "l_silu_d", "l_hid_d"))
        x_fin, o_psum, o_kept, o_out = mem.sem("l_x_fin"), mem.sem("l_o"), mem.sem("l_o_kept"), mem.sem("l_o_out")
        ga, cb, sb_, gb = (G.mod[:, 1, j, :] for j in (2, 4, 3, 5))
        y_bank, o_bank = G.bank[0:2], G.bank[2:4]
        g_bank, u_bank, c_bank = G.bank[5], G.bank[6], (G.bank[4], G.bank[7])
        n0 = G.ln_count
        G.ln_count += NC
        out_d = out.rearrange("b (t p) c -> p (b t) c", p=P)
        with nc.Block() as block:
            @block.sync
            def _(sp):
                for dst, name in ((w1, "w1"), (w3, "w3")):
                    sp.dma_start(dst[:, :, :], A["L1_ffn_" + name].rearrange("e d h -> d e h")).then_inc(w_in, 16)
                sp.dma_start(w2[:, :, :], A["L1_ffn_w2"].rearrange("(p e) h d -> (e h) p d", e=2)).then_inc(w_in, 16)
                for c in range(NC):
                    sp.wait_ge(o_kept, c + 1)
                    sp.dma_start(out_d[:, 4 * c:4 * c + 4, :], o_tok[:, 4 * c:4 * c + 4, :]).then_inc(o_out, 16)
                sp.wait_ge(o_out, 16 * NC)

            @block.tensor
            def _(pe):
                def centre(c):
                    pe.wait_ge(x_new, c + 1)
                    ln_centre(pe, G, n0 + c, G.x[:, chunk(c)])

                def logits(c):
                    pe.wait_ge(h_done, c + 1)
                    for t in range(4 * c, 4 * c + 4):
                        mm = pe.matmul(G.bank[4][:, chunk(t, E)], G.h[:, chunk(t, P)], G.gate1[:, :], start=True, stop=True)
                    mm.then_inc(logit_psum, 1)

                def factors(n):
                    c, p = n // PAIRS, n % PAIRS
                    if n >= 2:
                        pe.wait_ge(cs_done, n - 1)
                    for t in range(4):
                        for e in range(2):
                            mm = pe.matmul(c_bank[n % 2][chunk(e, 64), chunk(t, P)],
                                           chosen[:, 4 * c + t, 2 * p + e:2 * p + e + 1].to_broadcast([P, 64]),
                                           G.ident[:, :], start=True, stop=True)
                    mm.then_inc(c_psum, 1)

                def down(n):
                    c, p = n // PAIRS, n % PAIRS
                    pe.wait_ge(hid_done, n + 1)
                    if p == 0 and c >= 2:
                        pe.wait_ge(x_fin, c - 1)
                    pe.matmul(y_bank[c % 2][:, :], w2[:, p, :], hid[:, n % 2, :], start=(p == 0), stop=(p == PAIRS - 1),
                              skip_group_check=True).then_inc(y_psum, 1)

                def turn(c):
                    pe.wait_ge(x_fin, c + 1)
                    if c >= 2:
                        pe.wait_ge(o_kept, c - 1)
                    for t in range(4):
                        mm = pe.transpose(o_bank[c % 2][:, chunk(t, P)], G.x[:, chunk(4 * c + t, P)], G.ident[:, :])
                    mm.then_inc(o_psum, 1)

                centre(0)
                centre(1)
                for c in range(NC):
                    ln_variance(pe, G, n0 + c)
                    if c >= 1:
                        if c + 1 < NC:
                            centre(c + 1)
                        logits(c - 1)
                logits(NC - 1)
                pe.wait_ge(w_in, 48)
                pe.wait_ge(comb_done, 1)
                factors(0)
                for n in range(NN):
                    c, p = n // PAIRS, n % PAIRS
                    if n >= 1:
                        pe.wait_ge(gs_done, n)
                    pe.matmul(g_bank, w1[:, 2 * p:2 * p + 2, :].rearrange("p e h -> p (e h)"), G.h[:, chunk(c)],
                              start=True, stop=True).then_inc(g_psum, 1)
                    if n >= 2:
                        down(n - 2)
                    if n >= 1:
                        pe.wait_ge(us_done, n)
                    pe.matmul(u_bank, w3[:, 2 * p:2 * p + 2, :].rearrange("p e h -> p (e h)"), G.h[:, chunk(c)],
                              start=True, stop=True).then_inc(u_psum, 1)
                    if n + 1 < NN:
                        factors(n + 1)
                    if p == 2 and c >= 1:
                        turn(c - 1)
                down(NN - 2)
                down(NN - 1)
                turn(NC - 1)

            @block.scalar
            def _(act):
                ln_square(act, G, n0)
                for c in range(NC):
                    if c == 0:
                        ln_square(act, G, n0 + 1)
                    ln_rstd(act, G, n0 + c)
                    if 1 <= c < NC - 1:
                        ln_square(act, G, n0 + c + 1)
                act.wait_ge(shifted, 1)
                act.activation(logit[:, :, :], logit[:, :, :], ACT.Exp).then_inc(exp_done, 1)

                def keep_factors(n):
                    act.wait_ge(c_psum, n + 1)
                    if n >= 2:
                        act.wait_ge(us_done, n - 1)
                    act.copy(cs[:, n % 2, :], c_bank[n % 2]).then_inc(cs_done, 1)

                def keep_out(c):
                    act.wait_ge(o_psum, c + 1)
                    act.copy(o_tok[:, 4 * c:4 * c + 4, :], o_bank[c % 2].rearrange("p (t m) -> p t m", t=4)).then_inc(o_kept, 1)

                keep_factors(0)
                for n in range(NN):
                    c, p = n // PAIRS, n % PAIRS
                    if n + 1 < NN:
                        keep_factors(n + 1)
                    act.wait_ge(gs_done, n + 1)
                    act.activation(sg[:, n % 2, :], gs[:, n % 2, :], ACT.Silu).then_inc(silu_done, 1)
                    if p == 3 and c >= 1:
                        keep_out(c - 1)
                keep_out(NC - 1)

            @block.vector
            def _(dve):
                count = [0]

                def link(ins):
                    count[0] += 1
                    ins.then_inc(step, 1)
                    dve.wait_ge(step, count[0])

                for c in range(NC):
                    dve.scalar_tensor_tensor(G.x[:, chunk(c)], G.r[:, chunk(c)], ga[:, c // 2:c // 2 + 1],
                                             G.x[:, chunk(c)], ALU.mult, ALU.add).then_inc(x_new, 1)
                link(dve.memset(wide[:, :, E:14], BIG))
                link(dve.memset(pick[:, :, TOP:8], BIG))
                for c in range(NC):
                    ln_scale(dve, G, n0 + c, G.h[:, chunk(c)], cb[:, c // 2:c // 2 + 1])
                    dve.wait_ge(G.ln.scaled, n0 + c + 1)
                    dve.tensor_scalar(G.h[:, chunk(c)], G.h[:, chunk(c)], sb_[:, c // 2:c // 2 + 1], None, ALU.add)\
                        .then_inc(h_done, 1)
                dve.wait_ge(logit_psum, NC)
                link(dve.tensor_copy(logit[:, :, :], G.bank[4][:, 0:NT * E].rearrange("p (t e) -> p t e", t=NT)))
                link(dve.tensor_reduce(total[:, :, 0], logit[:, :, :], AX_X, ALU.max))
                dve.tensor_tensor(logit[:, :, :], logit[:, :, :], total[:, :, :].to_broadcast([P, NT, E]), ALU.subtract)\
                    .then_inc(shifted, 1)
                dve.wait_ge(exp_done, 1)
                link(dve.tensor_reduce(total[:, :, 0], logit[:, :, :], AX_X, ALU.add))
                link(dve.reciprocal(total[:, :, :], total[:, :, :]))
                link(dve.tensor_tensor(wide[:, :, 0:E], logit[:, :, :], total[:, :, :].to_broadcast([P, NT, E]), ALU.mult))
                for t in range(NT):
                    last = dve.max(best[:, t, :], wide[:, t, 0:E])
                link(last)
                link(dve.tensor_copy(pick[:, :, 0:TOP], best[:, :, 0:TOP]))
                for t in range(NT):
                    last = dve.match_replace(wide_out[:, t, :], pick[:, t, :], wide[:, t, :], -BIG)
                link(last)
                link(dve.tensor_tensor(chosen[:, :, :], wide_out[:, :, 0:E], wide[:, :, 0:E], ALU.not_equal))
                dve.tensor_tensor(chosen[:, :, :], chosen[:, :, :], wide[:, :, 0:E], ALU.mult).then_inc(comb_done, 1)

                def join(n):
                    dve.wait_ge(silu_done, n + 1)
                    dve.wait_ge(us_done, n + 1)
                    if n >= 2:
                        dve.wait_ge(y_psum, n - 1)
                    dve.tensor_tensor(hid[:, n % 2, :], sg[:, n % 2, :], us[:, n % 2, :], ALU.mult).then_inc(hid_done, 1)

                def residual(c):
                    dve.wait_ge(y_psum, PAIRS * (c + 1))
                    dve.scalar_tensor_tensor(G.x[:, chunk(c)], y_bank[c % 2], gb[:, c // 2:c // 2 + 1],
                                             G.x[:, chunk(c)], ALU.mult, ALU.add).then_inc(x_fin, 1)

                for n in range(NN):
                    c, p = n // PAIRS, n % PAIRS
                    dve.wait_ge(cs_done, n + 1)
                    dve.wait_ge(g_psum, n + 1)
                    dve.tensor_tensor(gs[:, n % 2, :], g_bank, cs[:, n % 2, :], ALU.mult).then_inc(gs_done, 1)
                    if p == 2 and c >= 1:
                        residual(c - 1)
                    dve.wait_ge(u_psum, n + 1)
                    dve.tensor_tensor(us[:, n % 2, :], u_bank, cs[:, n % 2, :], ALU.mult).then_inc(us_done, 1)
                    if n >= 1:
                        join(n - 1)
                join(NN - 1)
                residual(NC - 1)


def build(nc, A, out):
    G = Global()
    with ExitStack() as ctx:
        mem = G.mem = Memory(nc, ctx)
        psum = ctx.enter_context(nc.psum_tensor("psum", [P, 8, CH], F32))
        G.bank = [psum[:, i, :] for i in range(8)]
        G.pair = [psum[:, 0:2, :], psum[:, 2:4, :]]
        G.ident = mem.sb("ident", [P, P])
        G.identb = mem.sb("identb", [P, P], BF16)
        G.mask_qk = mem.sb("mask_qk", [P, P], BF16)
        G.mask_kq = mem.sb("mask_kq", [P, P], BF16)
        G.den_row = mem.sb("den_row", [P, P])
        G.mean = mem.sb("mean", [P, P])
        G.centre = mem.sb("centre", [P, P])
        G.eps = mem.sb("eps", [P, 1])
        G.x = mem.sb("x", [P, T])
        G.vec = mem.sb("vec", [P, 46])
        G.decay = mem.sb("decay", [P, LAYERS])
        G.mod = mem.sb("mod", [P, 2, 6, B])
        G.gate0 = mem.sb("gate0", [P, 64])
        G.gate1 = mem.sb("gate1", [P, 8])
        G.gate_bias = mem.sb("gate_bias", [P, 64])
        G.wqkv = mem.sb("wqkv", [P, 3, P])
        G.wo_t = mem.sb("wo_t", [P, 4, P])
        G.sq = mem.sb("ln_sq", [P, 2, CH])
        G.rs = mem.sb("ln_rs", [P, 2, CH])
        G.ln = LnSems(mem)
        G.raw = [mem.sb(f"moe_raw{k}", [P, 3, P]) for k in range(2)]
        G.raw_in = [mem.sem(f"moe_raw_in{k}") for k in range(2)]
        G.h = mem.sb("h", [P, T])
        G.x_l0, G.r_done = mem.sem("x_l0"), mem.sem("r_done")
        G.ln_count = NC
        G.comb_d = nc.dram_tensor("comb_rows", [64, T], F32).ap()
        G.psum3 = psum
        G.rows_d = [nc.dram_tensor("rows_q", [3 * DK, H, T], BF16).ap(),
                    nc.dram_tensor("rows_k", [ROWS, H, T], BF16).ap()]
        with ExitStack() as attn:
            m = Memory(nc, attn)
            G.qa = m.sb("qa", [ROWS + 3, RING, HG, S], BF16)
            G.ka = m.sb("ka", [96, RING, HG, S], BF16)
            G.part = m.sb("part", [P, 2, 3, 2, CH], BF16)
            G.parts_out = [[mem.sem(f"parts_out_{n}{par}") for par in range(2)] for n in "qk"]
            G.va = m.sb("va", [P, NG, 8, HG, 32])
            G.v_pad = mem.sem("v_pad")
            G.ones_done = mem.sem("ones_done")
            G.wo_psum, G.x_new = mem.sem("wo_psum"), mem.sem("x_new")
            G.qk_in = mem.sem("qk_in")
            stage_setup(nc, G, A)
            G.o = m.sb("o", [P, 4, T])
            stage_qkv(nc, G)
            stage_attention(nc, G)
            stage_router(nc, G, A)
        stage_experts(nc, G, A)
        G.r = mem.sb("r", [P, T])
        G.raw_a, G.raw_c = mem.sb("raw_a", [P, 4, P]), mem.sb("raw_c", [P, 9, P])
        G.a_in, G.c_in = mem.sem("rw_a_in"), mem.sem("rw_c_in")
        stage_rwkv_in(nc, G, A)
        stage_rwkv(nc, G, A)
        stage_last(nc, G, A, out)


_INS = ['L0_attn_x', 'L0_attn_WQ', 'L0_attn_WK', 'L0_attn_WV', 'L0_attn_WO', 'L0_ffn_gate_w', 'L0_ffn_gate_bias',
        'L0_ffn_eg_w', 'L0_ffn_eu_w', 'L0_ffn_ed_w', 'L0_ffn_sg_w', 'L0_ffn_su_w', 'L0_ffn_sd_w', 'L0_c', 'L0_wmod',
        'L1_attn_ln0_w', 'L1_attn_ln0_b', 'L1_attn_ln1_w', 'L1_attn_ln1_b', 'L1_attn_ln2_w', 'L1_attn_ln2_b',
        'L1_attn_time_decay', 'L1_attn_time_first', 'L1_attn_tmk', 'L1_attn_tmv', 'L1_attn_tmr', 'L1_attn_Wk',
        'L1_attn_Wv', 'L1_attn_Wr', 'L1_attn_Wo', 'L1_attn_cmk', 'L1_attn_cmr', 'L1_attn_Wck', 'L1_attn_Wcv',
        'L1_attn_Wcr', 'L1_ffn_gate_w', 'L1_ffn_w1', 'L1_ffn_w2', 'L1_ffn_w3', 'L1_c', 'L1_wmod']


def kernel(**inputs):
    import numpy as _np
    import concourse.bacc as _bacc
    from concourse.bass_utils import run_bass_kernel_spmd as _run

    nc = _bacc.Bacc("TRN2", target_bir_lowering=False, num_devices=1)
    arrays, aps = {}, {}
    for name in _INS:
        arrays["in_" + name] = _np.ascontiguousarray(inputs[name])
        aps[name] = nc.dram_tensor("in_" + name, arrays["in_" + name].shape, F32, kind="ExternalInput").ap()
    out = nc.dram_tensor("out_x", (B, S, P), F32, kind="ExternalOutput").ap()
    build(nc, aps, out)
    return _run(nc, [arrays], core_ids=[0]).results[0]["out_x"]
```
